# Optimizing a Trainium2 kernel written in Bass

```python
import numpy as np
import jax
import jax.numpy as jnp

def _softmax(x, axis=-1):
    return jax.nn.softmax(x, axis=axis)

def _gelu(x):
    return jax.nn.gelu(x, approximate=True)

def _silu(x):
    return jax.nn.silu(x)

def _sigmoid(x):
    return jax.nn.sigmoid(x)

def _layernorm(x, axis=-1, eps=1e-05):
    m = jnp.mean(x, axis=axis, keepdims=True)
    v = jnp.var(x, axis=axis, keepdims=True)
    return (x - m) / jnp.sqrt(v + eps)

def _scatter_add(tgt, idx, src, axis=0):
    return tgt.at[idx].add(src)

def _segment_sum(src, seg, n):
    return jax.ops.segment_sum(src, seg, n)
kernel_name = 'mk_early_fusion_d4_tok_img1024_r4_436ead'

def setup_inputs(seed: int=0):
    np.random.seed(seed)
    _w = jnp.asarray

    def _rec_inputs():
        import jax
        import jax.numpy as jnp
        _rk = jax.random.key(seed)
        x = 7.22013e-05 + 1.00017 * jax.random.normal(jax.random.fold_in(_rk, 1), (4, 1, 512, 256), jnp.float32)
        txt = 1.13155e-10 + 0.999995 * jax.random.normal(jax.random.fold_in(_rk, 2), (4, 32, 256), jnp.float32)
        return (x, txt)
    x, txt = _rec_inputs()

    def _L0_tok_setup():
        import jax, jax.numpy as jnp
        import numpy as np
        D_MODEL = 256
        NUM_HEADS = 16
        HEAD_DIM = D_MODEL // NUM_HEADS
        LN_EPS = 1e-05
        key = jax.random.key(seed)
        ks = jax.random.split(key, 7)
        B, S, D = (4, 512, D_MODEL)
        scale = 1.0 / np.sqrt(D)
        return {'x': jax.random.normal(ks[0], (B, 1, S, D), dtype=jnp.float32), 'W_qkv': jax.random.normal(ks[1], (D, 3 * D), dtype=jnp.float32) * scale, 'b_qkv': jnp.zeros((3 * D,), dtype=jnp.float32), 'W_out': jax.random.normal(ks[2], (D, D), dtype=jnp.float32) * scale, 'b_out': jnp.zeros((D,), dtype=jnp.float32), 'ln_gamma': jnp.ones((D,), dtype=jnp.float32), 'ln_beta': jnp.zeros((D,), dtype=jnp.float32)}
    _L0_tok_all = _L0_tok_setup()
    _L0_tok_in = {k: v for k, v in _L0_tok_all.items() if k in ('W_qkv', 'b_qkv', 'W_out', 'b_out', 'ln_gamma', 'ln_beta')}
    del _L0_tok_all

    def _L0_attn_setup():
        import jax, jax.numpy as jnp
        import numpy as np
        import math
        D_MODEL = 256
        N_HEADS = 16
        HEAD_DIM = D_MODEL // N_HEADS
        R = HEAD_DIM // 2
        ROPE_BASE = 10000.0
        B, T = (4, 512)

        def _fourier_bias(alpha, beta, t):
            omega = ROPE_BASE ** (-2.0 * jnp.arange(R, dtype=jnp.float32) / HEAD_DIM)
            disp = jnp.arange(-(t - 1), t, dtype=jnp.float32)
            angles = omega[:, None] * disp[None, :]
            vec = jnp.einsum('hr,rk->hk', alpha, jnp.cos(angles)) + jnp.einsum('hr,rk->hk', beta, jnp.sin(angles))
            i = jnp.arange(t)
            idx = i[:, None] - i[None, :] + (t - 1)
            return vec[:, idx]
        key = jax.random.key(seed)
        k1, k2, k3, k4, k5 = jax.random.split(key, 5)
        x = jax.random.normal(k1, (B, T, D_MODEL), dtype=jnp.float32)
        Wqkv = jax.random.normal(k2, (3 * D_MODEL, D_MODEL), dtype=jnp.float32) * (1.0 / math.sqrt(D_MODEL))
        Wout = jax.random.normal(k3, (D_MODEL, D_MODEL), dtype=jnp.float32) * (1.0 / math.sqrt(D_MODEL))
        alpha = jax.random.normal(k4, (N_HEADS, R), dtype=jnp.float32) * 0.01
        beta = jax.random.normal(k5, (N_HEADS, R), dtype=jnp.float32) * 0.01
        return {'x': x, 'Wqkv': Wqkv, 'Wout': Wout, 'alpha': alpha, 'beta': beta}
    _L0_attn_all = _L0_attn_setup()
    _L0_attn_in = {k: v for k, v in _L0_attn_all.items() if k in ('Wqkv', 'Wout', 'alpha', 'beta')}
    del _L0_attn_all

    def _L0_ffn_setup():
        import jax, jax.numpy as jnp
        import numpy as np
        E = 8
        TOPK = 2
        PRIME = 11
        HASH_OFF = 7919
        N_SHARED = 1
        key = jax.random.key(seed)
        ks = jax.random.split(key, 8)
        B, T, C, Hs, Hr = (4, 2048, 256, 512, 256)
        sc = lambda k, shape, fan: jax.random.normal(k, shape, jnp.float32) * fan ** (-0.5)
        return {'x': jax.random.normal(ks[0], (B, T, C), jnp.float32), 't_emb': jax.random.normal(ks[1], (B, C), jnp.float32), 'sw1': sc(ks[2], (C, Hs), C), 'sb1': jnp.zeros((Hs,), jnp.float32), 'sw3': sc(ks[3], (C, Hs), C), 'sb3': jnp.zeros((Hs,), jnp.float32), 'sw2': sc(ks[4], (Hs, C), Hs), 'sb2': jnp.zeros((C,), jnp.float32), 'w1': sc(ks[5], (E, C, Hr), C), 'b1': jnp.zeros((E, Hr), jnp.float32), 'w2': sc(ks[6], (E, Hr, C), Hr), 'b2': jnp.zeros((E, C), jnp.float32)}
    _L0_ffn_all = _L0_ffn_setup()
    _L0_ffn_in = {k: v for k, v in _L0_ffn_all.items() if k in ('t_emb', 'sw1', 'sb1', 'sw3', 'sb3', 'sw2', 'sb2', 'w1', 'b1', 'w2', 'b2')}
    del _L0_ffn_all

    def _L1_attn_setup():
        import jax, jax.numpy as jnp
        import numpy as np
        HEADS = 16
        EPS = 1e-06
        key = jax.random.key(seed)
        k0, k1, k2, k3, k4 = jax.random.split(key, 5)
        b, t, dim = (2, 512, 256)
        scale = 0.02
        return {'hidden_states': jax.random.normal(k0, (b, t, dim), dtype=jnp.float32), 'Wq': jax.random.normal(k1, (dim, dim), dtype=jnp.float32) * scale, 'Wk': jax.random.normal(k2, (dim, dim), dtype=jnp.float32) * scale, 'Wv': jax.random.normal(k3, (dim, dim), dtype=jnp.float32) * scale, 'Wo': jax.random.normal(k4, (dim, dim), dtype=jnp.float32) * scale}
    _L1_attn_all = _L1_attn_setup()
    _L1_attn_in = {k: v for k, v in _L1_attn_all.items() if k in ('Wq', 'Wk', 'Wv', 'Wo')}
    del _L1_attn_all

    def _L1_ffn_setup():
        import jax, jax.numpy as jnp
        import numpy as np
        D_MODEL = 256
        HIDDEN = 512
        MOE_DIM = 64
        N_EXPERTS = 8
        TOP_K = 2
        EXP_HIDDEN = HIDDEN // 2
        B, S = (4, 512)
        key = jax.random.key(seed)
        ks = jax.random.split(key, 20)

        def w(k, shape, fan_in):
            return (jax.random.normal(k, shape, dtype=jnp.float32) / np.sqrt(fan_in)).astype(jnp.float32)
        return {'inputs_embeds': jax.random.normal(ks[0], (B, S, D_MODEL), dtype=jnp.float32), 'enc_w': w(ks[1], (D_MODEL, HIDDEN), D_MODEL), 'enc_b': jnp.zeros((HIDDEN,), jnp.float32), 's2c_w': w(ks[2], (HIDDEN, MOE_DIM), HIDDEN), 's2c_b': jnp.zeros((MOE_DIM,), jnp.float32), 'r_w1': w(ks[3], (MOE_DIM, 64), MOE_DIM), 'r_b1': jnp.zeros((64,), jnp.float32), 'r_w2': w(ks[4], (64, N_EXPERTS), 64), 'r_b2': jnp.zeros((N_EXPERTS,), jnp.float32), 'e_w1': w(ks[5], (N_EXPERTS, MOE_DIM, EXP_HIDDEN), MOE_DIM), 'e_b1': jnp.zeros((N_EXPERTS, EXP_HIDDEN), jnp.float32), 'e_w2': w(ks[6], (N_EXPERTS, EXP_HIDDEN, MOE_DIM), EXP_HIDDEN), 'e_b2': jnp.zeros((N_EXPERTS, MOE_DIM), jnp.float32), 'c2s_w': w(ks[7], (MOE_DIM, HIDDEN), MOE_DIM), 'c2s_b': jnp.zeros((HIDDEN,), jnp.float32), 'dec_w': w(ks[8], (HIDDEN, D_MODEL), HIDDEN), 'dec_b': jnp.zeros((D_MODEL,), jnp.float32), 'ln_g': jnp.ones((D_MODEL,), jnp.float32), 'ln_b': jnp.zeros((D_MODEL,), jnp.float32)}
    _L1_ffn_all = _L1_ffn_setup()
    _L1_ffn_in = {k: v for k, v in _L1_ffn_all.items() if k in ('enc_w', 'enc_b', 's2c_w', 's2c_b', 'r_w1', 'r_b1', 'r_w2', 'r_b2', 'e_w1', 'e_b1', 'e_w2', 'e_b2', 'c2s_w', 'c2s_b', 'dec_w', 'dec_b', 'ln_g', 'ln_b')}
    del _L1_ffn_all

    def _L2_attn_setup():
        import jax, jax.numpy as jnp
        import numpy as np
        HEADS = 16
        HEAD_DIM = 64
        EMB = 256
        B, S = (4, 512)
        SCALE = 1.0 / 8.0
        MASK_PENALTY = -50.0
        key = jax.random.key(seed)
        ks = jax.random.split(key, 5)
        x = jax.random.normal(ks[0], (B, S, EMB), dtype=jnp.float32)
        Wq = jax.random.normal(ks[1], (EMB, HEADS * HEAD_DIM), dtype=jnp.float32) * 0.02
        Wk = jax.random.normal(ks[2], (EMB, HEADS * HEAD_DIM), dtype=jnp.float32) * 0.02
        Wv = jax.random.normal(ks[3], (EMB, HEADS * HEAD_DIM), dtype=jnp.float32) * 0.02
        Wr = jax.random.normal(ks[4], (HEADS * HEAD_DIM, EMB), dtype=jnp.float32) * 0.02
        return {'x': x, 'Wq': Wq, 'Wk': Wk, 'Wv': Wv, 'Wr': Wr}
    _L2_attn_all = _L2_attn_setup()
    _L2_attn_in = {k: v for k, v in _L2_attn_all.items() if k in ('Wq', 'Wk', 'Wv', 'Wr')}
    del _L2_attn_all

    def _L2_ffn_setup():
        import jax, jax.numpy as jnp
        import numpy as np
        DIM, HEADS, FFN, E = (256, 16, 1024, 8)
        B, S = (2, 256)
        EPS = 1e-05

        def _ln(x, g, b):
            mu = jnp.mean(x, axis=-1, keepdims=True)
            var = jnp.mean((x - mu) ** 2, axis=-1, keepdims=True)
            return (x - mu) * jax.lax.rsqrt(var + EPS) * g + b
        key = jax.random.key(seed)
        ks = jax.random.split(key, 20)
        sd = 0.02
        d, f = (DIM, FFN)
        return {'x': jax.random.normal(ks[0], (B, S, d), jnp.float32), 'ln1_g': jnp.ones((d,), jnp.float32), 'ln1_b': jnp.zeros((d,), jnp.float32), 'Wqkv': jax.random.normal(ks[1], (d, 3 * d), jnp.float32) * sd, 'bqkv': jnp.zeros((3 * d,), jnp.float32), 'Wo': jax.random.normal(ks[2], (d, d), jnp.float32) * sd, 'bo': jnp.zeros((d,), jnp.float32), 'ln2_g': jnp.ones((d,), jnp.float32), 'ln2_b': jnp.zeros((d,), jnp.float32), 'gate_w': jax.random.normal(ks[3], (d, E), jnp.float32) * sd, 'W1': jax.random.normal(ks[4], (E, d, f), jnp.float32) * sd, 'b1': jnp.zeros((E, f), jnp.float32), 'W2': jax.random.normal(ks[5], (E, f, d), jnp.float32) * sd, 'b2': jnp.zeros((E, d), jnp.float32), 'rW1': jax.random.normal(ks[6], (d, f), jnp.float32) * sd, 'rb1': jnp.zeros((f,), jnp.float32), 'rW2': jax.random.normal(ks[7], (f, d), jnp.float32) * sd, 'rb2': jnp.zeros((d,), jnp.float32), 'coef_w': jax.random.normal(ks[8], (d, 2), jnp.float32) * sd, 'coef_b': jnp.zeros((2,), jnp.float32)}
    _L2_ffn_all = _L2_ffn_setup()
    _L2_ffn_in = {k: v for k, v in _L2_ffn_all.items() if k in ('ln1_g', 'ln1_b', 'Wqkv', 'bqkv', 'Wo', 'bo', 'ln2_g', 'ln2_b', 'gate_w', 'W1', 'b1', 'W2', 'b2', 'rW1', 'rb1', 'rW2', 'rb2', 'coef_w', 'coef_b')}
    del _L2_ffn_all

    def _L3_attn_setup():
        import jax, jax.numpy as jnp
        import numpy as np
        H = 256
        NH = 16
        HD = H // NH
        B, S = (2, 512)
        key = jax.random.key(seed)
        ks = jax.random.split(key, 6)
        std = 0.02
        x = jax.random.normal(ks[0], (B, S, H), dtype=jnp.float32)
        w_qkv = jax.random.normal(ks[1], (3 * H, H), dtype=jnp.float32) * std
        b_qkv = jnp.zeros((3 * H,), dtype=jnp.float32)
        ln_g = jnp.ones((H,), dtype=jnp.float32)
        ln_b = jnp.zeros((H,), dtype=jnp.float32)
        w_ent = jax.random.normal(ks[2], (1, H), dtype=jnp.float32) * std
        b_ent = jnp.zeros((1,), dtype=jnp.float32)
        w_out = jax.random.normal(ks[3], (H, H), dtype=jnp.float32) * std
        b_out = jnp.zeros((H,), dtype=jnp.float32)
        return {'x': x, 'ln_g': ln_g, 'ln_b': ln_b, 'w_qkv': w_qkv, 'b_qkv': b_qkv, 'w_ent': w_ent, 'b_ent': b_ent, 'w_out': w_out, 'b_out': b_out}
    _L3_attn_all = _L3_attn_setup()
    _L3_attn_in = {k: v for k, v in _L3_attn_all.items() if k in ('ln_g', 'ln_b', 'w_qkv', 'b_qkv', 'w_ent', 'b_ent', 'w_out', 'b_out')}
    del _L3_attn_all

    def _L3_ffn_setup():
        import jax, jax.numpy as jnp
        import numpy as np
        TOP_K = 2
        key = jax.random.key(seed)
        k1, k2, k3, k4 = jax.random.split(key, 4)
        B, T, D, H, E = (2, 512, 256, 512, 8)
        x = jax.random.normal(k1, (B, T, D), dtype=jnp.float32)
        w12 = jax.random.normal(k2, (E, 2 * H, D), dtype=jnp.float32) * D ** (-0.5)
        w3 = jax.random.normal(k3, (E, D, H), dtype=jnp.float32) * H ** (-0.5)
        gate_w = jax.random.normal(k4, (E, D), dtype=jnp.float32) * D ** (-0.5)
        return {'x': x, 'w12': w12, 'w3': w3, 'gate_w': gate_w}
    _L3_ffn_all = _L3_ffn_setup()
    _L3_ffn_in = {k: v for k, v in _L3_ffn_all.items() if k in ('w12', 'w3', 'gate_w')}
    del _L3_ffn_all
    return {'x': x, 'txt': txt, 'L0_tok_W_qkv': _L0_tok_in['W_qkv'], 'L0_tok_b_qkv': _L0_tok_in['b_qkv'], 'L0_tok_W_out': _L0_tok_in['W_out'], 'L0_tok_b_out': _L0_tok_in['b_out'], 'L0_tok_ln_gamma': _L0_tok_in['ln_gamma'], 'L0_tok_ln_beta': _L0_tok_in['ln_beta'], 'L0_attn_Wqkv': _L0_attn_in['Wqkv'], 'L0_attn_Wout': _L0_attn_in['Wout'], 'L0_attn_alpha': _L0_attn_in['alpha'], 'L0_attn_beta': _L0_attn_in['beta'], 'L0_ffn_t_emb': _L0_ffn_in['t_emb'], 'L0_ffn_sw1': _L0_ffn_in['sw1'], 'L0_ffn_sb1': _L0_ffn_in['sb1'], 'L0_ffn_sw3': _L0_ffn_in['sw3'], 'L0_ffn_sb3': _L0_ffn_in['sb3'], 'L0_ffn_sw2': _L0_ffn_in['sw2'], 'L0_ffn_sb2': _L0_ffn_in['sb2'], 'L0_ffn_w1': _L0_ffn_in['w1'], 'L0_ffn_b1': _L0_ffn_in['b1'], 'L0_ffn_w2': _L0_ffn_in['w2'], 'L0_ffn_b2': _L0_ffn_in['b2'], 'L1_attn_Wq': _L1_attn_in['Wq'], 'L1_attn_Wk': _L1_attn_in['Wk'], 'L1_attn_Wv': _L1_attn_in['Wv'], 'L1_attn_Wo': _L1_attn_in['Wo'], 'L1_ffn_enc_w': _L1_ffn_in['enc_w'], 'L1_ffn_enc_b': _L1_ffn_in['enc_b'], 'L1_ffn_s2c_w': _L1_ffn_in['s2c_w'], 'L1_ffn_s2c_b': _L1_ffn_in['s2c_b'], 'L1_ffn_r_w1': _L1_ffn_in['r_w1'], 'L1_ffn_r_b1': _L1_ffn_in['r_b1'], 'L1_ffn_r_w2': _L1_ffn_in['r_w2'], 'L1_ffn_r_b2': _L1_ffn_in['r_b2'], 'L1_ffn_e_w1': _L1_ffn_in['e_w1'], 'L1_ffn_e_b1': _L1_ffn_in['e_b1'], 'L1_ffn_e_w2': _L1_ffn_in['e_w2'], 'L1_ffn_e_b2': _L1_ffn_in['e_b2'], 'L1_ffn_c2s_w': _L1_ffn_in['c2s_w'], 'L1_ffn_c2s_b': _L1_ffn_in['c2s_b'], 'L1_ffn_dec_w': _L1_ffn_in['dec_w'], 'L1_ffn_dec_b': _L1_ffn_in['dec_b'], 'L1_ffn_ln_g': _L1_ffn_in['ln_g'], 'L1_ffn_ln_b': _L1_ffn_in['ln_b'], 'L2_attn_Wq': _L2_attn_in['Wq'], 'L2_attn_Wk': _L2_attn_in['Wk'], 'L2_attn_Wv': _L2_attn_in['Wv'], 'L2_attn_Wr': _L2_attn_in['Wr'], 'L2_ffn_ln1_g': _L2_ffn_in['ln1_g'], 'L2_ffn_ln1_b': _L2_ffn_in['ln1_b'], 'L2_ffn_Wqkv': _L2_ffn_in['Wqkv'], 'L2_ffn_bqkv': _L2_ffn_in['bqkv'], 'L2_ffn_Wo': _L2_ffn_in['Wo'], 'L2_ffn_bo': _L2_ffn_in['bo'], 'L2_ffn_ln2_g': _L2_ffn_in['ln2_g'], 'L2_ffn_ln2_b': _L2_ffn_in['ln2_b'], 'L2_ffn_gate_w': _L2_ffn_in['gate_w'], 'L2_ffn_W1': _L2_ffn_in['W1'], 'L2_ffn_b1': _L2_ffn_in['b1'], 'L2_ffn_W2': _L2_ffn_in['W2'], 'L2_ffn_b2': _L2_ffn_in['b2'], 'L2_ffn_rW1': _L2_ffn_in['rW1'], 'L2_ffn_rb1': _L2_ffn_in['rb1'], 'L2_ffn_rW2': _L2_ffn_in['rW2'], 'L2_ffn_rb2': _L2_ffn_in['rb2'], 'L2_ffn_coef_w': _L2_ffn_in['coef_w'], 'L2_ffn_coef_b': _L2_ffn_in['coef_b'], 'L3_attn_ln_g': _L3_attn_in['ln_g'], 'L3_attn_ln_b': _L3_attn_in['ln_b'], 'L3_attn_w_qkv': _L3_attn_in['w_qkv'], 'L3_attn_b_qkv': _L3_attn_in['b_qkv'], 'L3_attn_w_ent': _L3_attn_in['w_ent'], 'L3_attn_b_ent': _L3_attn_in['b_ent'], 'L3_attn_w_out': _L3_attn_in['w_out'], 'L3_attn_b_out': _L3_attn_in['b_out'], 'L3_ffn_w12': _L3_ffn_in['w12'], 'L3_ffn_w3': _L3_ffn_in['w3'], 'L3_ffn_gate_w': _L3_ffn_in['gate_w']}

def reference(x, txt, L0_tok_W_qkv, L0_tok_b_qkv, L0_tok_W_out, L0_tok_b_out, L0_tok_ln_gamma, L0_tok_ln_beta, L0_attn_Wqkv, L0_attn_Wout, L0_attn_alpha, L0_attn_beta, L0_ffn_t_emb, L0_ffn_sw1, L0_ffn_sb1, L0_ffn_sw3, L0_ffn_sb3, L0_ffn_sw2, L0_ffn_sb2, L0_ffn_w1, L0_ffn_b1, L0_ffn_w2, L0_ffn_b2, L1_attn_Wq, L1_attn_Wk, L1_attn_Wv, L1_attn_Wo, L1_ffn_enc_w, L1_ffn_enc_b, L1_ffn_s2c_w, L1_ffn_s2c_b, L1_ffn_r_w1, L1_ffn_r_b1, L1_ffn_r_w2, L1_ffn_r_b2, L1_ffn_e_w1, L1_ffn_e_b1, L1_ffn_e_w2, L1_ffn_e_b2, L1_ffn_c2s_w, L1_ffn_c2s_b, L1_ffn_dec_w, L1_ffn_dec_b, L1_ffn_ln_g, L1_ffn_ln_b, L2_attn_Wq, L2_attn_Wk, L2_attn_Wv, L2_attn_Wr, L2_ffn_ln1_g, L2_ffn_ln1_b, L2_ffn_Wqkv, L2_ffn_bqkv, L2_ffn_Wo, L2_ffn_bo, L2_ffn_ln2_g, L2_ffn_ln2_b, L2_ffn_gate_w, L2_ffn_W1, L2_ffn_b1, L2_ffn_W2, L2_ffn_b2, L2_ffn_rW1, L2_ffn_rb1, L2_ffn_rW2, L2_ffn_rb2, L2_ffn_coef_w, L2_ffn_coef_b, L3_attn_ln_g, L3_attn_ln_b, L3_attn_w_qkv, L3_attn_b_qkv, L3_attn_w_ent, L3_attn_b_ent, L3_attn_w_out, L3_attn_b_out, L3_ffn_w12, L3_ffn_w3, L3_ffn_gate_w):
    import jax
    import jax.numpy as jnp

    def _L0_tok_ref(x, W_qkv, b_qkv, W_out, b_out, ln_gamma, ln_beta):
        import jax, jax.numpy as jnp
        import numpy as np
        D_MODEL = 256
        NUM_HEADS = 16
        HEAD_DIM = D_MODEL // NUM_HEADS
        LN_EPS = 1e-05
        x = jnp.squeeze(x, axis=1)
        B, S, D = x.shape
        qkv = x @ W_qkv + b_qkv
        qkv = qkv.reshape(B, S, NUM_HEADS, 3 * HEAD_DIM).transpose(0, 2, 1, 3)
        q, k, v = jnp.split(qkv, 3, axis=-1)
        scaled = jnp.einsum('bhqd,bhkd->bhqk', q, k) / jnp.sqrt(jnp.float32(HEAD_DIM))
        attn = jax.nn.softmax(scaled, axis=-1)
        values = jnp.einsum('bhqk,bhkd->bhqd', attn, v)
        values = values.transpose(0, 2, 1, 3).reshape(B, S, D)
        out = values @ W_out + b_out
        h = out + x
        mu = jnp.mean(h, axis=-1, keepdims=True)
        var = jnp.mean(jnp.square(h - mu), axis=-1, keepdims=True)
        return (h - mu) * jax.lax.rsqrt(var + LN_EPS) * ln_gamma + ln_beta

    def _L0_attn_ref(x, Wqkv, Wout, alpha, beta):
        import jax, jax.numpy as jnp
        import numpy as np
        import math
        D_MODEL = 256
        N_HEADS = 16
        HEAD_DIM = D_MODEL // N_HEADS
        R = HEAD_DIM // 2
        ROPE_BASE = 10000.0
        B, T = (4, 512)

        def _fourier_bias(alpha, beta, t):
            omega = ROPE_BASE ** (-2.0 * jnp.arange(R, dtype=jnp.float32) / HEAD_DIM)
            disp = jnp.arange(-(t - 1), t, dtype=jnp.float32)
            angles = omega[:, None] * disp[None, :]
            vec = jnp.einsum('hr,rk->hk', alpha, jnp.cos(angles)) + jnp.einsum('hr,rk->hk', beta, jnp.sin(angles))
            i = jnp.arange(t)
            idx = i[:, None] - i[None, :] + (t - 1)
            return vec[:, idx]
        b, t, d = x.shape
        qkv = x @ Wqkv.T
        q, k, v = jnp.split(qkv, 3, axis=-1)

        def heads(a):
            return a.reshape(b, t, N_HEADS, HEAD_DIM).transpose(0, 2, 1, 3)
        q, k, v = (heads(q), heads(k), heads(v))
        scale = 1.0 / math.sqrt(HEAD_DIM)
        logits = jnp.einsum('bhqd,bhkd->bhqk', q, k) * scale
        logits = logits + _fourier_bias(alpha, beta, t)[None]
        causal = jnp.tril(jnp.ones((t, t), dtype=bool))
        logits = jnp.where(causal[None, None], logits, -jnp.inf)
        attn = jax.nn.softmax(logits, axis=-1)
        out = jnp.einsum('bhqk,bhkd->bhqd', attn, v)
        out = out.transpose(0, 2, 1, 3).reshape(b, t, d)
        return out @ Wout.T

    def _L0_ffn_ref(x, t_emb, sw1, sb1, sw3, sb3, sw2, sb2, w1, b1, w2, b2):
        import jax, jax.numpy as jnp
        import numpy as np
        E = 8
        TOPK = 2
        PRIME = 11
        HASH_OFF = 7919
        N_SHARED = 1
        B, T, C = x.shape
        N = B * T
        xf = x.reshape(N, C)
        shared = jax.nn.silu(xf @ sw1 + sb1) * (xf @ sw3 + sb3) @ sw2 + sb2
        tok = jnp.arange(N)
        out = jnp.zeros((N, C), x.dtype)
        for k in range(TOPK):
            exp_ids = (tok * PRIME + k * HASH_OFF) % E
            sort_idx = jnp.argsort(exp_ids)
            xs = xf[sort_idx].reshape(E, N // E, C)
            h = jax.nn.gelu(jnp.einsum('enc,ech->enh', xs, w1) + b1[:, None, :], approximate=False)
            y = jnp.einsum('enh,ehc->enc', h, w2) + b2[:, None, :]
            out = out.at[sort_idx].add(y.reshape(N, C))
        out = out / TOPK
        return ((shared + out) / (N_SHARED + 1)).reshape(B, T, C)

    def _L1_attn_ref(hidden_states, Wq, Wk, Wv, Wo):
        import jax, jax.numpy as jnp
        import numpy as np
        HEADS = 16
        EPS = 1e-06
        b, t, dim = hidden_states.shape
        h = HEADS
        d = dim // h

        def proj(W):
            return (hidden_states @ W.T).reshape(b, t, h, d).transpose(0, 2, 1, 3)
        q = proj(Wq) * d ** (-0.5)
        k = proj(Wk)
        v = proj(Wv)
        s = jnp.einsum('bhqd,bhkd->bhqk', q, k)
        attn = 1.0 + s + 0.5 * s * s
        causal = jnp.tril(jnp.ones((t, t), dtype=bool))
        attn = jnp.where(causal, attn, 0.0)
        o = jnp.einsum('bhqk,bhkd->bhqd', attn, v)
        z = jnp.sum(attn, axis=-1, keepdims=True) + EPS
        o = o / z
        y = o.transpose(0, 2, 1, 3).reshape(b, t, dim)
        return y @ Wo.T

    def _L1_ffn_ref(inputs_embeds, enc_w, enc_b, s2c_w, s2c_b, r_w1, r_b1, r_w2, r_b2, e_w1, e_b1, e_w2, e_b2, c2s_w, c2s_b, dec_w, dec_b, ln_g, ln_b):
        import jax, jax.numpy as jnp
        import numpy as np
        D_MODEL = 256
        HIDDEN = 512
        MOE_DIM = 64
        N_EXPERTS = 8
        TOP_K = 2
        EXP_HIDDEN = HIDDEN // 2
        B, S = (4, 512)
        b, s, _ = inputs_embeds.shape
        spikes = jax.nn.sigmoid(inputs_embeds @ enc_w + enc_b)
        cont = spikes.reshape(b * s, -1) @ s2c_w + s2c_b
        rh = jax.nn.relu(cont @ r_w1 + r_b1)
        probs = jax.nn.softmax(rh @ r_w2 + r_b2, axis=-1)
        topw, topi = jax.lax.top_k(probs, TOP_K)
        topw = topw / jnp.sum(topw, axis=-1, keepdims=True)
        comb = jnp.sum(jax.nn.one_hot(topi, N_EXPERTS, dtype=cont.dtype) * topw[..., None], axis=1)
        eh = jax.nn.relu(jnp.einsum('nd,edh->neh', cont, e_w1) + e_b1)
        eo = jnp.einsum('neh,ehd->ned', eh, e_w2) + e_b2
        moe_out = jnp.einsum('ned,ne->nd', eo, comb)
        rates = jax.nn.sigmoid(moe_out @ c2s_w + c2s_b)
        x = rates.reshape(b, s, -1)
        dec = jax.nn.sigmoid(x @ dec_w + dec_b)
        mu = jnp.mean(dec, axis=-1, keepdims=True)
        var = jnp.var(dec, axis=-1, keepdims=True)
        return (dec - mu) * jax.lax.rsqrt(var + 1e-05) * ln_g + ln_b

    def _L2_attn_ref(x, Wq, Wk, Wv, Wr):
        import jax, jax.numpy as jnp
        import numpy as np
        HEADS = 16
        HEAD_DIM = 64
        EMB = 256
        B, S = (4, 512)
        SCALE = 1.0 / 8.0
        MASK_PENALTY = -50.0
        b, s, _ = x.shape
        q = (x @ Wq).reshape(b, s, HEADS, HEAD_DIM)
        k = (x @ Wk).reshape(b, s, HEADS, HEAD_DIM)
        v = (x @ Wv).reshape(b, s, HEADS, HEAD_DIM)
        scores = SCALE * jnp.einsum('bqhd,bkhd->bhqk', q, k)
        causal = jnp.triu(jnp.ones((s, s), dtype=x.dtype), k=1)
        scores = scores + MASK_PENALTY * causal
        attn = jax.nn.softmax(scores, axis=-1)
        out = jnp.einsum('bhqk,bkhd->bqhd', attn, v).reshape(b, s, HEADS * HEAD_DIM)
        return out @ Wr

    def _L2_ffn_ref(x, ln1_g, ln1_b, Wqkv, bqkv, Wo, bo, ln2_g, ln2_b, gate_w, W1, b1, W2, b2, rW1, rb1, rW2, rb2, coef_w, coef_b):
        import jax, jax.numpy as jnp
        import numpy as np
        DIM, HEADS, FFN, E = (256, 16, 1024, 8)
        B, S = (2, 256)
        EPS = 1e-05

        def _ln(x, g, b):
            mu = jnp.mean(x, axis=-1, keepdims=True)
            var = jnp.mean((x - mu) ** 2, axis=-1, keepdims=True)
            return (x - mu) * jax.lax.rsqrt(var + EPS) * g + b
        b, s, d = x.shape
        h, dh = (HEADS, d // HEADS)
        xn = _ln(x, ln1_g, ln1_b)
        qkv = xn @ Wqkv + bqkv
        q, k, v = jnp.split(qkv, 3, axis=-1)
        q = q.reshape(b, s, h, dh)
        k = k.reshape(b, s, h, dh)
        v = v.reshape(b, s, h, dh)
        scores = jnp.einsum('bqhd,bkhd->bhqk', q, k) / jnp.sqrt(jnp.float32(dh))
        attn = jax.nn.softmax(scores, axis=-1)
        ctx = jnp.einsum('bhqk,bkhd->bqhd', attn, v).reshape(b, s, d)
        x = x + ctx @ Wo + bo
        xn2 = _ln(x, ln2_g, ln2_b)
        xt = xn2.reshape(b * s, d)
        probs = jax.nn.softmax(xt @ gate_w, axis=-1)
        gate_val = jnp.max(probs, axis=-1, keepdims=True)
        expert_idx = jnp.argmax(probs, axis=-1)
        oh = jax.nn.one_hot(expert_idx, E, dtype=xt.dtype)
        xe = jnp.einsum('te,td->etd', oh, xt)
        he = jax.nn.gelu(jnp.einsum('etd,edf->etf', xe, W1) + b1[:, None, :], approximate=False)
        ye = jnp.einsum('etf,efd->etd', he, W2) + b2[:, None, :]
        moe_out = jnp.einsum('te,etd->td', oh, ye) * gate_val
        rm = jax.nn.gelu(xt @ rW1 + rb1, approximate=False) @ rW2 + rb2
        coef = jax.nn.softmax(xt @ coef_w + coef_b, axis=-1)
        ff = moe_out * coef[:, 0:1] + rm * coef[:, 1:2]
        return x + ff.reshape(b, s, d)

    def _L3_attn_ref(x, ln_g, ln_b, w_qkv, b_qkv, w_ent, b_ent, w_out, b_out):
        import jax, jax.numpy as jnp
        import numpy as np
        H = 256
        NH = 16
        HD = H // NH
        B, S = (2, 512)
        b, s, h = x.shape
        scale = 1.0 / jnp.sqrt(jnp.float32(HD))
        TEMP = 0.1
        mu = jnp.mean(x, axis=-1, keepdims=True)
        var = jnp.mean(jnp.square(x - mu), axis=-1, keepdims=True)
        xn = (x - mu) / jnp.sqrt(var + 1e-06) * ln_g + ln_b
        qkv = xn @ w_qkv.T + b_qkv
        qkv = qkv.reshape(b, s, 3, NH, HD).transpose(2, 0, 3, 1, 4)
        q, k, v = (qkv[0], qkv[1], qkv[2])
        scores = jnp.einsum('bhqd,bhkd->bhqk', q, k) * scale
        causal = jnp.tril(jnp.ones((s, s), dtype=bool))
        scores = jnp.where(causal[None, None], scores, -jnp.inf)
        probs = jax.nn.softmax(scores / TEMP, axis=-1)
        gate = jax.nn.sigmoid(xn @ w_ent.T + b_ent)
        gate = jnp.clip(gate, 0.1, 2.0)[:, None, None, :, 0]
        probs = probs * gate
        out = jnp.einsum('bhqk,bhkd->bhqd', probs, v)
        out = out.transpose(0, 2, 1, 3).reshape(b, s, h)
        return (out @ w_out.T + b_out) * 0.1

    def _L3_ffn_ref(x, w12, w3, gate_w):
        import jax, jax.numpy as jnp
        import numpy as np
        TOP_K = 2
        E = gate_w.shape[0]
        H = w3.shape[-1]
        scores = jnp.einsum('btd,ed->bte', x, gate_w)
        topk_scores, topk_idx = jax.lax.top_k(scores, TOP_K)
        topk_probs = jax.nn.softmax(topk_scores, axis=-1)
        total_probs = jnp.sum(jax.nn.one_hot(topk_idx, E, dtype=topk_probs.dtype) * topk_probs[..., None], axis=-2)
        h12 = jnp.einsum('btd,ehd->bteh', x, w12)
        h1, h2 = (h12[..., :H], h12[..., H:])
        hidden = jax.nn.silu(h1) * h2
        expert_out = jnp.einsum('bteh,edh->bted', hidden, w3)
        y = jnp.sum(total_probs[..., None] * expert_out, axis=-2)
        return y
    h = _L0_tok_ref(x, L0_tok_W_qkv, L0_tok_b_qkv, L0_tok_W_out, L0_tok_b_out, L0_tok_ln_gamma, L0_tok_ln_beta)
    h = jnp.concatenate([h, txt], axis=1)
    h = h + _L0_attn_ref(_layernorm(h, axis=-1), L0_attn_Wqkv, L0_attn_Wout, L0_attn_alpha, L0_attn_beta)
    h = h + _L0_ffn_ref(_layernorm(h, axis=-1), L0_ffn_t_emb, L0_ffn_sw1, L0_ffn_sb1, L0_ffn_sw3, L0_ffn_sb3, L0_ffn_sw2, L0_ffn_sb2, L0_ffn_w1, L0_ffn_b1, L0_ffn_w2, L0_ffn_b2)
    h = h + _L1_attn_ref(_layernorm(h, axis=-1), L1_attn_Wq, L1_attn_Wk, L1_attn_Wv, L1_attn_Wo)
    h = h + _L1_ffn_ref(_layernorm(h, axis=-1), L1_ffn_enc_w, L1_ffn_enc_b, L1_ffn_s2c_w, L1_ffn_s2c_b, L1_ffn_r_w1, L1_ffn_r_b1, L1_ffn_r_w2, L1_ffn_r_b2, L1_ffn_e_w1, L1_ffn_e_b1, L1_ffn_e_w2, L1_ffn_e_b2, L1_ffn_c2s_w, L1_ffn_c2s_b, L1_ffn_dec_w, L1_ffn_dec_b, L1_ffn_ln_g, L1_ffn_ln_b)
    h = h + _L2_attn_ref(_layernorm(h, axis=-1), L2_attn_Wq, L2_attn_Wk, L2_attn_Wv, L2_attn_Wr)
    h = h + _L2_ffn_ref(_layernorm(h, axis=-1), L2_ffn_ln1_g, L2_ffn_ln1_b, L2_ffn_Wqkv, L2_ffn_bqkv, L2_ffn_Wo, L2_ffn_bo, L2_ffn_ln2_g, L2_ffn_ln2_b, L2_ffn_gate_w, L2_ffn_W1, L2_ffn_b1, L2_ffn_W2, L2_ffn_b2, L2_ffn_rW1, L2_ffn_rb1, L2_ffn_rW2, L2_ffn_rb2, L2_ffn_coef_w, L2_ffn_coef_b)
    h = h + _L3_attn_ref(_layernorm(h, axis=-1), L3_attn_ln_g, L3_attn_ln_b, L3_attn_w_qkv, L3_attn_b_qkv, L3_attn_w_ent, L3_attn_b_ent, L3_attn_w_out, L3_attn_b_out)
    h = h + _L3_ffn_ref(_layernorm(h, axis=-1), L3_ffn_w12, L3_ffn_w3, L3_ffn_gate_w)
    return h

_drawn_inputs = setup_inputs


def setup_inputs(seed=0):
    import zlib

    import numpy as np

    out = dict(_drawn_inputs(seed))
    spreads = {'L0_tok_b_qkv': (0.0, 0.1),
     'L0_tok_b_out': (0.0, 0.1),
     'L0_tok_ln_gamma': (1.0, 0.2),
     'L0_tok_ln_beta': (0.0, 0.1),
     'L0_ffn_sb1': (0.0, 0.285),
     'L0_ffn_sb3': (0.0, 0.285),
     'L0_ffn_sb2': (0.0, 0.1),
     'L0_ffn_b1': (0.0, 0.32),
     'L0_ffn_b2': (0.0, 0.1),
     'L1_ffn_enc_b': (0.0, 0.304),
     'L1_ffn_s2c_b': (0.0, 0.1),
     'L1_ffn_r_b1': (0.0, 0.1),
     'L1_ffn_r_b2': (0.0, 0.1),
     'L1_ffn_e_b1': (0.0, 0.404),
     'L1_ffn_e_b2': (0.0, 0.311),
     'L1_ffn_c2s_b': (0.0, 0.1),
     'L1_ffn_dec_b': (0.0, 0.1),
     'L1_ffn_ln_g': (1.0, 0.2),
     'L1_ffn_ln_b': (0.0, 0.1),
     'L2_ffn_ln1_g': (1.0, 0.6),
     'L2_ffn_ln1_b': (0.0, 0.8),
     'L2_ffn_bqkv': (0.0, 0.446),
     'L2_ffn_bo': (0.0, 0.1),
     'L2_ffn_ln2_g': (1.0, 0.6),
     'L2_ffn_ln2_b': (0.0, 0.8),
     'L2_ffn_b1': (0.0, 0.8),
     'L2_ffn_b2': (0.0, 0.8),
     'L2_ffn_rb1': (0.0, 1.863),
     'L2_ffn_rb2': (0.0, 0.343),
     'L2_ffn_coef_b': (0.0, 0.8),
     'L3_attn_ln_g': (1.0, 0.6),
     'L3_attn_ln_b': (0.0, 0.8),
     'L3_attn_b_qkv': (0.0, 0.8),
     'L3_attn_b_out': (0.0, 2.0)}
    factors = {'L0_attn_alpha': 8.0,
     'L0_attn_beta': 8.0,
     'L1_attn_Wq': 8.0,
     'L1_attn_Wk': 8.0,
     'L2_attn_Wq': 8.0,
     'L2_attn_Wk': 8.0,
     'L2_ffn_gate_w': 5.879,
     'L2_ffn_W1': 6.295,
     'L2_ffn_W2': 6.636,
     'L2_ffn_coef_w': 7.345,
     'L3_attn_w_qkv': 8.0,
     'L3_attn_w_ent': 8.0,
     'L3_attn_w_out': 8.0,
     'L2_ffn_rW1': 2.77}
    for name, (base, spread) in spreads.items():
        noise = np.random.default_rng([zlib.crc32(name.encode()), seed]).standard_normal(out[name].shape)
        drawn = base * np.exp(spread * noise) if base else spread * noise
        out[name] = jnp.asarray(drawn.astype(out[name].dtype))
    for name, factor in factors.items():
        out[name] = (out[name] * factor).astype(out[name].dtype)
    return out
```

```python
import concourse.bass as bass
from concourse import mybir
from contextlib import ExitStack, contextmanager

F32 = mybir.dt.float32
BF16 = mybir.dt.bfloat16
ALU = mybir.AluOpType
ACT = mybir.ActivationFunctionType
AX = mybir.AxisListType

P = 128
B = 4
S_IMG, S_TXT = 512, 32
T = S_IMG + S_TXT
D = 256
KC = D // P
NH = 16
HD = 16
HD2 = 64
E = 8
BANK = 512
VW = 32
PART_ROWS = 6 * HD
MAX_ROW = 96
K_PARTS = (0, 0, 0, 1, 1, 2)
Q_PARTS = (0, 1, 2, 0, 1, 0)

VECTORS = [
    ("zero", 4), ("eps5", 1), ("eps6", 1), ("root_half", 1),
    ("tok_bq", 2), ("tok_bk", 2), ("tok_bo", 2), ("tok_g", 2), ("tok_b", 2),
    ("f0_sb1", 4), ("f0_sb3", 4), ("f0_sb2", 2), ("f0_b1", 16), ("f0_b2", 16),
    ("f1_enc", 4), ("f1_s2c", 1), ("f1_rb1", 1), ("f1_eb1", 16), ("f1_c2s", 4), ("f1_dec", 2),
    ("f1_g", 2), ("f1_b", 2),
    ("a2_g1", 2), ("a2_b1", 2), ("a2_bq", 2), ("a2_bk", 2), ("a2_bo", 2), ("a2_g2", 2), ("a2_b2", 2),
    ("f2_b1", 72),
    ("a3_g", 2), ("a3_b", 2), ("a3_bq", 2), ("a3_bk", 2), ("a3_bo", 2),
]
ROWS = [("tok_bv", D), ("a2_bv", D), ("a3_bv", D), ("f1_rb2", E), ("f2_coefb", 2), ("a3_ent", 1), ("falling", E)]
CONSTS = [("mean", P), ("ident", P), ("sum_rows", P), ("sum_rows2", HD2), ("pick", 9 * P),
          ("trig", T), ("fix_k", T), ("fix_q", T)]
CONSTS16 = [("ident", P), ("hard_q", P), ("hard_k", P), ("soft_q", P), ("soft_k", P),
            ("stack", 2 * 3 * 8 * PART_ROWS), ("trig_k", T)]


def columns(table):
    at, out = 0, {}
    for name, n in table:
        out[name] = (at, n)
        at += n
    return out, at


def chunks(n):
    return [(a, min(P, n - a)) for a in range(0, n, P)]


@contextmanager
def stage(nc, label):
    numbers = []
    with ExitStack() as scope:
        def sb(name, shape, dt):
            return scope.enter_context(nc.sbuf_tensor(f"{label}_{name}", shape, dt))

        def sem(name):
            s = scope.enter_context(nc.semaphore(f"{label}_{name}"))
            numbers.append(s.num)
            return s

        with nc.Block() as block:
            yield block, sb, sem
        nc.all_engine_barrier(sems_to_clear=range(min(numbers), max(numbers) + 1))


class Chain:

    def __init__(self, eng, sem):
        self.eng, self.sem, self.n = eng, sem, 0

    def __call__(self, ins):
        self.n += 1
        ins.then_inc(self.sem, 1)
        self.eng.wait_ge(self.sem, self.n)


def layer_norm(nc, env, label, src, dst, n, eps, gamma=None, beta=None, add_to=None):
    ps, vec = env["ps"], env["vec"]
    half = n // 2
    pieces = [(0, half), (half, n)]
    with stage(nc, label) as (block, sb, sem):
        square = sb("square", [P, KC, n], F32)
        std = sb("std", [P, 2, half], F32)
        rstd = sb("rstd", [P, 2, half], F32)
        mean_ready, centered, squared, var_ready, std_ready, step = map(
            sem, ("mean_ready", "centered", "squared", "var_ready", "std_ready", "step"))

        @block.tensor
        def _(pe):
            for i, (a, b) in enumerate(pieces):
                for c in range(KC):
                    mm = pe.matmul(ps[:, i, 0:half], env["c"]("mean"), src[:, c, a:b],
                                   start=(c == 0), stop=(c == KC - 1))
                mm.then_inc(mean_ready, 1)
            for i, (a, b) in enumerate(pieces):
                pe.wait_ge(squared, i + 1)
                for c in range(KC):
                    mm = pe.matmul(ps[:, 2 + i, 0:half], env["c"]("mean"), square[:, c, a:b],
                                   start=(c == 0), stop=(c == KC - 1))
                mm.then_inc(var_ready, 1)

        @block.scalar
        def _(act):
            for i, (a, b) in enumerate(pieces):
                act.wait_ge(centered, i + 1)
                act.activation(square[:, :, a:b], dst[:, :, a:b], ACT.Square).then_inc(squared, 1)
            for i in range(2):
                act.wait_ge(var_ready, i + 1)
                act.activation(std[:, i, :], ps[:, 2 + i, 0:half], ACT.Sqrt, bias=vec(eps)).then_inc(std_ready, 1)

        @block.vector
        def _(dve):
            chain = Chain(dve, step)
            for i, (a, b) in enumerate(pieces):
                dve.wait_ge(mean_ready, i + 1)
                for c in range(KC):
                    v = dve.tensor_tensor(dst[:, c, a:b], src[:, c, a:b], ps[:, i, 0:half], ALU.subtract)
                v.then_inc(centered, 1)
            for i, (a, b) in enumerate(pieces):
                dve.wait_ge(std_ready, i + 1)
                chain(dve.reciprocal(rstd[:, i, :], std[:, i, :]))
                for c in range(KC):
                    chain(dve.tensor_tensor(dst[:, c, a:b], dst[:, c, a:b], rstd[:, i, :], ALU.mult))
                    if gamma:
                        chain(dve.tensor_scalar(dst[:, c, a:b], dst[:, c, a:b], vec(gamma, c), vec(beta, c),
                                                ALU.mult, ALU.add))
                    if add_to is not None:
                        chain(dve.tensor_tensor(add_to[:, c, a:b], add_to[:, c, a:b], dst[:, c, a:b], ALU.add))


def attention_steps(wide, causal, poly, bias, gate, qk_groups, heads, slots, nch, n):
    count = [0]

    def use(kind, *args):
        count[0] += 1
        return (kind, *args, count[0] - 1)

    sides = "kqb" if bias else "kq"
    steps = []
    if not wide:
        steps += [use("dense", side, mc) for side in sides for mc in range(KC)]
    steps += [use("value", t, w) for t in range(nch) for w in range(2 if wide else 1)]

    def stacks(g):
        return [use("stack", side, g, h) for side in sides for h in range(heads)]

    def maxima(g):
        return [("smax", g, h, t) for t in range(nch) for h in range(heads)]

    def rows(g):
        return [use("mrow", g, h) for h in range(0, heads, min(heads, 2))]

    def numbered(step):
        return use(*step)

    steps += stacks(0)
    if not poly:
        steps += [numbered(s) for s in maxima(0)] + rows(0)
    blocks = [(g, t) for g in range(qk_groups) for t in range(nch)]
    ahead = []
    for i, (g, t) in enumerate(blocks):
        if t == 0 and g + 1 < qk_groups:
            steps += stacks(g + 1)
            ahead = [] if poly else maxima(g + 1)
        share = -(-len(ahead) // (nch - t)) if ahead else 0
        now, ahead = ahead[:share], ahead[share:]
        for h in range(heads):
            steps.append(use("prob", g, t, h))
            k = -(-len(now) // (heads - h))
            steps += [numbered(s) for s in now[:k]]
            now = now[k:]
        if i:
            steps.append(("av", *blocks[i - 1]))
            if blocks[i - 1][1] == nch - 1:
                steps.append(("ocopy", blocks[i - 1][0]))
            if i > 1 and blocks[i - 2][1] == nch - 1:
                steps.append(use("norm", blocks[i - 2][0]))
        if t == nch - 1 and g + 1 < qk_groups and not poly:
            steps += rows(g + 1)
    steps.append(("av", *blocks[-1]))
    steps.append(("ocopy", blocks[-1][0]))
    steps.append(use("norm", blocks[-1][0]))
    return steps


def attention(nc, env, label, x, n, wqkv, out, causal=False, poly=False, bias=False, wide=False,
              bq="zero", bk="zero", bv=None, gate=None, q_scale=1.0, exp_scale=1.0):
    ps, vec, c32, c16, row = env["ps"], env["vec"], env["c"], env["c16"], env["row"]
    heads = 1 if wide else 4
    groups = NH // heads
    slots = 2 if wide else 3
    sums = 2 if wide else 1
    hd = HD2 if wide else HD
    krows = P if wide else MAX_ROW + 3
    srows = P if wide else PART_ROWS
    cut = 256 if causal and not wide else n // 2
    toks = chunks(n)
    steps = attention_steps(wide, causal, poly, bias, gate, groups, heads, slots, len(toks), n)
    qdt = F32 if wide else BF16
    hard = causal and not wide
    mask_q, mask_k = c16("soft_q" if wide else "hard_q"), c16("soft_k" if wide else "hard_k")

    def bank(use, i):
        return 2 * (use % slots) + i

    def both(use, rows, w, lo=0):
        k = 2 * (use % slots)
        return ps[lo:rows, k:k + 2, 0:w]

    def q_pieces(t):
        a = P * t if hard else 0
        return [(i, max(a, lo), hi) for i, (lo, hi) in enumerate([(0, cut), (cut, n)]) if hi > a]

    def key_end(t):
        return min(P * (t + 1), n) if hard else n

    with stage(nc, label) as (block, sb, sem):
        if not wide:
            dense = {s: sb(f"dense_{s}", [P, KC, n], F32) for s in ("kqb" if bias else "kq")}
            part = {s: [sb(f"part_{s}{j}", [P, KC, n], BF16) for j in range(3)] for s in dense}
            rest = {s: sb(f"rest_{s}", [P, KC, n], F32) for s in "kq"}
            rest["b"] = rest["q"]
        kst = [sb(f"kst{i}", [P, heads, n], qdt) for i in range(2)]
        qst = [sb(f"qst{i}", [P, heads, n], qdt) for i in range(2)]
        bst = [sb(f"bst{i}", [PART_ROWS, heads, n], BF16) for i in range(2)] if bias else None
        vw = HD2 + 1 if wide else VW
        value = sb("value", [P, len(toks), NH, vw], F32)
        prob = sb("prob", [P, 2 * heads, n], F32)
        osum = sb("osum", [P, 2, n], F32)
        inv = sb("inv", [P, n], F32)
        maxes = sb("maxes", [P, len(toks), heads], F32)
        mneg = sb("mneg", [P, len(toks), heads], F32)
        mrest = sb("mrest", [P, len(toks), heads], F32)
        mparts = [sb(f"mparts{i}", [P, len(toks), heads, 3], BF16) for i in range(2)]
        gates = sb("gates", [P, len(toks)], F32)
        filled = [sem(f"filled{i}") for i in range(slots)]
        freed = [sem(f"freed{i}") for i in range(slots)]
        zeroed, set_up = sem("zeroed"), sem("set_up")
        dense_ready = {s: sem(f"dense_ready_{s}") for s in "kqb"}
        split_k, split_q, split_b = sem("split_k"), sem("split_q"), sem("split_b")
        pool_step, dve_step = sem("pool_step"), sem("dve_step")
        values_ready, gate_ready = sem("values_ready"), sem("gate_ready")
        k_stacked, q_stacked, b_stacked = sem("k_stacked"), sem("q_stacked"), sem("b_stacked")
        mparts_ready, mrows_ready = sem("mparts_ready"), sem("mrows_ready")
        exps_ready, shifted, masked = sem("exps_ready"), sem("shifted"), sem("masked")
        probs_used, sums_ready, sums_copied = sem("probs_used"), sem("sums_ready"), sem("sums_copied")
        inv_ready, normalised = sem("inv_ready"), sem("normalised")

        split_ready = {"k": split_k, "q": split_q, "b": split_b}
        stacked = {"k": k_stacked, "q": q_stacked, "b": b_stacked}
        stack = {"k": kst, "q": qst, "b": bst}

        def mask_into(pe, use, pieces, rows, lo, mask, width):
            for i, a, b in pieces:
                u, v = max(a, lo), min(b, lo + rows)
                if u < v:
                    mm = pe.matmul(ps[0:rows, bank(use, i), u - width(i, a):v - width(i, a)],
                                   c16("ident")[0:rows, 0:rows], mask[0:rows, u - lo:v - lo],
                                   start=False, stop=True, skip_group_check=True)
            return mm

        def sum_bank(g, i):
            return 2 * slots + 2 * (g % sums) + i

        @block.tensor
        def _(pe):
            pe.wait_ge(set_up, 1)
            for step in steps:
                kind, use = step[0], step[-1]
                if kind not in ("av", "ocopy") and use >= slots:
                    pe.wait_ge(freed[use % slots], use // slots)
                if kind == "dense":
                    _, side, mc, _ = step
                    for i, (a, b) in enumerate([(0, n // 2), (n // 2, n)]):
                        if side == "b":
                            mm = pe.matmul(ps[:, bank(use, i), 0:b - a], env["alpha_beta"][0:24, mc * P:mc * P + P],
                                           c32("trig")[0:24, a:b], start=True, stop=True)
                            continue
                        off = (D if side == "k" else 0) + mc * P
                        for c in range(KC):
                            mm = pe.matmul(ps[:, bank(use, i), 0:b - a], wqkv[:, c, off:off + P], x[:, c, a:b],
                                           start=(c == 0), stop=(c == KC - 1))
                    mm.then_inc(filled[use % slots], 1)
                elif kind == "value":
                    _, t, w, _ = step
                    a, rows = toks[t]
                    width = 512 if wide else D + (1 if gate else 0)
                    off = 2 * NH * hd + w * 512
                    for c in range(KC):
                        mm = pe.matmul(ps[0:rows, bank(use, 0), 0:width], x[:, c, a:a + rows],
                                       wqkv[:, c, off:off + width], start=(c == 0), stop=(c == KC - 1))
                    mm.then_inc(filled[use % slots], 1)
                elif kind == "stack":
                    _, side, g, h, _ = step
                    head = g * heads + h
                    if not wide and g == 0 and h == 0:
                        pe.wait_ge(split_ready[side], 1)
                    for i, (a, b) in enumerate([(0, n // 2), (n // 2, n)]):
                        if wide:
                            off = (NH * hd if side == "k" else 0) + head * hd
                            for c in range(KC):
                                mm = pe.matmul(ps[0:hd, bank(use, i), 0:b - a], wqkv[:, c, off:off + hd],
                                               x[:, c, a:b], start=(c == 0), stop=(c == KC - 1))
                        else:
                            for j in range(3):
                                mm = pe.matmul(ps[0:PART_ROWS, bank(use, i), 0:b - a],
                                               env["pick_parts"](side, j, head % 8),
                                               part[side][j][:, head // 8, a:b], start=(j == 0), stop=(j == 2))
                    mm.then_inc(filled[use % slots], 1)
                elif kind == "smax":
                    _, g, h, t, _ = step
                    a, rows = toks[t]
                    if t == 0:
                        pe.wait_ge(k_stacked, g * heads + h + 1)
                        pe.wait_ge(q_stacked, g * heads + h + 1)
                        if bias:
                            pe.wait_ge(b_stacked, g * heads + h + 1)
                    w = key_end(t) // 2
                    pieces = [(0, 0, w), (1, w, 2 * w)]
                    for i, u, v in pieces:
                        mm = pe.matmul(ps[0:rows, bank(use, i), 0:w], qst[g % 2][0:srows, h, a:a + rows],
                                       kst[g % 2][0:srows, h, u:v], start=True, stop=not (bias or hard or wide),
                                       skip_group_check=True)
                        if bias:
                            mm = pe.matmul(ps[0:rows, bank(use, i), 0:w], bst[g % 2][:, h, a:a + rows],
                                           c16("trig_k")[0:PART_ROWS, u:v], start=False, stop=True,
                                           skip_group_check=True)
                    if hard or wide:
                        mm = mask_into(pe, use, pieces, rows, a, mask_q, lambda i, u: u)
                    mm.then_inc(filled[use % slots], 1)
                elif kind == "mrow":
                    _, g, h, _ = step
                    pe.wait_ge(mparts_ready, g + 1)
                    for i in range(min(heads, 2)):
                        out16 = ps[:, bank(use, i), :].bitcast(BF16)
                        for t, (a, rows) in enumerate(toks):
                            mm = pe.transpose(out16[MAX_ROW:MAX_ROW + 3, a:a + rows],
                                              mparts[g % 2][0:rows, t, h + i, :], c16("ident")[0:rows, 0:rows])
                    mm.then_inc(filled[use % slots], 1)
                elif kind == "prob":
                    _, g, t, h, _ = step
                    a, rows = toks[t]
                    if t == 0:
                        if poly:
                            pe.wait_ge(k_stacked, g * heads + h + 1)
                            pe.wait_ge(q_stacked, g * heads + h + 1)
                        else:
                            pe.wait_ge(mrows_ready, g * (heads // min(heads, 2)) + h // 2 + 1)
                    k = PART_ROWS if poly else krows
                    pieces = q_pieces(t)
                    for i, u, v in pieces:
                        mm = pe.matmul(ps[0:rows, bank(use, i), 0:v - u], kst[g % 2][0:k, h, a:a + rows],
                                       qst[g % 2][0:k, h, u:v], start=True, stop=not (bias or (hard and not poly) or wide),
                                       skip_group_check=True)
                        if bias:
                            mm = pe.matmul(ps[0:rows, bank(use, i), 0:v - u], c16("trig_k")[0:PART_ROWS, a:a + rows],
                                           bst[g % 2][:, h, u:v], start=False, stop=True, skip_group_check=True)
                    if (hard and not poly) or wide:
                        mm = mask_into(pe, use, pieces, rows, a, mask_k, lambda i, u: u)
                    mm.then_inc(filled[use % slots], 1)
                elif kind == "av":
                    _, g, t = step
                    a, rows = toks[t]
                    block_no = g * len(toks) + t
                    if block_no == 0:
                        pe.wait_ge(values_ready, len(toks) * (2 if wide else 1))
                    pe.wait_ge(masked if poly else exps_ready, (block_no + 1) * heads)
                    if t == 0 and g >= sums:
                        pe.wait_ge(sums_copied, g - sums + 1)
                    for i, u, v in q_pieces(t):
                        o = u - (cut if i else 0)
                        for h in range(heads):
                            lo, m = (0, hd + 1) if wide else (VW * h, VW)
                            mm = pe.matmul(ps[lo:lo + m, sum_bank(g, i), o:o + v - u],
                                           value[0:rows, t, g * heads + h, :],
                                           prob[0:rows, (block_no % 2) * heads + h, u:v],
                                           start=(t == 0), stop=(t == len(toks) - 1), skip_group_check=True)
                    mm.then_inc(probs_used, 1)
                    if t == len(toks) - 1:
                        pass
                elif kind == "norm":
                    _, g, _ = step
                    pe.wait_ge(sums_copied, g + 1)
                    for i, (a, b) in enumerate([(0, n // 2), (n // 2, n)]):
                        if wide:
                            mm = pe.matmul(ps[0:hd, bank(use, i), 0:b - a], c32("sum_rows2")[0:hd + 1, :],
                                           osum[0:hd + 1, g % 2, a:b], start=True, stop=True)
                        else:
                            mm = pe.matmul(ps[:, bank(use, i), 0:b - a], c32("sum_rows"),
                                           osum[:, g % 2, a:b], start=True, stop=True)
                    mm.then_inc(filled[use % slots], 1)

        @block.scalar
        def _(act):
            act.wait_ge(set_up, 1)
            for step in steps:
                kind, use = step[0], step[-1]
                if kind == "dense":
                    _, side, mc, _ = step
                    act.wait_ge(filled[use % slots], use // slots + 1)
                    b = vec({"q": bq, "k": bk, "b": "zero"}[side], mc)
                    act.activation(dense[side][:, mc, :].rearrange("p (i w) -> p i w", i=2), both(use, P, n // 2),
                                   ACT.Identity, bias=b, scale=(q_scale if side == "q" else 1.0))\
                        .then_inc(freed[use % slots], 1)
                    if mc == KC - 1:
                        for back in (1, 0):
                            act.wait_ge(freed[(use - back) % slots], (use - back) // slots + 1)
                        act.activation(part[side][0][:, :, :], dense[side][:, :, :], ACT.Copy)\
                            .then_inc(dense_ready[side], 1)
                elif kind == "value" and gate:
                    _, t, w, _ = step
                    rows = toks[t][1]
                    act.wait_ge(filled[use % slots], use // slots + 1)
                    act.activation(gates[0:rows, t:t + 1], ps[0:rows, bank(use, 0), D:D + 1], ACT.Sigmoid,
                                   bias=row(gate)[0:rows, :]).then_inc(gate_ready, 1)
                elif kind == "stack" and step[1] in "kb":
                    _, side, g, h, _ = step
                    rows = hd if wide else PART_ROWS
                    act.wait_ge(filled[use % slots], use // slots + 1)
                    act.activation(stack[side][g % 2][0:rows, h, :].rearrange("p (i w) -> p i w", i=2),
                                   both(use, rows, n // 2), ACT.Copy).then_inc(stacked[side], 1)
                    act.wait_ge(stacked[side], g * heads + h + 1)
                    act.sem_inc(freed[use % slots], 1)
                elif kind == "prob":
                    _, g, t, h, _ = step
                    rows = toks[t][1]
                    block_no = g * len(toks) + t
                    act.wait_ge(filled[use % slots], use // slots + 1)
                    if block_no >= 2 and h == 0:
                        act.wait_ge(probs_used, block_no - 1)
                    dst = prob[0:rows, (block_no % 2) * heads + h, :]
                    func = ACT.Square if poly else ACT.Exp
                    args = {"bias": vec("root_half")[0:rows], "scale": 0.5 ** 0.5} if poly else {"scale": exp_scale}
                    pieces = q_pieces(t)
                    if len(pieces) == 2 and pieces[0][2] - pieces[0][1] == pieces[1][2] - pieces[1][1]:
                        w = pieces[0][2] - pieces[0][1]
                        act.activation(dst[:, pieces[0][1]:n].rearrange("p (i w) -> p i w", i=2), both(use, rows, w),
                                       func, **args).then_inc(exps_ready, 1)
                    else:
                        for i, u, v in pieces:
                            e = act.activation(dst[:, u:v], ps[0:rows, bank(use, i), 0:v - u], func, **args)
                        e.then_inc(exps_ready, 1)
                    act.wait_ge(exps_ready, block_no * heads + h + 1)
                    act.sem_inc(freed[use % slots], 1)
                elif kind == "ocopy":
                    g = step[1]
                    act.wait_ge(probs_used, (g + 1) * len(toks))
                    if g >= 2:
                        act.wait_ge(normalised, g - 1)
                    rows = hd + 1 if wide else P
                    k = sum_bank(g, 0)
                    if cut * 2 == n:
                        act.activation(osum[0:rows, g % 2, :].rearrange("p (i w) -> p i w", i=2),
                                       ps[0:rows, k:k + 2, 0:cut], ACT.Copy).then_inc(sums_copied, 1)
                    else:
                        act.activation(osum[0:rows, g % 2, 0:cut], ps[0:rows, k, 0:cut], ACT.Copy)
                        act.activation(osum[0:rows, g % 2, cut:n], ps[0:rows, k + 1, 0:n - cut], ACT.Copy)\
                            .then_inc(sums_copied, 1)

        def split(eng, chain, side, done):
            chain(eng.tensor_tensor(rest[side][:, :, :], dense[side][:, :, :], part[side][0][:, :, :], ALU.subtract))
            chain(eng.tensor_copy(part[side][1][:, :, :], rest[side][:, :, :]))
            eng.tensor_tensor(part[side][2][:, :, :], rest[side][:, :, :], part[side][1][:, :, :],
                              ALU.subtract).then_inc(done, 1)

        @block.gpsimd
        def _(pool):
            chain = Chain(pool, pool_step)
            if wide:
                for i in range(2):
                    chain(pool.tensor_copy(kst[i][64:96, 0, :], c32("fix_k")[64:96, :]))
                    chain(pool.tensor_copy(qst[i][64:96, 0, :], c32("fix_q")[64:96, :]))
                    chain(pool.memset(kst[i][96:128, :, :], 0.0))
                    chain(pool.memset(qst[i][96:128, :, :], 0.0))
                    chain(pool.memset(kst[i][MAX_ROW:MAX_ROW + 3, :, :], 1.0))
            else:
                chain(pool.memset(value[:, :, :, :], 0.0))
                if not poly:
                    for i in range(2):
                        chain(pool.memset(kst[i][MAX_ROW:MAX_ROW + 3, :, :], 1.0))
            chain(pool.memset(value[:, :, :, hd:hd + 1], 1.0))
            pool.memset(maxes[:, :, :], 0.0).then_inc(set_up, 1)
            if not wide:
                pool.wait_ge(dense_ready["k"], 1)
                split(pool, chain, "k", split_k)
            for step in steps:
                kind = step[0]
                if kind == "prob" and poly:
                    _, g, t, h, _ = step
                    a, rows = toks[t]
                    block_no = g * len(toks) + t
                    pool.wait_ge(shifted, block_no * heads + h + 1)
                    d = prob[0:rows, (block_no % 2) * heads + h, a:a + rows]
                    pool.affine_select(out=d, in_=d, compare_op=ALU.is_ge, fill=0.0, base=0,
                                       pattern=[[1, rows]], channel_multiplier=-1).then_inc(masked, 1)
                elif kind == "norm":
                    g = step[1]
                    pool.wait_ge(inv_ready, g + 1)
                    rows = hd if wide else P
                    pool.tensor_tensor(out[0:rows, g, 0:n], osum[0:rows, g % 2, :], inv[0:rows, :],
                                       ALU.mult).then_inc(normalised, 1)

        @block.vector
        def _(dve):
            chain = Chain(dve, dve_step)
            dve.wait_ge(set_up, 1)
            for step in steps:
                kind, use = step[0], step[-1]
                if kind == "value":
                    _, t, w, _ = step
                    rows = toks[t][1]
                    dve.wait_ge(filled[use % slots], use // slots + 1)
                    nh = 8 if wide else NH
                    src = ps[0:rows, bank(use, 0), 0:nh * hd].rearrange("p (h d) -> p h d", h=nh)
                    dst = value[0:rows, t, w * nh:(w + 1) * nh, 0:hd]
                    if bv:
                        bias_row = row(bv)[0:rows, :].rearrange("p (h d) -> p h d", h=NH)
                        if gate:
                            dve.wait_ge(gate_ready, t + 1)
                        v = dve.tensor_tensor(dst, src, bias_row, ALU.add)
                    else:
                        v = dve.tensor_copy(dst, src)
                    v.then_inc(freed[use % slots], 1)
                    if gate:
                        chain(dve.tensor_scalar(gates[0:rows, t:t + 1], gates[0:rows, t:t + 1], 0.1, 2.0,
                                                ALU.max, ALU.min))
                        dve.wait_ge(freed[use % slots], use // slots + 1)
                        v = dve.tensor_scalar(dst, dst, gates[0:rows, t:t + 1], None, ALU.mult)
                        v.then_inc(values_ready, 1)
                    else:
                        dve.wait_ge(freed[use % slots], use // slots + 1)
                        dve.sem_inc(values_ready, 1)
                elif kind == "stack" and step[1] == "q":
                    _, side, g, h, _ = step
                    if not wide and g == 0 and h == 0:
                        pass
                    rows = hd if wide else PART_ROWS
                    dve.wait_ge(filled[use % slots], use // slots + 1)
                    dve.tensor_copy(qst[g % 2][0:rows, h, :].rearrange("p (i w) -> p i w", i=2),
                                    both(use, rows, n // 2)).then_inc(q_stacked, 1)
                    dve.wait_ge(q_stacked, g * heads + h + 1)
                    dve.sem_inc(freed[use % slots], 1)
                elif kind == "smax":
                    _, g, h, t, _ = step
                    rows = toks[t][1]
                    dve.wait_ge(filled[use % slots], use // slots + 1)
                    m = dve.tensor_reduce(maxes[0:rows, t, h:h + 1], both(use, rows, key_end(t) // 2),
                                          op=ALU.max, axis=AX.XY)
                    m.then_inc(freed[use % slots], 1)
                    if t == len(toks) - 1 and h == heads - 1:
                        for back in range(slots):
                            if use - back >= 0:
                                u = use - back
                        dve.wait_ge(freed[use % slots], use // slots + 1)
                        out3 = mparts[g % 2]
                        chain(dve.tensor_scalar(mneg[:, :, :], maxes[:, :, :], -1.0, None, ALU.mult))
                        chain(dve.tensor_copy(out3[:, :, :, 0], mneg[:, :, :]))
                        chain(dve.tensor_tensor(mrest[:, :, :], mneg[:, :, :], out3[:, :, :, 0], ALU.subtract))
                        chain(dve.tensor_copy(out3[:, :, :, 1], mrest[:, :, :]))
                        dve.tensor_tensor(out3[:, :, :, 2], mrest[:, :, :], out3[:, :, :, 1],
                                          ALU.subtract).then_inc(mparts_ready, 1)
                elif kind == "mrow":
                    _, g, h, _ = step
                    dve.wait_ge(filled[use % slots], use // slots + 1)
                    k = min(heads, 2)
                    b0 = bank(use, 0)
                    src = ps[:, b0:b0 + k, :].bitcast(BF16)
                    dve.tensor_copy(qst[g % 2][MAX_ROW:MAX_ROW + 3, h:h + k, :],
                                    src[MAX_ROW:MAX_ROW + 3, :, 0:n]).then_inc(mrows_ready, 1)
                    dve.wait_ge(mrows_ready, g * (heads // k) + h // 2 + 1)
                    dve.sem_inc(freed[use % slots], 1)
                elif kind == "prob" and poly:
                    _, g, t, h, _ = step
                    rows = toks[t][1]
                    block_no = g * len(toks) + t
                    dve.wait_ge(exps_ready, block_no * heads + h + 1)
                    a = q_pieces(t)[0][1]
                    d = prob[0:rows, (block_no % 2) * heads + h, a:n]
                    dve.tensor_scalar(d, d, 0.5, None, ALU.add).then_inc(shifted, 1)
                elif kind == "norm":
                    g = step[1]
                    dve.wait_ge(filled[use % slots], use // slots + 1)
                    if g:
                        dve.wait_ge(normalised, g)
                    rows = hd if wide else P
                    dst = inv[0:rows, :].rearrange("p (i w) -> p i w", i=2)
                    if poly:
                        chain(dve.tensor_scalar(dst, both(use, rows, n // 2), 1e-6, None, ALU.add))
                        dve.sem_inc(freed[use % slots], 1)
                        dve.reciprocal(dst, dst).then_inc(inv_ready, 1)
                    else:
                        dve.reciprocal(dst, both(use, rows, n // 2)).then_inc(inv_ready, 1)
                        dve.wait_ge(inv_ready, g + 1)
                        dve.sem_inc(freed[use % slots], 1)
                elif kind == "dense" and step[2] == KC - 1 and step[1] in "qb":
                    side = step[1]
                    dve.wait_ge(dense_ready[side], 1)
                    split(dve, chain, side, split_ready[side])
                    dve.wait_ge(split_ready[side], 1)


def out_projection(nc, env, label, o, n, wo, res, dst, bo="zero", factor=None, wide=False):
    ps, vec = env["ps"], env["vec"]
    parts = NH if wide else 4
    rows = HD2 if wide else P
    pieces = [(0, n // 2), (n // 2, n)]
    with stage(nc, label) as (block, sb, sem):
        projected, step = sem("projected"), sem("step")
        scaled = sb("scaled", [P, 2, n // 2], F32)
        loaded = sem("loaded")
        if wide:
            w = sb("w", [HD2, NH, D], F32)
        else:
            w = wo

        @block.sync
        def _(sp):
            if wide:
                sp.dma_start(w[:, :, :], wo.rearrange("(h d) n -> d h n", d=HD2)).then_inc(loaded, 16)
                sp.wait_ge(loaded, 16)

        @block.tensor
        def _(pe):
            if wide:
                pe.wait_ge(loaded, 16)
            for mc in range(KC):
                for i, (a, b) in enumerate(pieces):
                    for k in range(parts):
                        mm = pe.matmul(ps[:, 2 * mc + i, 0:b - a], w[0:rows, k, mc * P:mc * P + P],
                                       o[0:rows, k, a:b], start=(k == 0), stop=(k == parts - 1))
                mm.then_inc(projected, 1)

        @block.vector
        def _(dve):
            chain = Chain(dve, step)
            for mc in range(KC):
                dve.wait_ge(projected, mc + 1)
                src = ps[:, 2 * mc:2 * mc + 2, 0:n // 2]
                r = res[:, mc, 0:n].rearrange("p (i w) -> p i w", i=2)
                d = dst[:, mc, 0:n].rearrange("p (i w) -> p i w", i=2)
                if factor is None:
                    chain(dve.scalar_tensor_tensor(out=d, in0=src, scalar=vec(bo, mc), in1=r, op0=ALU.add, op1=ALU.add))
                else:
                    chain(dve.tensor_scalar(scaled[:, :, :], src, vec(bo, mc), factor, ALU.add, ALU.mult))
                    chain(dve.tensor_tensor(d, r, scaled[:, :, :], ALU.add))


def hash_ffn(nc, env, label, x, h, w):
    ps, vec = env["ps"], env["vec"]
    fc, n = 4, T
    half, per = n // 2, n // E
    slots = 4
    pieces = [(0, half), (half, n)]
    steps = [(k, f) for f in range(fc) for k in "ab"] + [("c", mc) for mc in range(KC)]
    for e in range(E):
        steps.append(("u", e))
        if e:
            steps.append(("d", e - 1))
    steps.append(("d", E - 1))

    def mine(t, c, e):
        lo, hi = sorted((3 * e % E, (3 * e + 3) % E))
        return t[:, c, :].rearrange("p (j r) -> p r j", r=E)[:, lo:hi + 1:hi - lo, :]

    with stage(nc, label) as (block, sb, sem):
        w1 = sb("w1", [P, E, KC, D], F32)
        w2 = sb("w2", [P, E, KC, D], F32)
        gated = sb("gated", [P, fc, n], F32)
        silu = sb("silu", [P, fc, n], F32)
        hidden = sb("hidden", [P, 2, KC, 2 * per], F32)
        tmp = sb("tmp", [P, n], F32)
        filled = [sem(f"filled{i}") for i in range(slots)]
        freed = [sem(f"freed{i}") for i in range(slots)]
        w1_loaded = [sem(f"w1_loaded{e}") for e in range(E)]
        w2_loaded = [sem(f"w2_loaded{e}") for e in range(E)]
        silu_ready, gated_ready, hidden_ready, step = map(sem, ("silu_ready", "gated_ready", "hidden_ready", "step"))

        @block.sync
        def _(sp):
            for e in range(E):
                sp.dma_start(w1[:, e, :, :], w["f0_w1"][e].rearrange("(c p) n -> p c n", p=P)).then_inc(w1_loaded[e], 16)
                sp.dma_start(w2[:, e, :, :], w["f0_w2"][e].rearrange("(c p) n -> p c n", p=P)).then_inc(w2_loaded[e], 16)

        @block.tensor
        def _(pe):
            for use, (kind, k) in enumerate(steps):
                s = use % slots
                if use >= slots:
                    pe.wait_ge(freed[s], use // slots)
                if kind in "ab":
                    m = w["f0_sw1"] if kind == "a" else w["f0_sw3"]
                    for i, (a, b) in enumerate(pieces):
                        for c in range(KC):
                            mm = pe.matmul(ps[:, 2 * s + i, 0:half], m[:, c, k * P:k * P + P], x[:, c, a:b],
                                           start=(c == 0), stop=(c == KC - 1))
                elif kind == "c":
                    pe.wait_ge(gated_ready, fc)
                    for i, (a, b) in enumerate(pieces):
                        for f in range(fc):
                            mm = pe.matmul(ps[:, 2 * s + i, 0:half], w["f0_sw2"][:, f, k * P:k * P + P],
                                           gated[:, f, a:b], start=(f == 0), stop=(f == fc - 1))
                elif kind == "u":
                    pe.wait_ge(w1_loaded[k], 16)
                    for f in range(KC):
                        for c in range(KC):
                            mm = pe.matmul(ps[:, 2 * s + f, 0:2 * per].rearrange("p (r j) -> p r j", r=2),
                                           w1[:, k, c, f * P:f * P + P], mine(x, c, k),
                                           start=(c == 0), stop=(c == KC - 1))
                else:
                    pe.wait_ge(w2_loaded[k], 16)
                    pe.wait_ge(hidden_ready, k + 1)
                    for mc in range(KC):
                        for f in range(KC):
                            mm = pe.matmul(ps[:, 2 * s + mc, 0:2 * per], w2[:, k, f, mc * P:mc * P + P],
                                           hidden[:, k % 2, f, :], start=(f == 0), stop=(f == KC - 1))
                mm.then_inc(filled[s], 1)

        @block.scalar
        def _(act):
            for use, (kind, k) in enumerate(steps):
                s = use % slots
                if kind == "a":
                    act.wait_ge(filled[s], use // slots + 1)
                    act.activation(silu[:, k, :].rearrange("p (i w) -> p i w", i=2), ps[:, 2 * s:2 * s + 2, 0:half],
                                   ACT.Silu, bias=vec("f0_sb1", k)).then_inc(silu_ready, 1)
                    act.wait_ge(silu_ready, k + 1)
                    act.sem_inc(freed[s], 1)
                elif kind == "u":
                    act.wait_ge(filled[s], use // slots + 1)
                    if k >= 2:
                        u2 = steps.index(("d", k - 2))
                        act.wait_ge(filled[u2 % slots], u2 // slots + 1)
                    for f in range(KC):
                        a = act.activation(hidden[:, k % 2, f, :], ps[:, 2 * s + f, 0:2 * per], ACT.Gelu,
                                           bias=vec("f0_b1", 2 * k + f))
                    a.then_inc(hidden_ready, 1)
                    act.wait_ge(hidden_ready, k + 1)
                    act.sem_inc(freed[s], 1)

        @block.vector
        def _(dve):
            chain = Chain(dve, step)
            for use, (kind, k) in enumerate(steps):
                s = use % slots
                src = ps[:, 2 * s:2 * s + 2, 0:half]
                if kind == "b":
                    dve.wait_ge(filled[s], use // slots + 1)
                    dve.wait_ge(silu_ready, k + 1)
                    dve.scalar_tensor_tensor(out=gated[:, k, :].rearrange("p (i w) -> p i w", i=2), in0=src,
                                             scalar=vec("f0_sb3", k),
                                             in1=silu[:, k, :].rearrange("p (i w) -> p i w", i=2),
                                             op0=ALU.add, op1=ALU.mult).then_inc(gated_ready, 1)
                    dve.wait_ge(gated_ready, k + 1)
                    dve.sem_inc(freed[s], 1)
                elif kind == "c":
                    dve.wait_ge(filled[s], use // slots + 1)
                    chain(dve.tensor_scalar(tmp[:, :].rearrange("p (i w) -> p i w", i=2), src, vec("f0_sb2", k), 0.5,
                                            ALU.add, ALU.mult))
                    dve.sem_inc(freed[s], 1)
                    chain(dve.tensor_tensor(h[:, k, :], h[:, k, :], tmp[:, :], ALU.add))
                elif kind == "d":
                    dve.wait_ge(filled[s], use // slots + 1)
                    for mc in range(KC):
                        t3 = tmp[:, 0:2 * per].rearrange("p (r j) -> p r j", r=2)
                        chain(dve.tensor_scalar(tmp[:, 0:2 * per], ps[:, 2 * s + mc, 0:2 * per],
                                                vec("f0_b2", 2 * k + mc), 0.25, ALU.add, ALU.mult))
                        chain(dve.tensor_tensor(mine(h, mc, k), mine(h, mc, k), t3, ALU.add))
                    dve.sem_inc(freed[s], 1)


def dense_layers(nc, env, label, layers):
    ps, vec = env["ps"], env["vec"]
    half = T // 2
    slots = 4
    steps = [(li, mc) for li, layer in enumerate(layers) for mc in range(layer[4])]
    with stage(nc, label) as (block, sb, sem):
        filled = [sem(f"filled{i}") for i in range(slots)]
        evacuated = sem("evacuated")

        @block.tensor
        def _(pe):
            for use, (li, mc) in enumerate(steps):
                src, rows, weight, m, _, _, _, _ = layers[li]
                s = use % slots
                if mc == 0 and use:
                    pe.wait_ge(evacuated, use)
                elif use >= slots:
                    pe.wait_ge(evacuated, use - slots + 1)
                kcs = src.shape[1]
                for i in range(2):
                    for k in range(kcs):
                        mm = pe.matmul(ps[0:m, 2 * s + i, 0:half], weight[0:rows, k, mc * P:mc * P + m],
                                       src[0:rows, k, i * half:(i + 1) * half], start=(k == 0), stop=(k == kcs - 1))
                mm.then_inc(filled[s], 1)

        @block.scalar
        def _(act):
            for use, (li, mc) in enumerate(steps):
                _, _, _, m, _, dst, func, b = layers[li]
                s = use % slots
                act.wait_ge(filled[s], use // slots + 1)
                act.activation(dst[0:m, mc, :].rearrange("p (i w) -> p i w", i=2), ps[0:m, 2 * s:2 * s + 2, 0:half],
                               func, bias=vec(b, mc)[0:m]).then_inc(evacuated, 1)


def moe(nc, env, label, x, xrows, route_x, route_rows, route_w, route_b, top, w1, w2, hidden_chunks, outw, func,
        b1=None, b2=None, dense_expert=False, gated=False, finish=None):
    ps, vec, c32, row = env["ps"], env["vec"], env["c"], env["row"]
    half = T // 2
    slots = 2
    toks = chunks(T)
    nt = len(toks)
    ne = E + (1 if dense_expert else 0)
    xk = x.shape[1]
    rk = route_x.shape[1]
    rw = E + (2 if dense_expert else 0)
    width = hidden_chunks * (2 if gated else 1) * P
    mcs = -(-outw // P)
    om = min(outw, P)
    steps = [("logit", 0, 0), ("turn", 0, 0)]
    for e in range(ne):
        steps.append(("spread", e, 0))
        for f in range(hidden_chunks):
            steps.append(("up", e, f))
            if gated:
                steps.append(("up2", e, f))
    hid_bufs = 4

    with stage(nc, label) as (block, sb, sem):
        logits = sb("logits", [P, nt, rw], F32)
        names = ("left", "chosen", "first", "key", "weight", "pick1")
        left, chosen, first, key, weight, pick1 = [sb(k, [P, nt, E], F32) for k in names]
        top1, top2, mk, total, inv = [sb(k, [P, nt, 1], F32) for k in ("top1", "top2", "mk", "total", "inv")]
        cmax, csum, cinv = [sb(k, [P, nt, 1], F32) for k in ("cmax", "csum", "cinv")]
        coef = sb("coef", [P, nt, 2], F32)
        comb = sb("comb", [P, nt, 9], F32)
        comb_t = sb("comb_t", [9, T], F32)
        spread = sb("spread", [P, 2, T], F32)
        w1b = sb("w1b", [P, 2, xk, width], F32)
        w2b = sb("w2b", [P, 2, hidden_chunks, outw], F32)
        hidden = sb("hidden", [P, hid_bufs, T], F32)
        gate_act = sb("gate_act", [P, hid_bufs, T], F32) if gated else None
        w_route = sb("w_route", [P, rk, rw], F32)
        b2_rows = sb("b2_rows", [9, outw], F32) if b2 is not None else None
        filled = [sem(f"filled{i}") for i in range(slots)]
        freed = [sem(f"freed{i}") for i in range(slots)]
        route_loaded, b2_loaded = sem("route_loaded"), sem("b2_loaded")
        w1_loaded = [sem(f"w1_loaded{i}") for i in range(2)]
        w2_loaded = [sem(f"w2_loaded{i}") for i in range(2)]
        chain_sem, logits_ready, exp_ready, diff_ready, comb_ready, comb_t_ready = map(
            sem, ("chain", "logits_ready", "exp_ready", "diff_ready", "comb_ready", "comb_t_ready"))
        cleared, spread_ready, act_ready, hidden_ready, expert_up, down_done, acc_ready, out_step = map(
            sem, ("cleared", "spread_ready", "act_ready", "hidden_ready", "expert_up", "down_done", "acc_ready",
                  "out_step"))
        acc = lambda mc, i: ps[0:om, 4 + 2 * mc + i, 0:half]

        @block.sync
        def _(sp):
            sp.dma_start(w_route[0:route_rows, :, :], route_w.rearrange("(c p) n -> p c n", p=route_rows))\
                .then_inc(route_loaded, 16)
            if b2 is not None:
                sp.dma_start(b2_rows[0:ne, :], b2).then_inc(b2_loaded, 16)
            for e in range(ne):
                if e >= 2:
                    sp.wait_ge(down_done, (e - 1) * hidden_chunks)
                sp.dma_start(w1b[0:xrows, e % 2, :, :], w1[e].rearrange("(c p) n -> p c n", p=xrows))\
                    .then_inc(w1_loaded[e % 2], 16)
                sp.dma_start(w2b[:, e % 2, :, :], w2[e].rearrange("(c p) n -> p c n", p=P))\
                    .then_inc(w2_loaded[e % 2], 16)

        @block.tensor
        def _(pe):
            def down(e, f):
                pe.wait_ge(hidden_ready, e * hidden_chunks + f + 1)
                if f == 0:
                    pe.wait_ge(w2_loaded[e % 2], 16 * (e // 2 + 1))
                no = e * hidden_chunks + f
                last = no == ne * hidden_chunks - 1 and b2 is None
                for mc in range(mcs):
                    for i in range(2):
                        mm = pe.matmul(acc(mc, i), w2b[:, e % 2, f, mc * P:mc * P + om],
                                       hidden[:, no % hid_bufs, i * half:(i + 1) * half], start=(no == 0), stop=last)
                mm.then_inc(down_done, 1)

            pending = []
            for use, (kind, e, f) in enumerate(steps):
                s = use % slots
                if use >= slots:
                    pe.wait_ge(freed[s], use // slots)
                if kind == "logit":
                    pe.wait_ge(route_loaded, 16)
                    for t, (a, rows) in enumerate(toks):
                        for k in range(rk):
                            mm = pe.matmul(ps[0:rows, 2 * s, 16 * t:16 * t + rw], route_x[0:route_rows, k, a:a + rows],
                                           w_route[0:route_rows, k, :], start=(k == 0), stop=(k == rk - 1),
                                           skip_group_check=True)
                elif kind == "turn":
                    pe.wait_ge(comb_ready, 1)
                    for t, (a, rows) in enumerate(toks):
                        i = a // BANK
                        mm = pe.transpose(ps[0:9, 2 * s + i, a - i * BANK:a - i * BANK + rows], comb[0:rows, t, :],
                                          c32("ident")[0:rows, 0:rows])
                elif kind == "spread":
                    if e == 0:
                        pe.wait_ge(comb_t_ready, 2)
                    for i in range(2):
                        mm = pe.matmul(ps[:, 2 * s + i, 0:half], c32("pick")[0:9, e * P:e * P + P],
                                       comb_t[:, i * half:(i + 1) * half], start=True, stop=True)
                else:
                    if f == 0 and kind == "up":
                        pe.wait_ge(w1_loaded[e % 2], 16 * (e // 2 + 1))
                    off = (hidden_chunks * P if kind == "up2" else 0) + f * P
                    for i in range(2):
                        for k in range(xk):
                            mm = pe.matmul(ps[:, 2 * s + i, 0:half], w1b[0:xrows, e % 2, k, off:off + P],
                                           x[0:xrows, k, i * half:(i + 1) * half], start=(k == 0), stop=(k == xk - 1))
                mm.then_inc(filled[s], 1)
                if kind == ("up2" if gated else "up"):
                    pending.append((e, f))
                    if len(pending) > 1:
                        down(*pending.pop(0))
            down(*pending.pop(0))
            if b2 is not None:
                pe.wait_ge(b2_loaded, 16)
                for mc in range(mcs):
                    for i in range(2):
                        mm = pe.matmul(acc(mc, i), b2_rows[0:ne, mc * P:mc * P + om],
                                       comb_t[0:ne, i * half:(i + 1) * half], start=False, stop=True)
                mm.then_inc(acc_ready, 1)
            else:
                pe.wait_ge(down_done, ne * hidden_chunks)
                pe.sem_inc(acc_ready, 1)

        @block.scalar
        def _(act):
            act.wait_ge(diff_ready, 1)
            a = act.activation(weight[:, :, :], left[:, :, :], ACT.Exp)
            if dense_expert:
                a = act.activation(coef[:, :, :], coef[:, :, :], ACT.Exp)
            a.then_inc(exp_ready, 1)
            for use, (kind, e, f) in enumerate(steps):
                s = use % slots
                no = e * hidden_chunks + f
                src = ps[:, 2 * s:2 * s + 2, 0:half]
                if kind == "turn":
                    act.wait_ge(filled[s], use // slots + 1)
                    act.activation(comb_t[:, 0:BANK], ps[0:9, 2 * s, :], ACT.Copy).then_inc(comb_t_ready, 1)
                    act.activation(comb_t[:, BANK:T], ps[0:9, 2 * s + 1, 0:T - BANK], ACT.Copy).then_inc(comb_t_ready, 1)
                    act.wait_ge(comb_t_ready, 2)
                    act.sem_inc(freed[s], 1)
                elif kind == "spread":
                    act.wait_ge(filled[s], use // slots + 1)
                    if e >= 2:
                        act.wait_ge(hidden_ready, (e - 1) * hidden_chunks)
                    act.activation(spread[:, e % 2, :].rearrange("p (i w) -> p i w", i=2), src, ACT.Copy)\
                        .then_inc(spread_ready, 1)
                    act.wait_ge(spread_ready, e + 1)
                    act.sem_inc(freed[s], 1)
                elif kind == "up":
                    act.wait_ge(filled[s], use // slots + 1)
                    if no >= hid_bufs:
                        act.wait_ge(down_done, no - hid_bufs + 1)
                    dst = (gate_act if gated else hidden)[:, no % hid_bufs, :]
                    args = {} if b1 is None else {"bias": vec(b1, no)}
                    act.activation(dst.rearrange("p (i w) -> p i w", i=2), src, func, **args).then_inc(act_ready, 1)
                    act.wait_ge(act_ready, no + 1)
                    act.sem_inc(freed[s], 1)

        @block.vector
        def _(dve):
            chain = Chain(dve, chain_sem)

            def over_experts(t):
                return t[:, :, 0:1].to_broadcast([P, nt, E])

            chain(dve.memset(logits[:, :, :], 0.0))
            chain(dve.memset(comb[:, :, :], 0.0))
            dve.wait_ge(filled[0], 1)
            for t, (a, rows) in enumerate(toks):
                chain(dve.tensor_copy(logits[0:rows, t, :], ps[0:rows, 0, 16 * t:16 * t + rw]))
            dve.sem_inc(freed[0], 1)
            if route_b:
                bias_row = row(route_b)
                nb = 2 if dense_expert else E
                off = E if dense_expert else 0
                for t in range(nt):
                    chain(dve.tensor_tensor(logits[:, t, off:off + nb], logits[:, t, off:off + nb], bias_row, ALU.add))
            lg = logits[:, :, 0:E]
            chain(dve.tensor_reduce(top1[:, :, :], lg, op=ALU.max, axis=AX.X))
            chain(dve.tensor_tensor(left[:, :, :], lg, over_experts(top1), ALU.subtract))
            if dense_expert:
                lc = logits[:, :, E:E + 2]
                chain(dve.tensor_reduce(cmax[:, :, :], lc, op=ALU.max, axis=AX.X))
                chain(dve.tensor_tensor(coef[:, :, :], lc, cmax[:, :, 0:1].to_broadcast([P, nt, 2]), ALU.subtract))
            dve.sem_inc(diff_ready, 1)

            def pick_first(dst, of, best):
                chain(dve.tensor_tensor(key[:, :, :], of, over_experts(best), ALU.is_equal))
                for t in range(nt):
                    chain(dve.tensor_tensor(key[:, t, :], key[:, t, :], row("falling"), ALU.mult))
                chain(dve.tensor_reduce(mk[:, :, :], key[:, :, :], op=ALU.max, axis=AX.X))
                chain(dve.tensor_tensor(dst, key[:, :, :], over_experts(mk), ALU.is_equal))

            pick_first(pick1[:, :, :], lg, top1)
            if top == 2:
                chain(dve.scalar_tensor_tensor(out=chosen[:, :, :], in0=pick1[:, :, :], scalar=-1e30, in1=lg,
                                               op0=ALU.mult, op1=ALU.add))
                chain(dve.tensor_reduce(top2[:, :, :], chosen[:, :, :], op=ALU.max, axis=AX.X))
                pick_first(first[:, :, :], chosen[:, :, :], top2)
                chain(dve.tensor_tensor(pick1[:, :, :], pick1[:, :, :], first[:, :, :], ALU.add))
            dve.wait_ge(exp_ready, 1)
            if top == 2:
                chain(dve.tensor_tensor(weight[:, :, :], weight[:, :, :], pick1[:, :, :], ALU.mult))
                chain(dve.tensor_reduce(total[:, :, :], weight[:, :, :], op=ALU.add, axis=AX.X))
                chain(dve.reciprocal(inv[:, :, :], total[:, :, :]))
                chain(dve.tensor_tensor(comb[:, :, 0:E], weight[:, :, :], over_experts(inv), ALU.mult))
            else:
                chain(dve.tensor_reduce(total[:, :, :], weight[:, :, :], op=ALU.add, axis=AX.X))
                chain(dve.reciprocal(inv[:, :, :], total[:, :, :]))
                chain(dve.tensor_reduce(csum[:, :, :], coef[:, :, :], op=ALU.add, axis=AX.X))
                chain(dve.reciprocal(cinv[:, :, :], csum[:, :, :]))
                chain(dve.tensor_tensor(coef[:, :, :], coef[:, :, :], cinv[:, :, 0:1].to_broadcast([P, nt, 2]), ALU.mult))
                chain(dve.tensor_tensor(inv[:, :, :], inv[:, :, :], coef[:, :, 0:1], ALU.mult))
                chain(dve.tensor_tensor(comb[:, :, 0:E], pick1[:, :, :], over_experts(inv), ALU.mult))
                chain(dve.tensor_copy(comb[:, :, E:E + 1], coef[:, :, 1:2]))
            dve.sem_inc(comb_ready, 1)
            for use, (kind, e, f) in enumerate(steps):
                s = use % slots
                no = e * hidden_chunks + f
                if kind != ("up2" if gated else "up"):
                    continue
                if f == 0:
                    dve.wait_ge(spread_ready, e + 1)
                buf = hidden[:, no % hid_bufs, :]
                weights = spread[:, e % 2, :]
                dve.wait_ge(act_ready, no + 1)
                if gated:
                    g = gate_act[:, no % hid_bufs, :]
                    dve.wait_ge(filled[s], use // slots + 1)
                    if no >= hid_bufs:
                        dve.wait_ge(down_done, no - hid_bufs + 1)
                    chain(dve.tensor_tensor(buf.rearrange("p (i w) -> p i w", i=2), ps[:, 2 * s:2 * s + 2, 0:half],
                                            g.rearrange("p (i w) -> p i w", i=2), ALU.mult))
                    dve.sem_inc(freed[s], 1)
                dve.tensor_tensor(buf, buf, weights, ALU.mult).then_inc(hidden_ready, 1)
            dve.wait_ge(acc_ready, 1)
            for mc in range(mcs):
                src = ps[0:om, 4 + 2 * mc:6 + 2 * mc, 0:half]
                finish(dve, chain, mc, src)


def build(nc, a):
    vec_at, vec_n = columns(VECTORS)
    row_at, row_n = columns(ROWS)
    c_at, c_n = columns(CONSTS)
    c16_at, c16_n = columns(CONSTS16)
    with ExitStack() as scope:
        def sb(name, shape, dt=F32):
            return scope.enter_context(nc.sbuf_tensor(name, shape, dt))

        ps = scope.enter_context(nc.psum_tensor("banks", [P, 8, BANK], F32))
        vectors, rows = sb("vectors", [P, vec_n]), sb("rows", [P, row_n])
        consts, consts16 = sb("consts", [P, c_n]), sb("consts16", [P, c16_n], BF16)
        h, xa, xb = sb("h", [P, KC, T]), sb("xa", [P, KC, T]), sb("xb", [P, KC, T])
        ab = sb("alpha_beta_sb", [24, D])
        resident = {k: sb(f"{k}_sb", list(a[k].shape)) for k in
                    ("tok_qkv", "tok_o", "a0_qkv", "a0_o", "a1_qkv", "a1_o", "a2_qkv", "a2_o", "a3_qkv", "a3_o")}

        def vec(name, k=0):
            return vectors[:, vec_at[name][0] + k:vec_at[name][0] + k + 1]

        def row(name):
            return rows[:, row_at[name][0]:row_at[name][0] + row_at[name][1]]

        def c(name):
            return consts[:, c_at[name][0]:c_at[name][0] + c_at[name][1]]

        def c16(name):
            return consts16[:, c16_at[name][0]:c16_at[name][0] + c16_at[name][1]]

        def pick_parts(side, j, head):
            k = (((0 if side == "k" else 1) * 3 + j) * 8 + head) * PART_ROWS
            return c16("stack")[:, k:k + PART_ROWS]

        env = {"ps": ps, "vec": vec, "row": row, "c": c, "c16": c16, "pick_parts": pick_parts, "alpha_beta": ab}

        with stage(nc, "load") as (block, _, sem):
            loads = [(vectors[:, :], a["vectors"]), (rows[:, :], a["rows"]), (consts[:, :], a["consts"]),
                     (consts16[:, :], a["consts16"]), (ab[:, :], a["alpha_beta"])]
            loads += [(t[:, :, :], a[k]) for k, t in resident.items()]
            loaded = sem("loaded")

            @block.sync
            def _(sp):
                for dst, src in loads:
                    sp.dma_start(dst, src).then_inc(loaded, 16)
                sp.wait_ge(loaded, 16 * len(loads))

        with nc.Fori(0, B) as b:
            with stage(nc, "input") as (block, _, sem):
                loaded = sem("loaded")

                @block.sync
                def _(sp):
                    sp.dma_start(h[:, :, 0:S_IMG], a["x"][b]).then_inc(loaded, 16)
                    sp.dma_start(h[:, :, S_IMG:T], a["txt"][b]).then_inc(loaded, 16)
                    sp.wait_ge(loaded, 32)

            def small_attention(label, x, n, res, dst, bo="zero", factor=None, gamma=None, **kw):
                o = scope2.enter_context(nc.sbuf_tensor(f"{label}_o", [P, 4, n], F32))
                attention(nc, env, label, x, n, resident[f"{label}_qkv"], o, **kw)
                out_projection(nc, env, f"{label}_out", o, n, resident[f"{label}_o"], res, dst, bo=bo, factor=factor)

            with ExitStack() as scope2:
                small_attention("tok", h, S_IMG, h, h, bo="tok_bo", bq="tok_bq", bk="tok_bk", bv="tok_bv",
                                exp_scale=HD ** -0.5)
            layer_norm(nc, env, "ln_tok", h, h, S_IMG, "eps5", "tok_g", "tok_b")

            layer_norm(nc, env, "ln_a0", h, xa, T, "eps5")
            with ExitStack() as scope2:
                small_attention("a0", xa, T, h, h, causal=True, bias=True, q_scale=HD ** -0.5)
            layer_norm(nc, env, "ln_f0", h, xa, T, "eps5")
            with ExitStack() as scope2:
                f0 = {k: scope2.enter_context(nc.sbuf_tensor(f"{k}_sb", list(a[k].shape), F32))
                      for k in ("f0_sw1", "f0_sw3", "f0_sw2")}
                load_weights(nc, "f0_load", [(t, a[k]) for k, t in f0.items()])
                hash_ffn(nc, env, "f0", xa, h, {**f0, "f0_w1": a["f0_w1"], "f0_w2": a["f0_w2"]})

            layer_norm(nc, env, "ln_a1", h, xa, T, "eps5")
            with ExitStack() as scope2:
                small_attention("a1", xa, T, h, h, causal=True, poly=True, q_scale=HD ** -0.5)
            layer_norm(nc, env, "ln_f1", h, xa, T, "eps5")
            with ExitStack() as scope2:
                def sb2(name, shape):
                    return scope2.enter_context(nc.sbuf_tensor(name, shape, F32))
                f1 = {k: sb2(f"{k}_sb", list(a[k].shape)) for k in
                      ("f1_enc_w", "f1_s2c_w", "f1_r_w1", "f1_c2s_w", "f1_dec_w")}
                spikes = sb2("spikes", [P, 4, T])
                cont, rh, moe_out = sb2("cont", [64, 1, T]), sb2("rh", [64, 1, T]), sb2("moe_out", [64, 1, T])
                load_weights(nc, "f1_load", [(t, a[k]) for k, t in f1.items()])
                dense_layers(nc, env, "f1_in", [
                    (xa, P, f1["f1_enc_w"], P, 4, spikes, ACT.Sigmoid, "f1_enc"),
                    (spikes, P, f1["f1_s2c_w"], 64, 1, cont, ACT.Identity, "f1_s2c"),
                    (cont, 64, f1["f1_r_w1"], 64, 1, rh, ACT.Relu, "f1_rb1")])

                def keep(dve, chain, mc, src):
                    chain(dve.tensor_copy(moe_out[:, 0, :].rearrange("p (i w) -> p i w", i=2), src))

                moe(nc, env, "m1", cont, 64, rh, 64, a["f1_r_w2"], "f1_rb2", 2, a["f1_e_w1"], a["f1_e_w2"], 2, 64,
                    ACT.Relu, b1="f1_eb1", b2=a["f1_e_b2"], finish=keep)
                dense_layers(nc, env, "f1_out", [
                    (moe_out, 64, f1["f1_c2s_w"], P, 4, spikes, ACT.Sigmoid, "f1_c2s"),
                    (spikes, P, f1["f1_dec_w"], P, 2, xa, ACT.Sigmoid, "f1_dec")])
            layer_norm(nc, env, "ln_f1_out", xa, xb, T, "eps5", "f1_g", "f1_b", add_to=h)

            layer_norm(nc, env, "ln_w2", h, xa, T, "eps5")
            with ExitStack() as scope2:
                o = scope2.enter_context(nc.sbuf_tensor("w2_o", [HD2, NH, T], F32))
                with ExitStack() as scope3:
                    w = scope3.enter_context(nc.sbuf_tensor("w2_qkv_sb", list(a["w2_qkv"].shape), F32))
                    load_weights(nc, "w2_load", [(w, a["w2_qkv"])])
                    attention(nc, env, "w2", xa, T, w, o, causal=True, wide=True, exp_scale=HD2 ** -0.5)
                out_projection(nc, env, "w2_out", o, T, a["w2_r"], h, h, wide=True)

            layer_norm(nc, env, "ln_a2x", h, xa, T, "eps5")
            layer_norm(nc, env, "ln_a2", xa, xb, T, "eps5", "a2_g1", "a2_b1")
            with ExitStack() as scope2:
                small_attention("a2", xb, T, xa, xa, bo="a2_bo", bq="a2_bq", bk="a2_bk", bv="a2_bv",
                                exp_scale=HD ** -0.5)
            layer_norm(nc, env, "ln_f2", xa, xb, T, "eps5", "a2_g2", "a2_b2")

            def add_both(dve, chain, mc, src):
                d = h[:, mc, :]
                chain(dve.tensor_tensor(d, d, xa[:, mc, :], ALU.add))
                d = d.rearrange("p (i w) -> p i w", i=2)
                chain(dve.tensor_tensor(d, d, src, ALU.add))

            moe(nc, env, "m2", xb, P, xb, P, a["f2_route"], "f2_coefb", 1, a["f2_w1"], a["f2_w2"], 8, D, ACT.Gelu,
                b1="f2_b1", b2=a["f2_b2"], dense_expert=True, finish=add_both)

            layer_norm(nc, env, "ln_a3x", h, xa, T, "eps5")
            layer_norm(nc, env, "ln_a3", xa, xb, T, "eps6", "a3_g", "a3_b")
            with ExitStack() as scope2:
                small_attention("a3", xb, T, h, h, bo="a3_bo", factor=0.1, causal=True, bq="a3_bq", bk="a3_bk",
                                bv="a3_bv", gate="a3_ent", exp_scale=HD ** -0.5 / 0.1)
            layer_norm(nc, env, "ln_f3", h, xa, T, "eps5")

            def add_one(dve, chain, mc, src):
                d = h[:, mc, :].rearrange("p (i w) -> p i w", i=2)
                chain(dve.tensor_tensor(d, d, src, ALU.add))

            moe(nc, env, "m3", xa, P, xa, P, a["f3_route"], None, 2, a["f3_w1"], a["f3_w2"], 4, D, ACT.Silu,
                gated=True, finish=add_one)

            with stage(nc, "output") as (block, _, sem):
                stored = sem("stored")

                @block.sync
                def _(sp):
                    sp.dma_start(a["out"][b], h[:, :, :]).then_inc(stored, 16)
                    sp.wait_ge(stored, 16)


def load_weights(nc, label, pairs):
    with stage(nc, label) as (block, _, sem):
        loaded = sem("loaded")

        @block.sync
        def _(sp):
            for dst, src in pairs:
                sp.dma_start(dst[:, :, :], src).then_inc(loaded, 16)
            sp.wait_ge(loaded, 16 * len(pairs))


def kernel(**inputs):
    import ml_dtypes
    import numpy as np
    import concourse.bacc as bacc
    from concourse.bass_utils import run_bass_kernel_spmd

    i = {k: np.asarray(v) for k, v in inputs.items()}
    f32 = np.float32

    def halves(w, p=P):
        return np.ascontiguousarray(w.reshape(-1, p, w.shape[-1]).transpose(1, 0, 2))

    def by_partition(v, p=P):
        v = v.reshape(-1, p).T
        return np.concatenate([v, np.zeros((P - p, v.shape[1]), f32)]) if p < P else v

    def head_rows(w):
        out = np.zeros((4, VW, 4, w.shape[-1]), f32)
        out[:, :HD] = w.reshape(4, 4, HD, -1).transpose(1, 2, 0, 3)
        return out.reshape(P, 4, -1)

    tok_w = i["L0_tok_W_qkv"].reshape(D, NH, 3, HD).transpose(0, 2, 1, 3).reshape(D, 3 * D)
    tok_b = i["L0_tok_b_qkv"].reshape(NH, 3, HD).transpose(1, 0, 2).reshape(3, D)
    a2_b = i["L2_ffn_bqkv"].reshape(3, D)
    a3_b = i["L3_attn_b_qkv"].reshape(3, D)
    vectors = {
        "zero": np.zeros((P, 4), f32), "eps5": np.full((P, 1), 1e-5, f32), "eps6": np.full((P, 1), 1e-6, f32),
        "root_half": np.full((P, 1), 0.5 ** 0.5, f32),
        "tok_bq": by_partition(tok_b[0]), "tok_bk": by_partition(tok_b[1]), "tok_bo": by_partition(i["L0_tok_b_out"]),
        "tok_g": by_partition(i["L0_tok_ln_gamma"]), "tok_b": by_partition(i["L0_tok_ln_beta"]),
        "f0_sb1": by_partition(i["L0_ffn_sb1"]), "f0_sb3": by_partition(i["L0_ffn_sb3"]),
        "f0_sb2": by_partition(i["L0_ffn_sb2"]), "f0_b1": by_partition(i["L0_ffn_b1"]),
        "f0_b2": by_partition(i["L0_ffn_b2"]),
        "f1_enc": by_partition(i["L1_ffn_enc_b"]), "f1_s2c": by_partition(i["L1_ffn_s2c_b"], 64),
        "f1_rb1": by_partition(i["L1_ffn_r_b1"], 64), "f1_eb1": by_partition(i["L1_ffn_e_b1"]),
        "f1_c2s": by_partition(i["L1_ffn_c2s_b"]), "f1_dec": by_partition(i["L1_ffn_dec_b"]),
        "f1_g": by_partition(i["L1_ffn_ln_g"]), "f1_b": by_partition(i["L1_ffn_ln_b"]),
        "a2_g1": by_partition(i["L2_ffn_ln1_g"]), "a2_b1": by_partition(i["L2_ffn_ln1_b"]),
        "a2_bq": by_partition(a2_b[0]), "a2_bk": by_partition(a2_b[1]), "a2_bo": by_partition(i["L2_ffn_bo"]),
        "a2_g2": by_partition(i["L2_ffn_ln2_g"]), "a2_b2": by_partition(i["L2_ffn_ln2_b"]),
        "f2_b1": np.concatenate([by_partition(i["L2_ffn_b1"]), by_partition(i["L2_ffn_rb1"])], 1),
        "a3_g": by_partition(i["L3_attn_ln_g"]), "a3_b": by_partition(i["L3_attn_ln_b"]),
        "a3_bq": by_partition(a3_b[0]), "a3_bk": by_partition(a3_b[1]), "a3_bo": by_partition(i["L3_attn_b_out"]),
    }
    rows = {"tok_bv": tok_b[2], "a2_bv": a2_b[2], "a3_bv": a3_b[2], "f1_rb2": i["L1_ffn_r_b2"],
            "f2_coefb": i["L2_ffn_coef_b"], "a3_ent": i["L3_attn_b_ent"], "falling": np.arange(E, 0, -1, dtype=f32)}

    eye = np.eye(P, dtype=f32)
    sum_rows, sum_rows2 = np.zeros((P, P), f32), np.zeros((P, HD2), f32)
    for g in range(4):
        sum_rows[VW * g + HD, VW * g:VW * g + VW] = 1
    sum_rows2[HD2] = 1
    pick = np.zeros((P, 9, P), f32)
    for e in range(9):
        pick[e, e] = 1
    omega = (f32(10000.0) ** (f32(-2.0) * np.arange(HD // 2, dtype=f32) / f32(HD))).astype(np.float64)
    angle = omega[:, None] * np.arange(T)[None]
    cos, sin = np.cos(angle).astype(f32), np.sin(angle).astype(f32)
    trig = np.zeros((P, T), f32)
    trig[0:8], trig[8:16], trig[16:24] = cos, sin, -cos
    fix_k, fix_q = np.zeros((P, T), f32), np.zeros((P, T), f32)
    for t in range(1, 5):
        fix_k[HD2 + t - 1, P * t:P * t + P] = 1
        fix_q[HD2 + t - 1, :P * t] = -50.0 * 8
    consts = {"mean": np.full((P, P), 1 / D, f32), "ident": eye, "sum_rows": sum_rows, "sum_rows2": sum_rows2,
              "pick": pick.reshape(P, -1), "trig": trig, "fix_k": fix_k, "fix_q": fix_q}
    bf = ml_dtypes.bfloat16
    above = np.triu(np.ones((P, P), f32), 1)
    stack = np.zeros((P, 2, 3, 8, PART_ROWS), f32)
    for side, order in enumerate((K_PARTS, Q_PARTS)):
        for j, part in enumerate(order):
            for head in range(8):
                for d in range(HD):
                    stack[head * HD + d, side, part, head, j * HD + d] = 1
    keys = np.concatenate([cos, sin])
    key_parts, left = [], keys
    for _ in range(3):
        key_parts.append(left.astype(bf))
        left = left - key_parts[-1].astype(f32)
    trig_k = np.zeros((P, T), bf)
    for j, part in enumerate(K_PARTS):
        trig_k[j * HD:(j + 1) * HD] = key_parts[part]
    consts16 = {"ident": eye.astype(bf), "hard_q": (above * f32(-1e30)).astype(bf),
                "hard_k": (above.T * f32(-1e30)).astype(bf), "soft_q": (above * f32(-400)).astype(bf),
                "soft_k": (above.T * f32(-400)).astype(bf), "stack": stack.reshape(P, -1).astype(bf),
                "trig_k": trig_k}

    al, be = i["L0_attn_alpha"], i["L0_attn_beta"]
    ab = np.zeros((3, 8, NH, 2, 8), f32)
    for r in range(8):
        ab[0, r, :, 0, r] = al[:, r]
        ab[1, r, :, 0, r] = be[:, r]
        ab[1, r, :, 1, r] = al[:, r]
        ab[2, r, :, 1, r] = be[:, r]

    arrays = {
        "x": np.ascontiguousarray(i["x"].reshape(B, S_IMG, KC, P).transpose(0, 3, 2, 1)),
        "txt": np.ascontiguousarray(i["txt"].reshape(B, S_TXT, KC, P).transpose(0, 3, 2, 1)),
        "vectors": np.concatenate([vectors[k] for k, _ in VECTORS], 1),
        "rows": np.ascontiguousarray(np.broadcast_to(np.concatenate([rows[k] for k, _ in ROWS])[None],
                                                     (P, columns(ROWS)[1]))),
        "consts": np.concatenate([consts[k] for k, _ in CONSTS], 1),
        "consts16": np.concatenate([consts16[k] for k, _ in CONSTS16], 1),
        "alpha_beta": ab.reshape(24, D),
        "tok_qkv": halves(tok_w), "tok_o": head_rows(i["L0_tok_W_out"]),
        "a0_qkv": halves(i["L0_attn_Wqkv"].T), "a0_o": head_rows(i["L0_attn_Wout"].T),
        "a1_qkv": halves(np.concatenate([i["L1_attn_Wq"].T, i["L1_attn_Wk"].T, i["L1_attn_Wv"].T], 1)),
        "a1_o": head_rows(i["L1_attn_Wo"].T),
        "a2_qkv": halves(i["L2_ffn_Wqkv"]), "a2_o": head_rows(i["L2_ffn_Wo"]),
        "a3_qkv": halves(np.concatenate([i["L3_attn_w_qkv"].T, i["L3_attn_w_ent"].T], 1)),
        "a3_o": head_rows(i["L3_attn_w_out"].T),
        "w2_qkv": halves(np.concatenate([i["L2_attn_Wq"], i["L2_attn_Wk"], i["L2_attn_Wv"]], 1)),
        "w2_r": i["L2_attn_Wr"],
        "f0_sw1": halves(i["L0_ffn_sw1"]), "f0_sw3": halves(i["L0_ffn_sw3"]), "f0_sw2": halves(i["L0_ffn_sw2"]),
        "f0_w1": i["L0_ffn_w1"], "f0_w2": i["L0_ffn_w2"],
        "f1_enc_w": halves(i["L1_ffn_enc_w"]), "f1_s2c_w": halves(i["L1_ffn_s2c_w"]),
        "f1_r_w1": halves(i["L1_ffn_r_w1"], 64), "f1_r_w2": i["L1_ffn_r_w2"],
        "f1_e_w1": i["L1_ffn_e_w1"], "f1_e_w2": i["L1_ffn_e_w2"], "f1_e_b2": i["L1_ffn_e_b2"],
        "f1_c2s_w": halves(i["L1_ffn_c2s_w"], 64), "f1_dec_w": halves(i["L1_ffn_dec_w"]),
        "f2_route": np.concatenate([i["L2_ffn_gate_w"], i["L2_ffn_coef_w"]], 1),
        "f2_w1": np.concatenate([i["L2_ffn_W1"], i["L2_ffn_rW1"][None]]),
        "f2_w2": np.concatenate([i["L2_ffn_W2"], i["L2_ffn_rW2"][None]]),
        "f2_b2": np.concatenate([i["L2_ffn_b2"], i["L2_ffn_rb2"][None]]),
        "f3_route": i["L3_ffn_gate_w"].T, "f3_w1": i["L3_ffn_w12"].transpose(0, 2, 1),
        "f3_w2": i["L3_ffn_w3"].transpose(0, 2, 1),
    }
    nc = bacc.Bacc("TRN2", target_bir_lowering=False, num_devices=1)
    fed, aps = {}, {}
    for name, v in arrays.items():
        v = np.ascontiguousarray(v)
        fed[f"in_{name}"] = v
        aps[name] = nc.dram_tensor(f"in_{name}", v.shape, mybir.dt.from_np(v.dtype), kind="ExternalInput").ap()
    aps["out"] = nc.dram_tensor("out_0", (B, P, KC, T), F32, kind="ExternalOutput").ap()
    build(nc, aps)
    r = run_bass_kernel_spmd(nc, [fed], core_ids=[0])
    got = r.results[0]["out_0"]
    return np.ascontiguousarray(got.transpose(0, 3, 2, 1).reshape(B, T, D))
```

```python
import concourse.bass as bass
from concourse import mybir
from contextlib import ExitStack, contextmanager

F32 = mybir.dt.float32
BF16 = mybir.dt.bfloat16
F32R = mybir.dt.float32r
ALU = mybir.AluOpType
ACT = mybir.ActivationFunctionType
AX = mybir.AxisListType

P = 128
B = 4
S_IMG, S_TXT = 512, 32
T = S_IMG + S_TXT
D = 256
KC = D // P
NH = 16
HD = 16
HD2 = 64
E = 8
BANK = 512
VW = 32
PART_ROWS = 96
MAX_ROW = 96
K_PARTS = ((0, 0), (16, 0), (32, 1))
Q_PARTS = ((0, 0), (16, 1), (32, 0))
TRIG_PARTS = ((64, 0), (80, 0), (99, 1))
BIAS_PARTS = ((64, 0), (80, 1), (99, 0))

VECTORS = [
    ("zero", 4), ("eps5", 1), ("eps6", 1), ("root_half", 1),
    ("tok_bq", 2), ("tok_bk", 2), ("tok_bo", 2), ("tok_g", 2), ("tok_b", 2),
    ("f0_sb1", 4), ("f0_sb3", 4), ("f0_sb2", 2), ("f0_b1", 16), ("f0_b2", 16),
    ("f1_enc", 4), ("f1_s2c", 1), ("f1_rb1", 1), ("f1_eb1", 16), ("f1_c2s", 4), ("f1_dec", 2),
    ("f1_g", 2), ("f1_b", 2),
    ("a2_g1", 2), ("a2_b1", 2), ("a2_bq", 2), ("a2_bk", 2), ("a2_bo", 2), ("a2_g2", 2), ("a2_b2", 2),
    ("f2_b1", 72),
    ("a3_g", 2), ("a3_b", 2), ("a3_bq", 2), ("a3_bk", 2), ("a3_bo", 2),
]
ROWS = [("tok_bv", D), ("a2_bv", D), ("a3_bv", D), ("f1_rb2", E), ("f2_coefb", 2), ("a3_ent", 1), ("falling", E)]
CONSTS = [("mean", P), ("ident", P), ("sum_rows", P), ("pick", 9 * P), ("trig", T), ("trig_k", T),
          ("fix_k", T), ("fix_q", T)]
STACKS = {"k": (K_PARTS, PART_ROWS), "q": (Q_PARTS, P), "b": (BIAS_PARTS, P)}
CONSTS16 = [("ident", P), ("hard_q", P), ("hard_k", P), ("soft_q", P), ("soft_k", P)]


def columns(table):
    at, out = 0, {}
    for name, n in table:
        out[name] = (at, n)
        at += n
    return out, at


def chunks(n):
    return [(a, min(P, n - a)) for a in range(0, n, P)]


def windows(n):
    out = [(a, 0) for a in range(0, n - P + 1, P)]
    return out + ([(n - P, P - n % P)] if n % P else [])


@contextmanager
def stage(nc, label):
    numbers = []
    with ExitStack() as scope:
        def sb(name, shape, dt):
            return scope.enter_context(nc.sbuf_tensor(f"{label}_{name}", shape, dt))

        def sem(name):
            s = scope.enter_context(nc.semaphore(f"{label}_{name}"))
            numbers.append(s.num)
            return s

        with nc.Block() as block:
            yield block, sb, sem
        nc.all_engine_barrier(sems_to_clear=range(min(numbers), max(numbers) + 1))


class Chain:

    def __init__(self, eng, sem):
        self.eng, self.sem, self.n = eng, sem, 0

    def __call__(self, ins):
        self.n += 1
        ins.then_inc(self.sem, 1)
        self.eng.wait_ge(self.sem, self.n)


def layer_norm(nc, env, label, src, dst, n, eps, gamma=None, beta=None, add_to=None,
               prefetch=()):
    ps, vec = env["ps"], env["vec"]
    half = n // 2
    pieces = [(0, half), (half, n)]
    with stage(nc, label) as (block, sb, sem):
        square = sb("square", [P, KC, n], F32)
        log = sb("log", [P, 2, half], F32)
        rstd = sb("rstd", [P, 2, half], F32)
        prefetched = sem("prefetched")
        if prefetch:
            @block.sync
            def _(sp):
                for to, of in prefetch:
                    sp.dma_start(to, of).then_inc(prefetched, 16)
                sp.wait_ge(prefetched, 16 * len(prefetch))

        mean_ready, centered, squared, var_ready, log_ready, rstd_ready, step = map(
            sem, ("mean_ready", "centered", "squared", "var_ready", "log_ready", "rstd_ready", "step"))

        @block.tensor
        def _(pe):
            for i, (a, b) in enumerate(pieces):
                for c in range(KC):
                    mm = pe.matmul(ps[:, i, 0:half], env["c"]("mean"), src[:, c, a:b],
                                   start=(c == 0), stop=(c == KC - 1))
                mm.then_inc(mean_ready, 1)
            for i, (a, b) in enumerate(pieces):
                pe.wait_ge(squared, i + 1)
                for c in range(KC):
                    mm = pe.matmul(ps[:, 2 + i, 0:half], env["c"]("mean"), square[:, c, a:b],
                                   start=(c == 0), stop=(c == KC - 1))
                mm.then_inc(var_ready, 1)

        @block.scalar
        def _(act):
            act.preload_act_table_set("natural_log_exp_and_others")
            for i, (a, b) in enumerate(pieces):
                act.wait_ge(centered, i + 1)
                act.activation(square[:, :, a:b], dst[:, :, a:b], ACT.Square).then_inc(squared, 1)
            for i in range(2):
                act.wait_ge(var_ready, i + 1)
                act.activation(log[:, i, :], ps[:, 2 + i, 0:half], ACT.Ln, bias=vec(eps)).then_inc(log_ready, 1)
                act.wait_ge(log_ready, i + 1)
                act.activation(rstd[:, i, :], log[:, i, :], ACT.Exp, scale=-0.5).then_inc(rstd_ready, 1)

        @block.vector
        def _(dve):
            chain = Chain(dve, step)
            for i, (a, b) in enumerate(pieces):
                dve.wait_ge(mean_ready, i + 1)
                for c in range(KC):
                    v = dve.tensor_tensor(dst[:, c, a:b], src[:, c, a:b], ps[:, i, 0:half], ALU.subtract)
                v.then_inc(centered, 1)
            for i, (a, b) in enumerate(pieces):
                dve.wait_ge(rstd_ready, i + 1)
                for c in range(KC):
                    chain(dve.tensor_tensor(dst[:, c, a:b], dst[:, c, a:b], rstd[:, i, :], ALU.mult))
                    if gamma:
                        chain(dve.tensor_scalar(dst[:, c, a:b], dst[:, c, a:b], vec(gamma, c), vec(beta, c),
                                                ALU.mult, ALU.add))
                    if add_to is not None:
                        chain(dve.tensor_tensor(add_to[:, c, a:b], add_to[:, c, a:b], dst[:, c, a:b], ALU.add))


def mixed(main, others):
    out, n = [], 0
    for k, step in enumerate(main):
        out.append(step)
        upto = len(others) * (k + 1) // len(main)
        out += others[n:upto]
        n = upto
    return out


def attention_order(wide, poly, bias, heads, nch, parts):
    groups = NH // heads

    def stacks(g, h):
        return [("stack", side, g, h) for side in "kq"]

    def maxima(g, h):
        return [] if poly else [("smax", g, h, t) for t in range(nch)]

    def ahead(g):
        out = stacks(g, 0) + stacks(g, 1) + maxima(g, 0) + stacks(g, 2) + maxima(g, 1) + stacks(g, 3)
        return out + (maxima(g, 2) + [("mrow", g, 0)] + maxima(g, 3) if not poly else [])

    def sums(g, t, part):
        last = t == nch - 1 and part == parts[t] - 1
        return [("av", g, t, part)] + ([("ocopy", g)] if last else [])

    steps = []
    if wide:
        values = [("value", t, w) for w in range(2) for t in range(nch)]
        steps += stacks(0, 0) + values[:1] + mixed(values[1:], maxima(0, 0) + stacks(1, 0)) + [("mrow", 0, 0)]
        before = None
        for g in range(groups):
            more = maxima(g + 1, 0) if g + 1 < groups else []
            for t in range(nch):
                steps.append(("prob", g, t, 0))
                if t == nch - 1 and g + 1 < groups:
                    nxt = stacks(g + 2, 0) if g + 2 < groups else [None, None]
                    steps += [nxt[0], ("mrow", g + 1, 0), nxt[1]]
                if before:
                    for part in range(parts[before[1]]):
                        steps += sums(*before, part)
                before = (g, t)
                share = (2, 1, 2, 0, 0)[t]
                steps += more[:share]
                more = more[share:]
        for part in range(parts[nch - 1]):
            steps += sums(*before, part)
    else:
        sides = "kqb" if bias else "kq"
        steps += [("dense", side, 0) for side in sides]
        first = ahead(0)
        steps += first[:4]
        steps += mixed(first[4:], [("value", t, 0) for t in range(nch)] + [("dense", side, 1) for side in sides])
        deferred = [] if poly else [("mrow", 0, 2)]
        before, norm = None, None
        for g in range(groups):
            probs = [("prob", g, t, h) for t in range(nch) for h in range(heads)]
            main = mixed(probs, ahead(g + 1) if g + 1 < groups else [])
            for s in main:
                steps.append(s)
                if s[0] != "prob":
                    continue
                _, _, t, h = s
                if t == 0 and h == 1:
                    steps += deferred
                    deferred = [] if poly else [("mrow", g + 1, 2)]
                if before and h in (1, 2) and h - 1 < parts[before[1]]:
                    steps += sums(*before, h - 1)
                if t == 1 and h == 0 and g:
                    steps.append(("norm", g - 1))
                if h == heads - 1:
                    before = (g, t)
        for part in range(parts[nch - 1]):
            steps += sums(*before, part)
        steps.append(("norm", groups - 1))
    out, uses = [], 0
    for s in steps:
        if s is None:
            continue
        if s[0] not in ("av", "ocopy"):
            s, uses = (*s, uses), uses + 1
        out.append(s)
    return out


def attention(nc, env, label, x, n, wqkv, out, causal=False, poly=False, bias=False, wide=False,
              bq="zero", bk="zero", bv=None, gate=None, exp_scale=1.0, prefetch=()):
    ps, vec, c32, c16, row = env["ps"], env["vec"], env["c"], env["c16"], env["row"]
    heads = 1 if wide else 4
    groups = NH // heads
    slots = 3
    sum_banks = 2 * slots
    pairs = heads // min(heads, 2)
    hd = HD2 if wide else HD
    mrows = P if bias else PART_ROWS
    krows = P if bias else MAX_ROW + 3
    cut = 256 if causal and not wide else n // 2
    toks = windows(n)
    nch = len(toks)
    hard = causal and not wide
    mask_q, mask_k = c16("soft_q" if wide else "hard_q"), c16("soft_k" if wide else "hard_k")
    halves = [(0, n // 2), (n // 2, n)]

    def bank(use, i):
        return 2 * (use % slots) + i

    def both(use, lo, hi, w):
        k = 2 * (use % slots)
        return ps[lo:hi, k:k + 2, 0:w]

    def two(ap):
        return ap.rearrange("p (i w) -> p i w", i=2)

    def q_pieces(t):
        a = P * t if hard else 0
        return [(i, max(a, lo), hi) for i, (lo, hi) in enumerate([(0, cut), (cut, n)]) if hi > a]

    def key_end(t):
        return min(P * (t + 1), n) if hard else n

    steps = attention_order(wide, poly, bias, heads, nch, [len(q_pieces(t)) for t in range(nch)])

    with stage(nc, label) as (block, sb, sem):
        sides = () if wide else ("kqb" if bias else "kq")
        high = {s: sb(f"high_{s}", [P, KC, n], F32R) for s in sides}
        low = {s: sb(f"low_{s}", [P, KC, n], F32R) for s in sides}
        kst = [sb(f"kst{i}", [P, heads, n], F32R) for i in range(2)]
        qst = [sb(f"qst{i}", [P, heads, n], F32R) for i in range(2)]
        kst2 = [sb(f"kst2_{i}", [P, heads, n], F32R) for i in range(2)] if wide else kst
        qst2 = [sb(f"qst2_{i}", [P, heads, n], F32R) for i in range(2)] if wide else qst
        value = sb("value", [P, nch, NH, HD2 if wide else VW], F32)
        ones = sb("ones", [P, HD2], F32) if wide else None
        prob = sb("prob", [P, 2 * heads, n], F32)
        osum = sb("osum", [P, 2, n], F32)
        inv = sb("inv", [P, n], F32)
        maxes = sb("maxes", [P, nch, heads], F32)
        mneg = sb("mneg", [P, nch, heads], F32)
        mrest = sb("mrest", [P, nch, heads], F32)
        mparts = [sb(f"mparts{i}", [P, nch, heads, 3], BF16) for i in range(2)]
        gates = sb("gates", [P, nch], F32)
        filled = [sem(f"filled{i}") for i in range(slots)]
        set_up, prefetched = sem("set_up"), sem("prefetched")
        high_ready, low_ready = {s: sem(f"high_ready_{s}") for s in sides}, {s: sem(f"low_ready_{s}") for s in sides}
        pool_step, dve_step = sem("pool_step"), sem("dve_step")
        values_read, values_ready, gate_ready = sem("values_read"), sem("values_ready"), sem("gate_ready")
        maxes_taken = sem("maxes_taken")
        k_high, q_high, k_stacked, q_stacked = sem("k_high"), sem("q_high"), sem("k_stacked"), sem("q_stacked")
        mparts_ready, mrows_ready = sem("mparts_ready"), sem("mrows_ready")
        exps_ready, shifted, masked = sem("exps_ready"), sem("shifted"), sem("masked")
        probs_used, sums_copied = sem("probs_used"), sem("sums_copied")
        logs_ready, inv_ready, normalised = sem("logs_ready"), sem("inv_ready"), sem("normalised")

        last_reader = {("dense", s): low_ready[s] for s in sides}
        last_reader |= {("stack", "k"): k_stacked, ("stack", "q"): q_stacked, "value": values_read,
                        "smax": maxes_taken, "mrow": mrows_ready, "prob": exps_ready, "norm": logs_ready}
        kind_of = {step[-1]: tuple(step[:2]) if step[0] in ("dense", "stack") else step[0]
                   for step in steps if step[0] not in ("av", "ocopy")}
        nth, seen = {}, {}
        for u in sorted(kind_of):
            seen[kind_of[u]] = seen.get(kind_of[u], 0) + 1
            nth[u] = seen[kind_of[u]]

        def mask_into(pe, use, pieces, t, mask):
            lo = toks[t][1]
            first = toks[t][0] + lo
            for i, a, b in pieces:
                u, v = max(a, first), min(b, first + P - lo)
                if u < v:
                    mm = pe.matmul(ps[:, bank(use, i), u - a:v - a], c16("ident"),
                                   mask[:, lo + u - first:lo + v - first],
                                   start=False, stop=True, skip_group_check=True)
            return mm

        if prefetch:
            @block.sync
            def _(sp):
                for dst, src in prefetch:
                    sp.dma_start(dst, src).then_inc(prefetched, 16)
                sp.wait_ge(prefetched, 16 * len(prefetch))

        @block.tensor
        def _(pe):
            for step in steps:
                kind, use = step[0], step[-1]
                if kind not in ("av", "ocopy") and use >= slots:
                    pe.wait_ge(last_reader[kind_of[use - slots]], nth[use - slots])
                if kind == "dense":
                    _, side, mc, _ = step
                    for i, (a, b) in enumerate(halves):
                        if side == "b":
                            mm = pe.matmul(ps[:, bank(use, i), 0:b - a], env["alpha_beta"][0:24, mc * P:mc * P + P],
                                           c32("trig")[0:24, a:b], start=True, stop=True)
                            continue
                        off = (D if side == "k" else 0) + mc * P
                        for c in range(KC):
                            mm = pe.matmul(ps[:, bank(use, i), 0:b - a], wqkv[:, c, off:off + P], x[:, c, a:b],
                                           start=(c == 0), stop=(c == KC - 1))
                    mm.then_inc(filled[use % slots], 1)
                elif kind == "value":
                    _, t, w, _ = step
                    a = toks[t][0]
                    width = 512 if wide else D + (1 if gate else 0)
                    off = 4 * NH * HD2 + w * 512 if wide else 2 * D
                    for c in range(KC):
                        mm = pe.matmul(ps[:, bank(use, 0), 0:width], x[:, c, a:a + P],
                                       wqkv[:, c, off:off + width], start=(c == 0), stop=(c == KC - 1))
                    mm.then_inc(filled[use % slots], 1)
                elif kind == "stack":
                    _, side, g, h, _ = step
                    head = g * heads + h
                    if not wide and head % 8 == 0:
                        pe.wait_ge(low_ready[side], head // 8 + 1)
                        if bias and side == "q":
                            pe.wait_ge(low_ready["b"], head // 8 + 1)
                    for i, (a, b) in enumerate(halves):
                        if wide:
                            off = (2 * NH * hd if side == "k" else 0) + 2 * head * hd
                            for c in range(KC):
                                mm = pe.matmul(ps[:, bank(use, i), 0:b - a], wqkv[:, c, off:off + 2 * hd],
                                               x[:, c, a:b], start=(c == 0), stop=(c == KC - 1))
                            continue
                        chain = [(side, 0, high), (side, 1, low)]
                        if bias and side == "q":
                            chain += [("b", 0, high), ("b", 1, low)]
                        for j, (s, no, part) in enumerate(chain):
                            pick = env["pick_parts"](s, no, head % 8)
                            mm = pe.matmul(ps[0:pick.shape[1], bank(use, i), 0:b - a], pick,
                                           part[s][:, head // 8, a:b], start=(j == 0), stop=(j == len(chain) - 1),
                                           skip_group_check=True)
                    mm.then_inc(filled[use % slots], 1)
                elif kind == "smax":
                    _, g, h, t, _ = step
                    a = toks[t][0]
                    if t == 0:
                        pe.wait_ge(k_stacked, g * heads + h + 1)
                        pe.wait_ge(q_stacked, g * heads + h + 1)
                        if g < 2 and h == 0:
                            pe.wait_ge(set_up, g + 2)
                    w = key_end(t) // 2
                    pieces = [(0, 0, w), (1, w, 2 * w)]
                    for i, u, v in pieces:
                        if wide:
                            pe.matmul(ps[:, bank(use, i), 0:w], qst[g % 2][:, h, a:a + P], kst[g % 2][:, h, u:v],
                                      start=True, stop=False, skip_group_check=True)
                        mm = pe.matmul(ps[:, bank(use, i), 0:w], qst2[g % 2][0:mrows, h, a:a + P],
                                       kst2[g % 2][0:mrows, h, u:v], start=not wide, stop=not (hard or wide),
                                       skip_group_check=True)
                    if hard or wide:
                        mm = mask_into(pe, use, pieces, t, mask_q)
                    mm.then_inc(filled[use % slots], 1)
                elif kind == "mrow":
                    _, g, h, _ = step
                    pe.wait_ge(mparts_ready, g * pairs + h // 2 + 1)
                    for i in range(min(heads, 2)):
                        out16 = ps[:, bank(use, i), :].bitcast(BF16)
                        for t, (a, lo) in enumerate(toks):
                            mm = pe.transpose(out16[MAX_ROW:MAX_ROW + 3, a + lo:a + P],
                                              mparts[g % 2][lo:P, t, h + i, :], c16("ident")[lo:P, lo:P])
                    mm.then_inc(filled[use % slots], 1)
                elif kind == "prob":
                    _, g, t, h, _ = step
                    a = toks[t][0]
                    if t == 0:
                        if poly:
                            pe.wait_ge(k_stacked, g * heads + h + 1)
                            pe.wait_ge(q_stacked, g * heads + h + 1)
                        else:
                            pe.wait_ge(mrows_ready, g * pairs + h // 2 + 1)
                    k = PART_ROWS if poly else krows
                    pieces = q_pieces(t)
                    plain = not ((hard and not poly) or wide)
                    for i, u, v in pieces:
                        if wide:
                            pe.matmul(ps[:, bank(use, i), 0:v - u], kst[g % 2][:, h, a:a + P], qst[g % 2][:, h, u:v],
                                      start=True, stop=False, skip_group_check=True)
                        mm = pe.matmul(ps[:, bank(use, i), 0:v - u], kst2[g % 2][0:k, h, a:a + P],
                                       qst2[g % 2][0:k, h, u:v], start=not wide, stop=plain, skip_group_check=True)
                    if not plain:
                        mm = mask_into(pe, use, pieces, t, mask_k)
                    mm.then_inc(filled[use % slots], 1)
                elif kind == "av":
                    _, g, t, part = step
                    lo = toks[t][1]
                    block_no = g * nch + t
                    if part == 0:
                        if block_no == 0:
                            pe.wait_ge(values_ready if gate else values_read, nch * (2 if wide else 1))
                            if wide:
                                pe.wait_ge(set_up, 4)
                        pe.wait_ge(masked if poly else exps_ready, (block_no + 1) * heads)
                        if t == 0 and g:
                            pe.wait_ge(sums_copied, g)
                    start, stop = t == 0, t == nch - 1
                    i, u, v = q_pieces(t)[part]
                    o = u - (cut if i else 0)
                    if wide:
                        for at, w in ((HD2 * (g % 2), value[lo:P, t, g, :]), (HD2 * (1 - g % 2), ones[lo:P, :])):
                            mm = pe.matmul(ps[at:at + HD2, sum_banks + i, o:o + v - u], w,
                                           prob[lo:P, block_no % 2, u:v], start=start, stop=stop,
                                           skip_group_check=True)
                    else:
                        for h in range(heads):
                            mm = pe.matmul(ps[VW * h:VW * h + VW, sum_banks + i, o:o + v - u],
                                           value[lo:P, t, g * heads + h, :],
                                           prob[lo:P, (block_no % 2) * heads + h, u:v], start=start, stop=stop,
                                           skip_group_check=True)
                    if part == len(q_pieces(t)) - 1:
                        mm.then_inc(probs_used, 1)
                elif kind == "norm":
                    _, g, _ = step
                    pe.wait_ge(sums_copied, g + 1)
                    for i, (a, b) in enumerate(halves):
                        mm = pe.matmul(ps[:, bank(use, i), 0:b - a], c32("sum_rows"),
                                       osum[:, g % 2, a:b], start=True, stop=True)
                    mm.then_inc(filled[use % slots], 1)

        @block.scalar
        def _(act):
            for step in steps:
                kind, use = step[0], step[-1]
                if kind == "dense":
                    _, side, mc, _ = step
                    act.wait_ge(filled[use % slots], use // slots + 1)
                    b = vec({"q": bq, "k": bk, "b": "zero"}[side], mc)
                    act.activation(two(high[side][:, mc, :]), both(use, 0, P, n // 2), ACT.Identity, bias=b)\
                        .then_inc(high_ready[side], 1)
                elif kind == "value" and gate:
                    _, t, w, _ = step
                    lo = toks[t][1]
                    act.wait_ge(filled[use % slots], use // slots + 1)
                    act.activation(gates[lo:P, t:t + 1], ps[lo:P, bank(use, 0), D:D + 1], ACT.Sigmoid,
                                   bias=row(gate)[lo:P, :]).then_inc(gate_ready, 1)
                elif kind == "stack":
                    _, side, g, h, _ = step
                    if wide:
                        act.wait_ge(filled[use % slots], use // slots + 1)
                        if side == "q":
                            act.activation(two(qst2[g % 2][0:hd, h, :]), both(use, 0, hd, n // 2), ACT.Copy)
                        dst, done = (kst, k_high) if side == "k" else (qst, q_high)
                        act.activation(two(dst[g % 2][:, h, :]), both(use, 0, P, n // 2), ACT.Copy).then_inc(done, 1)
                    elif side == "k":
                        act.wait_ge(filled[use % slots], use // slots + 1)
                        rows = HD2 if bias else PART_ROWS
                        act.activation(two(kst[g % 2][0:rows, h, :]), both(use, 0, rows, n // 2), ACT.Copy)\
                            .then_inc(k_stacked, 1)
                elif kind == "prob":
                    _, g, t, h, _ = step
                    lo = toks[t][1]
                    block_no = g * nch + t
                    if block_no == 0 and h == 0:
                        act.preload_act_table_set("natural_log_exp_and_others")
                    act.wait_ge(filled[use % slots], use // slots + 1)
                    if block_no >= 2 and h == 0:
                        act.wait_ge(probs_used, block_no - 1)
                    dst = prob[lo:P, (block_no % 2) * heads + h, :]
                    func = ACT.Square if poly else ACT.Exp
                    args = {"scale": exp_scale}
                    if poly:
                        args = {"bias": vec("root_half")[lo:P], "scale": exp_scale * 0.5 ** 0.5}
                    pieces = q_pieces(t)
                    if len(pieces) == 2 and pieces[0][2] - pieces[0][1] == pieces[1][2] - pieces[1][1]:
                        act.activation(two(dst[:, pieces[0][1]:n]), both(use, lo, P, pieces[0][2] - pieces[0][1]),
                                       func, **args).then_inc(exps_ready, 1)
                    else:
                        for i, u, v in pieces:
                            e = act.activation(dst[:, u:v], ps[lo:P, bank(use, i), 0:v - u], func, **args)
                        e.then_inc(exps_ready, 1)
                elif kind == "ocopy":
                    g = step[1]
                    act.wait_ge(probs_used, (g + 1) * nch)
                    k = sum_banks
                    if wide:
                        at, pair = HD2 * (g % 2), g // 2
                        if pair >= 2:
                            act.wait_ge(inv_ready, pair - 1)
                        act.activation(two(osum[at:at + HD2, pair % 2, :]),
                                       ps[HD2 - at:P - at, k:k + 2, 0:cut], ACT.Ln)
                        act.activation(two(out[at:at + HD2, pair, :]), ps[at:at + HD2, k:k + 2, 0:cut], ACT.Copy)\
                            .then_inc(sums_copied, 1)
                        if g % 2:
                            act.wait_ge(sums_copied, g + 1)
                            if pair:
                                act.wait_ge(normalised, pair)
                            act.activation(inv[:, :], osum[:, pair % 2, :], ACT.Exp, scale=-1.0).then_inc(inv_ready, 1)
                        continue
                    if g >= 2:
                        act.wait_ge(normalised, g - 1)
                    if cut * 2 == n:
                        act.activation(two(osum[:, g % 2, :]), ps[:, k:k + 2, 0:cut], ACT.Copy).then_inc(sums_copied, 1)
                    else:
                        act.activation(osum[:, g % 2, 0:cut], ps[:, k, 0:cut], ACT.Copy)
                        act.activation(osum[:, g % 2, cut:n], ps[:, k + 1, 0:n - cut], ACT.Copy)\
                            .then_inc(sums_copied, 1)
                elif kind == "mrow":
                    _, g, h, _ = step
                    act.wait_ge(filled[use % slots], use // slots + 1)
                    k = min(heads, 2)
                    b0 = bank(use, 0)
                    src = ps[:, b0:b0 + k, :].bitcast(BF16)
                    act.activation(qst2[g % 2][MAX_ROW:MAX_ROW + 3, h:h + k, :],
                                   src[MAX_ROW:MAX_ROW + 3, :, 0:n], ACT.Copy).then_inc(mrows_ready, 1)
                elif kind == "norm":
                    g = step[1]
                    act.wait_ge(filled[use % slots], use // slots + 1)
                    if g:
                        act.wait_ge(normalised, g)
                    act.activation(two(inv[:, :]), both(use, 0, P, n // 2), ACT.Ln,
                                   bias=vec("eps6" if poly else "zero")).then_inc(logs_ready, 1)
                    act.wait_ge(logs_ready, g + 1)
                    act.activation(inv[:, :], inv[:, :], ACT.Exp, scale=-1.0).then_inc(inv_ready, 1)

        @block.gpsimd
        def _(pool):
            chain = Chain(pool, pool_step)
            if wide:
                pool.memset(maxes[:, :, :], 0.0).then_inc(set_up, 1)
                pool.wait_ge(set_up, 1)
            else:
                chain(pool.memset(value[:, :, :, :], 0.0))
                chain(pool.memset(value[:, :, :, HD:HD + 1], 1.0))
                pool.memset(maxes[:, :, :], 0.0).then_inc(set_up, 1)
                pool.wait_ge(set_up, 1)
            for i in range(2):
                if wide:
                    chain(pool.memset(kst2[i][96:128, :, :].bitcast(F32), 0.0))
                    chain(pool.memset(qst2[i][96:128, :, :].bitcast(F32), 0.0))
                    chain(pool.tensor_copy(kst2[i][64:96, 0, :], c32("fix_k")[64:96, :]))
                    chain(pool.tensor_copy(qst2[i][64:96, 0, :], c32("fix_q")[64:96, :]))
                    pool.memset(kst2[i][MAX_ROW:MAX_ROW + 3, :, :].bitcast(F32), 1.0).then_inc(set_up, 1)
                elif bias:
                    for h in range(heads):
                        chain(pool.tensor_copy(kst[i][64:128, h, :], c32("trig_k")[64:128, :]))
                    pool.sem_inc(set_up, 1)
                elif not poly:
                    pool.memset(kst[i][MAX_ROW:MAX_ROW + 3, :, :].bitcast(F32), 1.0).then_inc(set_up, 1)
                else:
                    continue
                pool.wait_ge(set_up, i + 2)
            if wide:
                pool.memset(ones[:, :], 1.0).then_inc(set_up, 1)
            for step in steps:
                kind = step[0]
                if kind == "prob" and poly:
                    _, g, t, h, _ = step
                    a, lo = toks[t]
                    block_no = g * nch + t
                    pool.wait_ge(shifted, block_no * heads + h + 1)
                    if block_no or h:
                        pool.wait_ge(masked, block_no * heads + h)
                    d = prob[lo:P, (block_no % 2) * heads + h, a + lo:a + P]
                    pool.affine_select(out=d, in_=d, compare_op=ALU.is_ge, fill=0.0, base=0,
                                       pattern=[[1, P - lo]], channel_multiplier=-1).then_inc(masked, 1)
                elif kind == "norm":
                    g = step[1]
                    pool.wait_ge(inv_ready, g + 1)
                    if poly:
                        pool.wait_ge(masked, (g + 1) * nch * heads)
                    pool.tensor_tensor(out[:, g, 0:n], osum[:, g % 2, :], inv[:, :], ALU.mult).then_inc(normalised, 1)
                elif kind == "ocopy" and wide and step[1] % 2:
                    pair = step[1] // 2
                    pool.wait_ge(inv_ready, pair + 1)
                    pool.tensor_tensor(out[:, pair, :], out[:, pair, :], inv[:, :], ALU.mult).then_inc(normalised, 1)

        @block.vector
        def _(dve):
            chain = Chain(dve, dve_step)
            for no, step in enumerate(steps):
                if no == next(k for k, s in enumerate(steps) if s[0] != "dense"):
                    dve.wait_ge(set_up, 1)
                kind, use = step[0], step[-1]
                if kind == "dense":
                    _, side, mc, _ = step
                    dve.wait_ge(high_ready[side], mc + 1)
                    dve.scalar_tensor_tensor(out=two(low[side][:, mc, :]), in0=both(use, 0, P, n // 2),
                                             scalar=vec({"q": bq, "k": bk, "b": "zero"}[side], mc),
                                             in1=two(high[side][:, mc, :].bitcast(F32)), op0=ALU.add,
                                             op1=ALU.subtract).then_inc(low_ready[side], 1)
                elif kind == "value":
                    _, t, w, _ = step
                    lo = toks[t][1]
                    dve.wait_ge(filled[use % slots], use // slots + 1)
                    nh = 8 if wide else NH
                    src = ps[lo:P, bank(use, 0), 0:nh * hd].rearrange("p (h d) -> p h d", h=nh)
                    dst = value[lo:P, t, w * nh:(w + 1) * nh, 0:hd]
                    if bv:
                        bias_row = row(bv)[lo:P, :].rearrange("p (h d) -> p h d", h=NH)
                        if gate:
                            dve.wait_ge(gate_ready, t + 1)
                        v = dve.tensor_tensor(dst, src, bias_row, ALU.add)
                    else:
                        v = dve.tensor_copy(dst, src)
                    v.then_inc(values_read, 1)
                    if gate:
                        chain(dve.tensor_scalar(gates[lo:P, t:t + 1], gates[lo:P, t:t + 1], 0.1, 2.0,
                                                ALU.max, ALU.min))
                        dve.wait_ge(values_read, t + 1)
                        dve.tensor_scalar(dst, dst, gates[lo:P, t:t + 1], None, ALU.mult).then_inc(values_ready, 1)
                elif kind == "stack" and wide:
                    _, side, g, h, _ = step
                    if side == "k":
                        dve.wait_ge(k_high, g + 1)
                        dve.tensor_tensor(two(kst2[g % 2][0:hd, h, :]), both(use, 0, hd, n // 2),
                                          two(kst[g % 2][0:hd, h, :].bitcast(F32)), ALU.subtract).then_inc(k_stacked, 1)
                    else:
                        dve.wait_ge(q_high, g + 1)
                        dve.tensor_tensor(two(qst[g % 2][hd:P, h, :]), both(use, hd, P, n // 2),
                                          two(qst[g % 2][hd:P, h, :].bitcast(F32)), ALU.subtract).then_inc(q_stacked, 1)
                elif kind == "stack" and step[1] == "q":
                    _, side, g, h, _ = step
                    rows = P if bias else PART_ROWS
                    dve.wait_ge(filled[use % slots], use // slots + 1)
                    dve.tensor_copy(two(qst[g % 2][0:rows, h, :]), both(use, 0, rows, n // 2)).then_inc(q_stacked, 1)
                elif kind == "smax":
                    _, g, h, t, _ = step
                    lo = toks[t][1]
                    dve.wait_ge(filled[use % slots], use // slots + 1)
                    dve.tensor_reduce(maxes[lo:P, t, h:h + 1], both(use, lo, P, key_end(t) // 2),
                                      op=ALU.max, axis=AX.XY).then_inc(maxes_taken, 1)
                    if t == nch - 1 and (wide or h % 2):
                        dve.wait_ge(maxes_taken, nth[use])
                        k = slice(h + 1 - min(heads, 2), h + 1)
                        out3, m, r = mparts[g % 2][:, :, k, :], mneg[:, :, k], mrest[:, :, k]
                        chain(dve.tensor_scalar(m, maxes[:, :, k], -1.0, None, ALU.mult))
                        chain(dve.tensor_copy(out3[:, :, :, 0], m))
                        chain(dve.tensor_tensor(r, m, out3[:, :, :, 0], ALU.subtract))
                        chain(dve.tensor_copy(out3[:, :, :, 1], r))
                        dve.tensor_tensor(out3[:, :, :, 2], r, out3[:, :, :, 1], ALU.subtract)\
                            .then_inc(mparts_ready, 1)
                elif kind == "prob" and poly:
                    _, g, t, h, _ = step
                    lo = toks[t][1]
                    block_no = g * nch + t
                    dve.wait_ge(exps_ready, block_no * heads + h + 1)
                    d = prob[lo:P, (block_no % 2) * heads + h, q_pieces(t)[0][1]:n]
                    dve.tensor_scalar(d, d, 0.5, None, ALU.add).then_inc(shifted, 1)


def out_projection(nc, env, label, o, n, wo, res, dst, bo="zero", factor=None, parts=4):
    ps, vec = env["ps"], env["vec"]
    pieces = [(0, n // 2), (n // 2, n)]
    with stage(nc, label) as (block, sb, sem):
        projected, step = sem("projected"), sem("step")
        scaled = sb("scaled", [P, 2, n // 2], F32)

        @block.tensor
        def _(pe):
            for mc in range(KC):
                for i, (a, b) in enumerate(pieces):
                    for k in range(parts):
                        mm = pe.matmul(ps[:, 2 * mc + i, 0:b - a], wo[:, k, mc * P:mc * P + P],
                                       o[:, k, a:b], start=(k == 0), stop=(k == parts - 1))
                mm.then_inc(projected, 1)

        @block.vector
        def _(dve):
            chain = Chain(dve, step)
            for mc in range(KC):
                dve.wait_ge(projected, mc + 1)
                src = ps[:, 2 * mc:2 * mc + 2, 0:n // 2]
                r = res[:, mc, 0:n].rearrange("p (i w) -> p i w", i=2)
                d = dst[:, mc, 0:n].rearrange("p (i w) -> p i w", i=2)
                if factor is None:
                    chain(dve.scalar_tensor_tensor(out=d, in0=src, scalar=vec(bo, mc), in1=r, op0=ALU.add, op1=ALU.add))
                else:
                    chain(dve.tensor_scalar(scaled[:, :, :], src, vec(bo, mc), factor, ALU.add, ALU.mult))
                    chain(dve.tensor_tensor(d, r, scaled[:, :, :], ALU.add))


def hash_ffn(nc, env, label, x, h, w):
    ps, vec = env["ps"], env["vec"]
    fc, n = 4, T
    half, per = n // 2, n // E
    slots = 4
    pieces = [(0, half), (half, n)]
    steps = [(k, f) for f in range(fc) for k in "ab"] + [("c", mc) for mc in range(KC)]
    for e in range(E):
        steps.append(("u", e))
        if e:
            steps.append(("d", e - 1))
    steps.append(("d", E - 1))

    def mine(t, c, e):
        lo, hi = sorted((3 * e % E, (3 * e + 3) % E))
        return t[:, c, :].rearrange("p (j r) -> p r j", r=E)[:, lo:hi + 1:hi - lo, :]

    with stage(nc, label) as (block, sb, sem):
        w1 = sb("w1", [P, E, KC, D], F32)
        w2 = sb("w2", [P, E, KC, D], F32)
        gated = sb("gated", [P, fc, n], F32)
        silu = sb("silu", [P, fc, n], F32)
        hidden = sb("hidden", [P, 2, KC, 2 * per], F32)
        tmp = sb("tmp", [P, n], F32)
        filled = [sem(f"filled{i}") for i in range(slots)]
        freed = [sem(f"freed{i}") for i in range(slots)]
        w1_loaded = [sem(f"w1_loaded{e}") for e in range(E)]
        w2_loaded = [sem(f"w2_loaded{e}") for e in range(E)]
        silu_ready, gated_ready, hidden_ready, step = map(sem, ("silu_ready", "gated_ready", "hidden_ready", "step"))

        @block.sync
        def _(sp):
            for e in range(E):
                sp.dma_start(w1[:, e, :, :], w["f0_w1"][e].rearrange("(c p) n -> p c n", p=P)).then_inc(w1_loaded[e], 16)
                sp.dma_start(w2[:, e, :, :], w["f0_w2"][e].rearrange("(c p) n -> p c n", p=P)).then_inc(w2_loaded[e], 16)

        @block.tensor
        def _(pe):
            for use, (kind, k) in enumerate(steps):
                s = use % slots
                if use >= slots:
                    pe.wait_ge(freed[s], use // slots)
                if kind in "ab":
                    m = w["f0_sw1"] if kind == "a" else w["f0_sw3"]
                    for i, (a, b) in enumerate(pieces):
                        for c in range(KC):
                            mm = pe.matmul(ps[:, 2 * s + i, 0:half], m[:, c, k * P:k * P + P], x[:, c, a:b],
                                           start=(c == 0), stop=(c == KC - 1))
                elif kind == "c":
                    pe.wait_ge(gated_ready, fc)
                    for i, (a, b) in enumerate(pieces):
                        for f in range(fc):
                            mm = pe.matmul(ps[:, 2 * s + i, 0:half], w["f0_sw2"][:, f, k * P:k * P + P],
                                           gated[:, f, a:b], start=(f == 0), stop=(f == fc - 1))
                elif kind == "u":
                    pe.wait_ge(w1_loaded[k], 16)
                    for f in range(KC):
                        for c in range(KC):
                            mm = pe.matmul(ps[:, 2 * s + f, 0:2 * per].rearrange("p (r j) -> p r j", r=2),
                                           w1[:, k, c, f * P:f * P + P], mine(x, c, k),
                                           start=(c == 0), stop=(c == KC - 1))
                else:
                    pe.wait_ge(w2_loaded[k], 16)
                    pe.wait_ge(hidden_ready, k + 1)
                    for mc in range(KC):
                        for f in range(KC):
                            mm = pe.matmul(ps[:, 2 * s + mc, 0:2 * per], w2[:, k, f, mc * P:mc * P + P],
                                           hidden[:, k % 2, f, :], start=(f == 0), stop=(f == KC - 1))
                mm.then_inc(filled[s], 1)

        @block.scalar
        def _(act):
            for use, (kind, k) in enumerate(steps):
                s = use % slots
                if kind == "a":
                    act.wait_ge(filled[s], use // slots + 1)
                    act.activation(silu[:, k, :].rearrange("p (i w) -> p i w", i=2), ps[:, 2 * s:2 * s + 2, 0:half],
                                   ACT.Silu, bias=vec("f0_sb1", k)).then_inc(silu_ready, 1)
                    act.wait_ge(silu_ready, k + 1)
                    act.sem_inc(freed[s], 1)
                elif kind == "u":
                    act.wait_ge(filled[s], use // slots + 1)
                    if k >= 2:
                        u2 = steps.index(("d", k - 2))
                        act.wait_ge(filled[u2 % slots], u2 // slots + 1)
                    for f in range(KC):
                        a = act.activation(hidden[:, k % 2, f, :], ps[:, 2 * s + f, 0:2 * per], ACT.Gelu,
                                           bias=vec("f0_b1", 2 * k + f))
                    a.then_inc(hidden_ready, 1)
                    act.wait_ge(hidden_ready, k + 1)
                    act.sem_inc(freed[s], 1)

        @block.vector
        def _(dve):
            chain = Chain(dve, step)
            for use, (kind, k) in enumerate(steps):
                s = use % slots
                src = ps[:, 2 * s:2 * s + 2, 0:half]
                if kind == "b":
                    dve.wait_ge(filled[s], use // slots + 1)
                    dve.wait_ge(silu_ready, k + 1)
                    dve.scalar_tensor_tensor(out=gated[:, k, :].rearrange("p (i w) -> p i w", i=2), in0=src,
                                             scalar=vec("f0_sb3", k),
                                             in1=silu[:, k, :].rearrange("p (i w) -> p i w", i=2),
                                             op0=ALU.add, op1=ALU.mult).then_inc(gated_ready, 1)
                    dve.wait_ge(gated_ready, k + 1)
                    dve.sem_inc(freed[s], 1)
                elif kind == "c":
                    dve.wait_ge(filled[s], use // slots + 1)
                    chain(dve.tensor_scalar(tmp[:, :].rearrange("p (i w) -> p i w", i=2), src, vec("f0_sb2", k), 0.5,
                                            ALU.add, ALU.mult))
                    dve.sem_inc(freed[s], 1)
                    chain(dve.tensor_tensor(h[:, k, :], h[:, k, :], tmp[:, :], ALU.add))
                elif kind == "d":
                    dve.wait_ge(filled[s], use // slots + 1)
                    for mc in range(KC):
                        t3 = tmp[:, 0:2 * per].rearrange("p (r j) -> p r j", r=2)
                        chain(dve.tensor_scalar(tmp[:, 0:2 * per], ps[:, 2 * s + mc, 0:2 * per],
                                                vec("f0_b2", 2 * k + mc), 0.25, ALU.add, ALU.mult))
                        chain(dve.tensor_tensor(mine(h, mc, k), mine(h, mc, k), t3, ALU.add))
                    dve.sem_inc(freed[s], 1)


def dense_layers(nc, env, label, layers):
    ps, vec = env["ps"], env["vec"]
    half = T // 2
    slots = 4
    steps = [(li, mc) for li, layer in enumerate(layers) for mc in range(layer[4])]
    with stage(nc, label) as (block, sb, sem):
        filled = [sem(f"filled{i}") for i in range(slots)]
        evacuated = sem("evacuated")

        @block.tensor
        def _(pe):
            for use, (li, mc) in enumerate(steps):
                src, rows, weight, m, _, _, _, _ = layers[li]
                s = use % slots
                if mc == 0 and use:
                    pe.wait_ge(evacuated, use)
                elif use >= slots:
                    pe.wait_ge(evacuated, use - slots + 1)
                kcs = src.shape[1]
                for i in range(2):
                    for k in range(kcs):
                        mm = pe.matmul(ps[0:m, 2 * s + i, 0:half], weight[0:rows, k, mc * P:mc * P + m],
                                       src[0:rows, k, i * half:(i + 1) * half], start=(k == 0), stop=(k == kcs - 1))
                mm.then_inc(filled[s], 1)

        @block.scalar
        def _(act):
            for use, (li, mc) in enumerate(steps):
                _, _, _, m, _, dst, func, b = layers[li]
                s = use % slots
                act.wait_ge(filled[s], use // slots + 1)
                act.activation(dst[0:m, mc, :].rearrange("p (i w) -> p i w", i=2), ps[0:m, 2 * s:2 * s + 2, 0:half],
                               func, bias=vec(b, mc)[0:m]).then_inc(evacuated, 1)


def moe(nc, env, label, x, xrows, route_x, route_rows, route_w, route_b, top, w1, w2, hidden_chunks, outw, func,
        b1=None, b2=None, dense_expert=False, gated=False, finish=None,
        prefetch=()):
    ps, vec, c32, row = env["ps"], env["vec"], env["c"], env["row"]
    half = T // 2
    slots = 2
    toks = chunks(T)
    nt = len(toks)
    ne = E + (1 if dense_expert else 0)
    xk = x.shape[1]
    rk = route_x.shape[1]
    rw = E + (2 if dense_expert else 0)
    width = hidden_chunks * (2 if gated else 1) * P
    mcs = -(-outw // P)
    om = min(outw, P)
    steps = [("logit", 0, 0), ("turn", 0, 0)]
    for e in range(ne):
        steps.append(("spread", e, 0))
        for f in range(hidden_chunks):
            steps.append(("up", e, f))
            if gated:
                steps.append(("up2", e, f))
    hid_bufs = 4

    with stage(nc, label) as (block, sb, sem):
        logits = sb("logits", [P, nt, rw], F32)
        names = ("left", "chosen", "first", "key", "weight", "pick1")
        left, chosen, first, key, weight, pick1 = [sb(k, [P, nt, E], F32) for k in names]
        top1, top2, mk, total, inv = [sb(k, [P, nt, 1], F32) for k in ("top1", "top2", "mk", "total", "inv")]
        cmax, csum, cinv = [sb(k, [P, nt, 1], F32) for k in ("cmax", "csum", "cinv")]
        coef = sb("coef", [P, nt, 2], F32)
        comb = sb("comb", [P, nt, 9], F32)
        comb_t = sb("comb_t", [9, T], F32)
        spread = sb("spread", [P, 2, T], F32)
        w1b = sb("w1b", [P, 2, xk, width], F32)
        w2b = sb("w2b", [P, 2, hidden_chunks, outw], F32)
        hidden = sb("hidden", [P, hid_bufs, T], F32)
        gate_act = sb("gate_act", [P, hid_bufs, T], F32) if gated else None
        w_route = sb("w_route", [P, rk, rw], F32)
        b2_rows = sb("b2_rows", [9, outw], F32) if b2 is not None else None
        filled = [sem(f"filled{i}") for i in range(slots)]
        logits_read, product_ready = sem("logits_read"), sem("product_ready")
        route_loaded, b2_loaded, prefetched = sem("route_loaded"), sem("b2_loaded"), sem("prefetched")
        w1_loaded = [sem(f"w1_loaded{i}") for i in range(2)]
        w2_loaded = [sem(f"w2_loaded{i}") for i in range(2)]
        chain_sem, logits_ready, exp_ready, diff_ready, comb_ready, comb_t_ready = map(
            sem, ("chain", "logits_ready", "exp_ready", "diff_ready", "comb_ready", "comb_t_ready"))
        cleared, spread_ready, act_ready, hidden_ready, expert_up, down_done, acc_ready, out_step = map(
            sem, ("cleared", "spread_ready", "act_ready", "hidden_ready", "expert_up", "down_done", "acc_ready",
                  "out_step"))
        acc = lambda mc, i: ps[0:om, 4 + 2 * mc + i, 0:half]

        @block.sync
        def _(sp):
            sp.dma_start(w_route[0:route_rows, :, :], route_w.rearrange("(c p) n -> p c n", p=route_rows))\
                .then_inc(route_loaded, 16)
            if b2 is not None:
                sp.dma_start(b2_rows[0:ne, :], b2).then_inc(b2_loaded, 16)
            for dst, src in prefetch:
                sp.dma_start(dst, src).then_inc(prefetched, 16)
            for e in range(ne):
                if e >= 2:
                    sp.wait_ge(down_done, (e - 1) * hidden_chunks)
                sp.dma_start(w1b[0:xrows, e % 2, :, :], w1[e].rearrange("(c p) n -> p c n", p=xrows))\
                    .then_inc(w1_loaded[e % 2], 16)
                sp.dma_start(w2b[:, e % 2, :, :], w2[e].rearrange("(c p) n -> p c n", p=P))\
                    .then_inc(w2_loaded[e % 2], 16)
            if prefetch:
                sp.wait_ge(prefetched, 16 * len(prefetch))

        def last_read(use):
            kind, e, f = steps[use]
            no = e * hidden_chunks + f
            return {"logit": (logits_read, 1), "turn": (comb_t_ready, 2), "spread": (spread_ready, e + 1),
                    "up": (act_ready, no + 1), "up2": (product_ready, no + 1)}[kind]

        @block.tensor
        def _(pe):
            def down(e, f):
                pe.wait_ge(hidden_ready, e * hidden_chunks + f + 1)
                if f == 0:
                    pe.wait_ge(w2_loaded[e % 2], 16 * (e // 2 + 1))
                no = e * hidden_chunks + f
                last = no == ne * hidden_chunks - 1 and b2 is None
                for mc in range(mcs):
                    for i in range(2):
                        mm = pe.matmul(acc(mc, i), w2b[:, e % 2, f, mc * P:mc * P + om],
                                       hidden[:, no % hid_bufs, i * half:(i + 1) * half], start=(no == 0), stop=last)
                mm.then_inc(down_done, 1)

            pending = []
            for use, (kind, e, f) in enumerate(steps):
                s = use % slots
                if use >= slots:
                    pe.wait_ge(*last_read(use - slots))
                if kind == "logit":
                    pe.wait_ge(route_loaded, 16)
                    for t, (a, rows) in enumerate(toks):
                        for k in range(rk):
                            mm = pe.matmul(ps[0:rows, 2 * s, 16 * t:16 * t + rw], route_x[0:route_rows, k, a:a + rows],
                                           w_route[0:route_rows, k, :], start=(k == 0), stop=(k == rk - 1),
                                           skip_group_check=True)
                elif kind == "turn":
                    pe.wait_ge(comb_ready, 1)
                    for t, (a, rows) in enumerate(toks):
                        i = a // BANK
                        mm = pe.transpose(ps[0:9, 2 * s + i, a - i * BANK:a - i * BANK + rows], comb[0:rows, t, :],
                                          c32("ident")[0:rows, 0:rows])
                elif kind == "spread":
                    if e == 0:
                        pe.wait_ge(comb_t_ready, 2)
                    for i in range(2):
                        mm = pe.matmul(ps[:, 2 * s + i, 0:half], c32("pick")[0:9, e * P:e * P + P],
                                       comb_t[:, i * half:(i + 1) * half], start=True, stop=True)
                else:
                    if f == 0 and kind == "up":
                        pe.wait_ge(w1_loaded[e % 2], 16 * (e // 2 + 1))
                    off = (hidden_chunks * P if kind == "up2" else 0) + f * P
                    for i in range(2):
                        for k in range(xk):
                            mm = pe.matmul(ps[:, 2 * s + i, 0:half], w1b[0:xrows, e % 2, k, off:off + P],
                                           x[0:xrows, k, i * half:(i + 1) * half], start=(k == 0), stop=(k == xk - 1))
                mm.then_inc(filled[s], 1)
                if kind == ("up2" if gated else "up"):
                    pending.append((e, f))
                    if len(pending) > 1:
                        down(*pending.pop(0))
            down(*pending.pop(0))
            if b2 is not None:
                pe.wait_ge(b2_loaded, 16)
                for mc in range(mcs):
                    for i in range(2):
                        mm = pe.matmul(acc(mc, i), b2_rows[0:ne, mc * P:mc * P + om],
                                       comb_t[0:ne, i * half:(i + 1) * half], start=False, stop=True)
                mm.then_inc(acc_ready, 1)
            else:
                pe.wait_ge(down_done, ne * hidden_chunks)
                pe.sem_inc(acc_ready, 1)

        @block.scalar
        def _(act):
            act.wait_ge(diff_ready, 1)
            a = act.activation(weight[:, :, :], left[:, :, :], ACT.Exp)
            if dense_expert:
                a = act.activation(coef[:, :, :], coef[:, :, :], ACT.Exp)
            a.then_inc(exp_ready, 1)
            for use, (kind, e, f) in enumerate(steps):
                s = use % slots
                no = e * hidden_chunks + f
                src = ps[:, 2 * s:2 * s + 2, 0:half]
                if kind == "turn":
                    act.wait_ge(filled[s], use // slots + 1)
                    act.activation(comb_t[:, 0:BANK], ps[0:9, 2 * s, :], ACT.Copy).then_inc(comb_t_ready, 1)
                    act.activation(comb_t[:, BANK:T], ps[0:9, 2 * s + 1, 0:T - BANK], ACT.Copy).then_inc(comb_t_ready, 1)
                elif kind == "spread":
                    act.wait_ge(filled[s], use // slots + 1)
                    if e >= 2:
                        act.wait_ge(hidden_ready, (e - 1) * hidden_chunks)
                    act.activation(spread[:, e % 2, :].rearrange("p (i w) -> p i w", i=2), src, ACT.Copy)\
                        .then_inc(spread_ready, 1)
                elif kind == "up":
                    act.wait_ge(filled[s], use // slots + 1)
                    if no >= hid_bufs:
                        act.wait_ge(down_done, no - hid_bufs + 1)
                    dst = (gate_act if gated else hidden)[:, no % hid_bufs, :]
                    args = {} if b1 is None else {"bias": vec(b1, no)}
                    act.activation(dst.rearrange("p (i w) -> p i w", i=2), src, func, **args).then_inc(act_ready, 1)

        @block.vector
        def _(dve):
            chain = Chain(dve, chain_sem)

            def over_experts(t):
                return t[:, :, 0:1].to_broadcast([P, nt, E])

            chain(dve.memset(logits[:, :, :], 0.0))
            chain(dve.memset(comb[:, :, :], 0.0))
            dve.wait_ge(filled[0], 1)
            for t, (a, rows) in enumerate(toks):
                chain(dve.tensor_copy(logits[0:rows, t, :], ps[0:rows, 0, 16 * t:16 * t + rw]))
            dve.sem_inc(logits_read, 1)
            if route_b:
                bias_row = row(route_b)
                nb = 2 if dense_expert else E
                off = E if dense_expert else 0
                for t in range(nt):
                    chain(dve.tensor_tensor(logits[:, t, off:off + nb], logits[:, t, off:off + nb], bias_row, ALU.add))
            lg = logits[:, :, 0:E]
            chain(dve.tensor_reduce(top1[:, :, :], lg, op=ALU.max, axis=AX.X))
            chain(dve.tensor_tensor(left[:, :, :], lg, over_experts(top1), ALU.subtract))
            if dense_expert:
                lc = logits[:, :, E:E + 2]
                chain(dve.tensor_reduce(cmax[:, :, :], lc, op=ALU.max, axis=AX.X))
                chain(dve.tensor_tensor(coef[:, :, :], lc, cmax[:, :, 0:1].to_broadcast([P, nt, 2]), ALU.subtract))
            dve.sem_inc(diff_ready, 1)

            def pick_first(dst, of, best):
                chain(dve.tensor_tensor(key[:, :, :], of, over_experts(best), ALU.is_equal))
                for t in range(nt):
                    chain(dve.tensor_tensor(key[:, t, :], key[:, t, :], row("falling"), ALU.mult))
                chain(dve.tensor_reduce(mk[:, :, :], key[:, :, :], op=ALU.max, axis=AX.X))
                chain(dve.tensor_tensor(dst, key[:, :, :], over_experts(mk), ALU.is_equal))

            pick_first(pick1[:, :, :], lg, top1)
            if top == 2:
                chain(dve.scalar_tensor_tensor(out=chosen[:, :, :], in0=pick1[:, :, :], scalar=-1e30, in1=lg,
                                               op0=ALU.mult, op1=ALU.add))
                chain(dve.tensor_reduce(top2[:, :, :], chosen[:, :, :], op=ALU.max, axis=AX.X))
                pick_first(first[:, :, :], chosen[:, :, :], top2)
                chain(dve.tensor_tensor(pick1[:, :, :], pick1[:, :, :], first[:, :, :], ALU.add))
            dve.wait_ge(exp_ready, 1)
            if top == 2:
                chain(dve.tensor_tensor(weight[:, :, :], weight[:, :, :], pick1[:, :, :], ALU.mult))
                chain(dve.tensor_reduce(total[:, :, :], weight[:, :, :], op=ALU.add, axis=AX.X))
                chain(dve.reciprocal(inv[:, :, :], total[:, :, :]))
                chain(dve.tensor_tensor(comb[:, :, 0:E], weight[:, :, :], over_experts(inv), ALU.mult))
            else:
                chain(dve.tensor_reduce(total[:, :, :], weight[:, :, :], op=ALU.add, axis=AX.X))
                chain(dve.reciprocal(inv[:, :, :], total[:, :, :]))
                chain(dve.tensor_reduce(csum[:, :, :], coef[:, :, :], op=ALU.add, axis=AX.X))
                chain(dve.reciprocal(cinv[:, :, :], csum[:, :, :]))
                chain(dve.tensor_tensor(coef[:, :, :], coef[:, :, :], cinv[:, :, 0:1].to_broadcast([P, nt, 2]), ALU.mult))
                chain(dve.tensor_tensor(inv[:, :, :], inv[:, :, :], coef[:, :, 0:1], ALU.mult))
                chain(dve.tensor_tensor(comb[:, :, 0:E], pick1[:, :, :], over_experts(inv), ALU.mult))
                chain(dve.tensor_copy(comb[:, :, E:E + 1], coef[:, :, 1:2]))
            dve.sem_inc(comb_ready, 1)
            for use, (kind, e, f) in enumerate(steps):
                s = use % slots
                no = e * hidden_chunks + f
                if kind != ("up2" if gated else "up"):
                    continue
                if f == 0:
                    dve.wait_ge(spread_ready, e + 1)
                buf = hidden[:, no % hid_bufs, :]
                weights = spread[:, e % 2, :]
                dve.wait_ge(act_ready, no + 1)
                if gated:
                    g = gate_act[:, no % hid_bufs, :]
                    dve.wait_ge(filled[s], use // slots + 1)
                    if no >= hid_bufs:
                        dve.wait_ge(down_done, no - hid_bufs + 1)
                    dve.tensor_tensor(buf.rearrange("p (i w) -> p i w", i=2), ps[:, 2 * s:2 * s + 2, 0:half],
                                      g.rearrange("p (i w) -> p i w", i=2), ALU.mult).then_inc(product_ready, 1)
                    dve.wait_ge(product_ready, no + 1)
                dve.tensor_tensor(buf, buf, weights, ALU.mult).then_inc(hidden_ready, 1)
            dve.wait_ge(acc_ready, 1)
            for mc in range(mcs):
                src = ps[0:om, 4 + 2 * mc:6 + 2 * mc, 0:half]
                finish(dve, chain, mc, src)


def build(nc, a):
    vec_at, vec_n = columns(VECTORS)
    row_at, row_n = columns(ROWS)
    c_at, c_n = columns(CONSTS)
    c16_at, c16_n = columns(CONSTS16)
    with ExitStack() as scope:
        def sb(name, shape, dt=F32):
            return scope.enter_context(nc.sbuf_tensor(name, shape, dt))

        ps = scope.enter_context(nc.psum_tensor("banks", [P, 8, BANK], F32))
        vectors, rows = sb("vectors", [P, vec_n]), sb("rows", [P, row_n])
        consts, consts16 = sb("consts", [P, c_n]), sb("consts16", [P, c16_n], BF16)
        h, xa, xb = sb("h", [P, KC, T]), sb("xa", [P, KC, T]), sb("xb", [P, KC, T])
        ab = sb("alpha_beta_sb", [24, D])
        wqkv = [sb(f"wqkv{k}", [P, KC, 3 * D + 1]) for k in range(2)]
        wo = [sb(f"wo{k}", [P, 4, D]) for k in range(2)]
        place = {"tok": 0, "a0": 1, "a1": 0, "a2": 1, "a3": 0}
        stacks = {k: sb(f"stack_{k}", [P, 2, 8, w], F32R) for k, (_, w) in STACKS.items()}

        def vec(name, k=0):
            return vectors[:, vec_at[name][0] + k:vec_at[name][0] + k + 1]

        def row(name):
            return rows[:, row_at[name][0]:row_at[name][0] + row_at[name][1]]

        def c(name):
            return consts[:, c_at[name][0]:c_at[name][0] + c_at[name][1]]

        def c16(name):
            return consts16[:, c16_at[name][0]:c16_at[name][0] + c16_at[name][1]]

        def pick_parts(side, part, head):
            return stacks[side][:, part, head, :]

        def weights(label):
            k = place[label]
            width = a[f"{label}_qkv"].shape[-1]
            return [(wqkv[k][:, :, 0:width], a[f"{label}_qkv"]), (wo[k][:, :, :], a[f"{label}_o"])]

        env = {"ps": ps, "vec": vec, "row": row, "c": c, "c16": c16, "pick_parts": pick_parts, "alpha_beta": ab}

        with stage(nc, "load") as (block, sb2, sem):
            loads = [(vectors[:, :], a["vectors"]), (rows[:, :], a["rows"]), (consts[:, :], a["consts"]),
                     (consts16[:, :], a["consts16"]), (ab[:, :], a["alpha_beta"])]
            loads += weights("tok")
            raw = {k: sb2(f"raw_{k}", [P, 2, 8, w], F32) for k, (_, w) in STACKS.items()}
            loaded, stacks_loaded = sem("loaded"), sem("stacks_loaded")
            rounded = sem("rounded")

            @block.sync
            def _(sp):
                for k, t in raw.items():
                    sp.dma_start(t[:, :, :, :], a[f"stack_{k}"]).then_inc(stacks_loaded, 16)
                for dst, src in loads:
                    sp.dma_start(dst, src).then_inc(loaded, 16)
                sp.wait_ge(loaded, 16 * len(loads))

            @block.vector
            def _(dve):
                dve.wait_ge(stacks_loaded, 16 * len(raw))
                for k, t in raw.items():
                    dve.tensor_copy(stacks[k][:, :, :, :], t[:, :, :, :]).then_inc(rounded, 1)

        with nc.Fori(0, B) as b:
            with stage(nc, "input") as (block, _, sem):
                loaded = sem("loaded")

                @block.sync
                def _(sp):
                    sp.dma_start(h[:, :, 0:S_IMG], a["x"][b]).then_inc(loaded, 16)
                    sp.dma_start(h[:, :, S_IMG:T], a["txt"][b]).then_inc(loaded, 16)
                    sp.wait_ge(loaded, 32)

            def small_attention(label, x, n, res, dst, bo="zero", factor=None, gamma=None, **kw):
                o = scope2.enter_context(nc.sbuf_tensor(f"{label}_o", [P, 4, n], F32))
                k = place[label]
                attention(nc, env, label, x, n, wqkv[k], o, **kw)
                out_projection(nc, env, f"{label}_out", o, n, wo[k], res, dst, bo=bo, factor=factor)

            with ExitStack() as scope2:
                small_attention("tok", h, S_IMG, h, h, bo="tok_bo", bq="tok_bq", bk="tok_bk", bv="tok_bv",
                                exp_scale=HD ** -0.5, prefetch=weights("a0"))
            layer_norm(nc, env, "ln_tok", h, h, S_IMG, "eps5", "tok_g", "tok_b")

            layer_norm(nc, env, "ln_a0", h, xa, T, "eps5")
            with ExitStack() as scope2:
                small_attention("a0", xa, T, h, h, causal=True, bias=True, exp_scale=HD ** -0.5,
                                prefetch=weights("a1"))
            with ExitStack() as scope2:
                f0 = {k: scope2.enter_context(nc.sbuf_tensor(f"{k}_sb", list(a[k].shape), F32))
                      for k in ("f0_sw1", "f0_sw3", "f0_sw2")}
                layer_norm(nc, env, "ln_f0", h, xa, T, "eps5",
                           prefetch=[(t[:, :, :], a[k]) for k, t in f0.items()])
                hash_ffn(nc, env, "f0", xa, h, {**f0, "f0_w1": a["f0_w1"], "f0_w2": a["f0_w2"]})

            layer_norm(nc, env, "ln_a1", h, xa, T, "eps5")
            with ExitStack() as scope2:
                small_attention("a1", xa, T, h, h, causal=True, poly=True, exp_scale=HD ** -0.5,
                                prefetch=weights("a2"))
            with ExitStack() as scope2:
                def sb2(name, shape):
                    return scope2.enter_context(nc.sbuf_tensor(name, shape, F32))
                f1 = {k: sb2(f"{k}_sb", list(a[k].shape)) for k in
                      ("f1_enc_w", "f1_s2c_w", "f1_r_w1", "f1_c2s_w", "f1_dec_w")}
                spikes = sb2("spikes", [P, 4, T])
                cont, rh, moe_out = sb2("cont", [64, 1, T]), sb2("rh", [64, 1, T]), sb2("moe_out", [64, 1, T])
                layer_norm(nc, env, "ln_f1", h, xa, T, "eps5",
                           prefetch=[(t[:, :, :], a[k]) for k, t in f1.items()])
                dense_layers(nc, env, "f1_in", [
                    (xa, P, f1["f1_enc_w"], P, 4, spikes, ACT.Sigmoid, "f1_enc"),
                    (spikes, P, f1["f1_s2c_w"], 64, 1, cont, ACT.Identity, "f1_s2c"),
                    (cont, 64, f1["f1_r_w1"], 64, 1, rh, ACT.Relu, "f1_rb1")])

                def keep(dve, chain, mc, src):
                    chain(dve.tensor_copy(moe_out[:, 0, :].rearrange("p (i w) -> p i w", i=2), src))

                moe(nc, env, "m1", cont, 64, rh, 64, a["f1_r_w2"], "f1_rb2", 2, a["f1_e_w1"], a["f1_e_w2"], 2, 64,
                    ACT.Relu, b1="f1_eb1", b2=a["f1_e_b2"], finish=keep)
                dense_layers(nc, env, "f1_out", [
                    (moe_out, 64, f1["f1_c2s_w"], P, 4, spikes, ACT.Sigmoid, "f1_c2s"),
                    (spikes, P, f1["f1_dec_w"], P, 2, xa, ACT.Sigmoid, "f1_dec")])
            layer_norm(nc, env, "ln_f1_out", xa, xb, T, "eps5", "f1_g", "f1_b", add_to=h)

            with ExitStack() as scope2:
                o = scope2.enter_context(nc.sbuf_tensor("w2_o", [P, NH // 2, T], F32))
                wr = scope2.enter_context(nc.sbuf_tensor("w2_r_sb", list(a["w2_r"].shape), F32))
                w = scope2.enter_context(nc.sbuf_tensor("w2_qkv_sb", list(a["w2_qkv"].shape), F32))
                layer_norm(nc, env, "ln_w2", h, xa, T, "eps5",
                           prefetch=[(w[:, c, :], a["w2_qkv"][:, c, :]) for c in range(KC)])
                attention(nc, env, "w2", xa, T, w, o, causal=True, wide=True, exp_scale=HD2 ** -0.5,
                          prefetch=[(wr[:, :, :], a["w2_r"])])
                out_projection(nc, env, "w2_out", o, T, wr, h, h, parts=NH // 2)

            layer_norm(nc, env, "ln_a2x", h, xa, T, "eps5")
            layer_norm(nc, env, "ln_a2", xa, xb, T, "eps5", "a2_g1", "a2_b1")
            with ExitStack() as scope2:
                small_attention("a2", xb, T, xa, xa, bo="a2_bo", bq="a2_bq", bk="a2_bk", bv="a2_bv",
                                exp_scale=HD ** -0.5, prefetch=weights("a3"))
            layer_norm(nc, env, "ln_f2", xa, xb, T, "eps5", "a2_g2", "a2_b2")

            def add_both(dve, chain, mc, src):
                d = h[:, mc, :]
                chain(dve.tensor_tensor(d, d, xa[:, mc, :], ALU.add))
                d = d.rearrange("p (i w) -> p i w", i=2)
                chain(dve.tensor_tensor(d, d, src, ALU.add))

            moe(nc, env, "m2", xb, P, xb, P, a["f2_route"], "f2_coefb", 1, a["f2_w1"], a["f2_w2"], 8, D, ACT.Gelu,
                b1="f2_b1", b2=a["f2_b2"], dense_expert=True, finish=add_both)

            layer_norm(nc, env, "ln_a3x", h, xa, T, "eps5")
            layer_norm(nc, env, "ln_a3", xa, xb, T, "eps6", "a3_g", "a3_b")
            with ExitStack() as scope2:
                small_attention("a3", xb, T, h, h, bo="a3_bo", factor=0.1, causal=True, bq="a3_bq", bk="a3_bk",
                                bv="a3_bv", gate="a3_ent", exp_scale=HD ** -0.5 / 0.1)
            layer_norm(nc, env, "ln_f3", h, xa, T, "eps5")

            def add_one(dve, chain, mc, src):
                d = h[:, mc, :].rearrange("p (i w) -> p i w", i=2)
                chain(dve.tensor_tensor(d, d, src, ALU.add))

            moe(nc, env, "m3", xa, P, xa, P, a["f3_route"], None, 2, a["f3_w1"], a["f3_w2"], 4, D, ACT.Silu,
                gated=True, finish=add_one, prefetch=weights("tok"))

            with stage(nc, "output") as (block, _, sem):
                stored = sem("stored")

                @block.sync
                def _(sp):
                    sp.dma_start(a["out"][b], h[:, :, :]).then_inc(stored, 16)
                    sp.wait_ge(stored, 16)


def kernel(**inputs):
    import ml_dtypes
    import numpy as np
    import concourse.bacc as bacc
    from concourse.bass_utils import run_bass_kernel_spmd

    i = {k: np.asarray(v) for k, v in inputs.items()}
    f32 = np.float32

    def halves(w, p=P):
        return np.ascontiguousarray(w.reshape(-1, p, w.shape[-1]).transpose(1, 0, 2))

    def by_partition(v, p=P):
        v = v.reshape(-1, p).T
        return np.concatenate([v, np.zeros((P - p, v.shape[1]), f32)]) if p < P else v

    def head_rows(w):
        out = np.zeros((4, VW, 4, w.shape[-1]), f32)
        out[:, :HD] = w.reshape(4, 4, HD, -1).transpose(1, 2, 0, 3)
        return out.reshape(P, 4, -1)

    def twice(w):
        return np.repeat(w.reshape(D, NH, 1, HD2), 2, 2).reshape(D, -1)

    tok_w = i["L0_tok_W_qkv"].reshape(D, NH, 3, HD).transpose(0, 2, 1, 3).reshape(D, 3 * D)
    tok_b = i["L0_tok_b_qkv"].reshape(NH, 3, HD).transpose(1, 0, 2).reshape(3, D)
    a2_b = i["L2_ffn_bqkv"].reshape(3, D)
    a3_b = i["L3_attn_b_qkv"].reshape(3, D)
    vectors = {
        "zero": np.zeros((P, 4), f32), "eps5": np.full((P, 1), 1e-5, f32), "eps6": np.full((P, 1), 1e-6, f32),
        "root_half": np.full((P, 1), 0.5 ** 0.5, f32),
        "tok_bq": by_partition(tok_b[0]), "tok_bk": by_partition(tok_b[1]), "tok_bo": by_partition(i["L0_tok_b_out"]),
        "tok_g": by_partition(i["L0_tok_ln_gamma"]), "tok_b": by_partition(i["L0_tok_ln_beta"]),
        "f0_sb1": by_partition(i["L0_ffn_sb1"]), "f0_sb3": by_partition(i["L0_ffn_sb3"]),
        "f0_sb2": by_partition(i["L0_ffn_sb2"]), "f0_b1": by_partition(i["L0_ffn_b1"]),
        "f0_b2": by_partition(i["L0_ffn_b2"]),
        "f1_enc": by_partition(i["L1_ffn_enc_b"]), "f1_s2c": by_partition(i["L1_ffn_s2c_b"], 64),
        "f1_rb1": by_partition(i["L1_ffn_r_b1"], 64), "f1_eb1": by_partition(i["L1_ffn_e_b1"]),
        "f1_c2s": by_partition(i["L1_ffn_c2s_b"]), "f1_dec": by_partition(i["L1_ffn_dec_b"]),
        "f1_g": by_partition(i["L1_ffn_ln_g"]), "f1_b": by_partition(i["L1_ffn_ln_b"]),
        "a2_g1": by_partition(i["L2_ffn_ln1_g"]), "a2_b1": by_partition(i["L2_ffn_ln1_b"]),
        "a2_bq": by_partition(a2_b[0]), "a2_bk": by_partition(a2_b[1]), "a2_bo": by_partition(i["L2_ffn_bo"]),
        "a2_g2": by_partition(i["L2_ffn_ln2_g"]), "a2_b2": by_partition(i["L2_ffn_ln2_b"]),
        "f2_b1": np.concatenate([by_partition(i["L2_ffn_b1"]), by_partition(i["L2_ffn_rb1"])], 1),
        "a3_g": by_partition(i["L3_attn_ln_g"]), "a3_b": by_partition(i["L3_attn_ln_b"]),
        "a3_bq": by_partition(a3_b[0]), "a3_bk": by_partition(a3_b[1]), "a3_bo": by_partition(i["L3_attn_b_out"]),
    }
    rows = {"tok_bv": tok_b[2], "a2_bv": a2_b[2], "a3_bv": a3_b[2], "f1_rb2": i["L1_ffn_r_b2"],
            "f2_coefb": i["L2_ffn_coef_b"], "a3_ent": i["L3_attn_b_ent"], "falling": np.arange(E, 0, -1, dtype=f32)}

    eye = np.eye(P, dtype=f32)
    sum_rows = np.zeros((P, P), f32)
    for g in range(4):
        sum_rows[VW * g + HD, VW * g:VW * g + VW] = 1
    pick = np.zeros((P, 9, P), f32)
    for e in range(9):
        pick[e, e] = 1
    omega = (f32(10000.0) ** (f32(-2.0) * np.arange(HD // 2, dtype=f32) / f32(HD))).astype(np.float64)
    angle = omega[:, None] * np.arange(T)[None]
    cos, sin = np.cos(angle).astype(f32), np.sin(angle).astype(f32)
    trig = np.zeros((P, T), f32)
    trig[0:8], trig[8:16], trig[16:24] = 4 * cos, 4 * sin, -4 * cos
    keys = np.concatenate([cos, sin])
    key_high = (keys.view(np.uint32) + np.uint32(1 << 11) & np.uint32(0xFFFFF000)).view(f32)
    trig_k = np.zeros((P, T), f32)
    for at, part in TRIG_PARTS:
        trig_k[at:at + HD] = (key_high, keys - key_high)[part]
    trig_k[MAX_ROW:MAX_ROW + 3] = 1
    fix_k, fix_q = np.zeros((P, T), f32), np.zeros((P, T), f32)
    for t in range(1, 5):
        fix_k[HD2 + t - 1, P * t:P * t + P] = 1
        fix_q[HD2 + t - 1, :P * t] = -50.0 * 8
    consts = {"mean": np.full((P, P), 1 / D, f32), "ident": eye, "sum_rows": sum_rows, "trig_k": trig_k,
              "pick": pick.reshape(P, -1), "trig": trig, "fix_k": fix_k, "fix_q": fix_q}
    bf = ml_dtypes.bfloat16
    above = np.triu(np.ones((P, P), f32), 1)
    stacks = {}
    for side, (order, width) in STACKS.items():
        stacks[side] = np.zeros((P, 2, 8, width), f32)
        for at, part in order:
            for head in range(8):
                for d in range(HD):
                    stacks[side][head * HD + d, part, head, at + d] = 1
    consts16 = {"ident": eye.astype(bf), "hard_q": (above * f32(-1e30)).astype(bf),
                "hard_k": (above.T * f32(-1e30)).astype(bf), "soft_q": (above * f32(-400)).astype(bf),
                "soft_k": (above.T * f32(-400)).astype(bf)}

    al, be = i["L0_attn_alpha"], i["L0_attn_beta"]
    ab = np.zeros((3, 8, NH, 2, 8), f32)
    for r in range(8):
        ab[0, r, :, 0, r] = al[:, r]
        ab[1, r, :, 0, r] = be[:, r]
        ab[1, r, :, 1, r] = al[:, r]
        ab[2, r, :, 1, r] = be[:, r]

    arrays = {
        "x": np.ascontiguousarray(i["x"].reshape(B, S_IMG, KC, P).transpose(0, 3, 2, 1)),
        "txt": np.ascontiguousarray(i["txt"].reshape(B, S_TXT, KC, P).transpose(0, 3, 2, 1)),
        "vectors": np.concatenate([vectors[k] for k, _ in VECTORS], 1),
        "rows": np.ascontiguousarray(np.broadcast_to(np.concatenate([rows[k] for k, _ in ROWS])[None],
                                                     (P, columns(ROWS)[1]))),
        "consts": np.concatenate([consts[k] for k, _ in CONSTS], 1),
        "consts16": np.concatenate([consts16[k] for k, _ in CONSTS16], 1),
        "alpha_beta": ab.reshape(24, D),
        "tok_qkv": halves(tok_w), "tok_o": head_rows(i["L0_tok_W_out"]),
        "a0_qkv": halves(i["L0_attn_Wqkv"].T), "a0_o": head_rows(i["L0_attn_Wout"].T),
        "a1_qkv": halves(np.concatenate([i["L1_attn_Wq"].T, i["L1_attn_Wk"].T, i["L1_attn_Wv"].T], 1)),
        "a1_o": head_rows(i["L1_attn_Wo"].T),
        "a2_qkv": halves(i["L2_ffn_Wqkv"]), "a2_o": head_rows(i["L2_ffn_Wo"]),
        "a3_qkv": halves(np.concatenate([i["L3_attn_w_qkv"].T, i["L3_attn_w_ent"].T], 1)),
        "a3_o": head_rows(i["L3_attn_w_out"].T),
        "w2_qkv": halves(np.concatenate([twice(i["L2_attn_Wq"]), twice(i["L2_attn_Wk"]), i["L2_attn_Wv"]], 1)),
        **{f"stack_{k}": v for k, v in stacks.items()},
        "w2_r": halves(i["L2_attn_Wr"]),
        "f0_sw1": halves(i["L0_ffn_sw1"]), "f0_sw3": halves(i["L0_ffn_sw3"]), "f0_sw2": halves(i["L0_ffn_sw2"]),
        "f0_w1": i["L0_ffn_w1"], "f0_w2": i["L0_ffn_w2"],
        "f1_enc_w": halves(i["L1_ffn_enc_w"]), "f1_s2c_w": halves(i["L1_ffn_s2c_w"]),
        "f1_r_w1": halves(i["L1_ffn_r_w1"], 64), "f1_r_w2": i["L1_ffn_r_w2"],
        "f1_e_w1": i["L1_ffn_e_w1"], "f1_e_w2": i["L1_ffn_e_w2"], "f1_e_b2": i["L1_ffn_e_b2"],
        "f1_c2s_w": halves(i["L1_ffn_c2s_w"], 64), "f1_dec_w": halves(i["L1_ffn_dec_w"]),
        "f2_route": np.concatenate([i["L2_ffn_gate_w"], i["L2_ffn_coef_w"]], 1),
        "f2_w1": np.concatenate([i["L2_ffn_W1"], i["L2_ffn_rW1"][None]]),
        "f2_w2": np.concatenate([i["L2_ffn_W2"], i["L2_ffn_rW2"][None]]),
        "f2_b2": np.concatenate([i["L2_ffn_b2"], i["L2_ffn_rb2"][None]]),
        "f3_route": i["L3_ffn_gate_w"].T, "f3_w1": i["L3_ffn_w12"].transpose(0, 2, 1),
        "f3_w2": i["L3_ffn_w3"].transpose(0, 2, 1),
    }
    nc = bacc.Bacc("TRN2", target_bir_lowering=False, num_devices=1)
    fed, aps = {}, {}
    for name, v in arrays.items():
        v = np.ascontiguousarray(v)
        fed[f"in_{name}"] = v
        aps[name] = nc.dram_tensor(f"in_{name}", v.shape, mybir.dt.from_np(v.dtype), kind="ExternalInput").ap()
    aps["out"] = nc.dram_tensor("out_0", (B, P, KC, T), F32, kind="ExternalOutput").ap()
    build(nc, aps)
    r = run_bass_kernel_spmd(nc, [fed], core_ids=[0])
    got = r.results[0]["out_0"]
    return np.ascontiguousarray(got.transpose(0, 3, 2, 1).reshape(B, T, D))
```

```python
import concourse.bass as bass
from concourse import mybir
from contextlib import ExitStack, contextmanager

F32 = mybir.dt.float32
BF16 = mybir.dt.bfloat16
F32R = mybir.dt.float32r
ALU = mybir.AluOpType
ACT = mybir.ActivationFunctionType
AX = mybir.AxisListType

P = 128
B = 4
S_IMG, S_TXT = 512, 32
T = S_IMG + S_TXT
D = 256
KC = D // P
NH = 16
HD = 16
HD2 = 64
E = 8
BANK = 512
VW = 32
PART_ROWS = 96
MAX_ROW = 96
K_PARTS = ((0, 0), (16, 0), (32, 1))
Q_PARTS = ((0, 0), (16, 1), (32, 0))
TRIG_PARTS = ((64, 0), (80, 0), (99, 1))
BIAS_PARTS = ((64, 0), (80, 1), (99, 0))

VECTORS = [
    ("zero", 4), ("eps5", 1), ("eps6", 1), ("root_half", 1),
    ("tok_bq", 2), ("tok_bk", 2), ("tok_bo", 2), ("tok_g", 2), ("tok_b", 2),
    ("f0_sb1", 4), ("f0_sb3", 4), ("f0_sb2", 2), ("f0_b1", 16), ("f0_b2", 16),
    ("f1_enc", 4), ("f1_s2c", 1), ("f1_rb1", 1), ("f1_eb1", 16), ("f1_c2s", 4), ("f1_dec", 2),
    ("f1_g", 2), ("f1_b", 2),
    ("a2_g1", 2), ("a2_b1", 2), ("a2_bq", 2), ("a2_bk", 2), ("a2_bo", 2), ("a2_g2", 2), ("a2_b2", 2),
    ("f2_b1", 72),
    ("a3_g", 2), ("a3_b", 2), ("a3_bq", 2), ("a3_bk", 2), ("a3_bo", 2),
]
ROWS = [("tok_bv", D), ("a2_bv", D), ("a3_bv", D), ("f1_rb2", E), ("f2_coefb", 2), ("a3_ent", 1), ("falling", E)]
CONSTS = [("mean", P), ("ident", P), ("sum_rows", P), ("pick", 9 * P), ("trig", T), ("trig_k", T),
          ("fix_k", T), ("fix_q", T)]
STACKS = {"k": (K_PARTS, PART_ROWS), "q": (Q_PARTS, P), "b": (BIAS_PARTS, P)}
CONSTS16 = [("ident", P), ("hard_q", P), ("hard_k", P), ("soft_q", P), ("soft_k", P)]


def columns(table):
    at, out = 0, {}
    for name, n in table:
        out[name] = (at, n)
        at += n
    return out, at


def chunks(n):
    return [(a, min(P, n - a)) for a in range(0, n, P)]


def windows(n):
    out = [(a, 0) for a in range(0, n - P + 1, P)]
    return out + ([(n - P, P - n % P)] if n % P else [])


@contextmanager
def stage(nc, label):
    numbers = []
    with ExitStack() as scope:
        def sb(name, shape, dt):
            return scope.enter_context(nc.sbuf_tensor(f"{label}_{name}", shape, dt))

        def sem(name):
            s = scope.enter_context(nc.semaphore(f"{label}_{name}"))
            numbers.append(s.num)
            return s

        with nc.Block() as block:
            yield block, sb, sem
        nc.all_engine_barrier(sems_to_clear=range(min(numbers), max(numbers) + 1))


class Chain:

    def __init__(self, eng, sem):
        self.eng, self.sem, self.n = eng, sem, 0

    def __call__(self, ins):
        self.n += 1
        ins.then_inc(self.sem, 1)
        self.eng.wait_ge(self.sem, self.n)


def layer_norm(nc, env, label, src, dst, n, eps, gamma=None, beta=None, add_to=None,
               prefetch=(), project=None):
    ps, vec = env["ps"], env["vec"]
    half = n // 2
    pieces = [(0, half), (half, n)]
    with stage(nc, label) as (block, sb, sem):
        square = sb("square", [P, KC, n], F32)
        log = sb("log", [P, 2, half], F32)
        rstd = sb("rstd", [P, 2, half], F32)
        prefetched = sem("prefetched")
        if prefetch:
            @block.sync
            def _(sp):
                for to, of in prefetch:
                    sp.dma_start(to, of).then_inc(prefetched, 16)
                sp.wait_ge(prefetched, 16 * len(prefetch))

        mean_ready, centered, squared, var_ready, log_ready, rstd_ready, step = map(
            sem, ("mean_ready", "centered", "squared", "var_ready", "log_ready", "rstd_ready", "step"))
        if project:
            o, w, parts, bo, factor = project
            projected, added = sem("projected"), sem("added")
            scaled = sb("scaled", [P, 2 * KC, half], F32) if factor else None

        @block.tensor
        def _(pe):
            def projection(i, mc):
                a, b = pieces[i]
                for k in range(parts):
                    mm = pe.matmul(ps[:, 4 + 2 * i + mc, 0:half], w[:, k, mc * P:mc * P + P], o[:, k, a:b],
                                   start=(k == 0), stop=(k == parts - 1))
                mm.then_inc(projected, 1)

            def mean(i):
                a, b = pieces[i]
                if project:
                    pe.wait_ge(added, KC * (i + 1))
                for c in range(KC):
                    mm = pe.matmul(ps[:, i, 0:half], env["c"]("mean"), src[:, c, a:b],
                                   start=(c == 0), stop=(c == KC - 1))
                mm.then_inc(mean_ready, 1)

            def variance(i):
                a, b = pieces[i]
                pe.wait_ge(squared, i + 1)
                for c in range(KC):
                    mm = pe.matmul(ps[:, 2 + i, 0:half], env["c"]("mean"), square[:, c, a:b],
                                   start=(c == 0), stop=(c == KC - 1))
                mm.then_inc(var_ready, 1)

            if project:
                projection(0, 0)
                projection(0, 1)
                projection(1, 0)
                mean(0)
                projection(1, 1)
                variance(0)
                mean(1)
            else:
                mean(0)
                mean(1)
                variance(0)
            variance(1)

        @block.scalar
        def _(act):
            act.preload_act_table_set("natural_log_exp_and_others")
            for i, (a, b) in enumerate(pieces):
                act.wait_ge(centered, i + 1)
                act.activation(square[:, :, a:b], dst[:, :, a:b], ACT.Square).then_inc(squared, 1)
            for i in range(2):
                act.wait_ge(var_ready, i + 1)
                act.activation(log[:, i, :], ps[:, 2 + i, 0:half], ACT.Ln, bias=vec(eps)).then_inc(log_ready, 1)
                act.wait_ge(log_ready, i + 1)
                act.activation(rstd[:, i, :], log[:, i, :], ACT.Exp, scale=-0.5).then_inc(rstd_ready, 1)

        @block.vector
        def _(dve):
            chain = Chain(dve, step)

            def add(i, mc):
                a, b = pieces[i]
                d, p = src[:, mc, a:b], ps[:, 4 + 2 * i + mc, 0:half]
                dve.wait_ge(projected, KC * i + mc + 1)
                if factor is None:
                    dve.scalar_tensor_tensor(out=d, in0=p, scalar=vec(bo, mc), in1=d, op0=ALU.add,
                                             op1=ALU.add).then_inc(added, 1)
                else:
                    t = scaled[:, KC * i + mc, :]
                    chain(dve.tensor_scalar(t, p, vec(bo, mc), factor, ALU.add, ALU.mult))
                    dve.tensor_tensor(d, d, t, ALU.add).then_inc(added, 1)

            if project:
                for mc in range(KC):
                    add(0, mc)
                add(1, 0)
            for i, (a, b) in enumerate(pieces):
                if i and project:
                    add(1, 1)
                dve.wait_ge(mean_ready, i + 1)
                if project:
                    dve.wait_ge(added, KC * (i + 1))
                for c in range(KC):
                    v = dve.tensor_tensor(dst[:, c, a:b], src[:, c, a:b], ps[:, i, 0:half], ALU.subtract)
                v.then_inc(centered, 1)
            for i, (a, b) in enumerate(pieces):
                dve.wait_ge(rstd_ready, i + 1)
                for c in range(KC):
                    chain(dve.tensor_tensor(dst[:, c, a:b], dst[:, c, a:b], rstd[:, i, :], ALU.mult))
                    if gamma:
                        chain(dve.tensor_scalar(dst[:, c, a:b], dst[:, c, a:b], vec(gamma, c), vec(beta, c),
                                                ALU.mult, ALU.add))
                    if add_to is not None:
                        chain(dve.tensor_tensor(add_to[:, c, a:b], add_to[:, c, a:b], dst[:, c, a:b], ALU.add))


def mixed(main, others):
    out, n = [], 0
    for k, step in enumerate(main):
        out.append(step)
        upto = len(others) * (k + 1) // len(main)
        out += others[n:upto]
        n = upto
    return out


def attention_order(wide, poly, bias, heads, nch, parts):
    groups = NH // heads

    def stacks(g, h):
        return [("stack", side, g, h) for side in "kq"]

    def maxima(g, h):
        return [] if poly else [("smax", g, h, t) for t in range(nch)]

    def ahead(g):
        out = stacks(g, 0) + stacks(g, 1) + maxima(g, 0) + stacks(g, 2) + maxima(g, 1) + stacks(g, 3)
        return out + (maxima(g, 2) + [("mrow", g, 0)] + maxima(g, 3) if not poly else [])

    def sums(g, t, part):
        last = t == nch - 1 and part == parts[t] - 1
        return [("av", g, t, part)] + ([("ocopy", g)] if last else [])

    steps = []
    if wide:
        values = [("value", t, w) for w in range(2) for t in range(nch)]
        steps += stacks(0, 0) + values[:1] + mixed(values[1:], maxima(0, 0) + stacks(1, 0)) + [("mrow", 0, 0)]
        before = None
        for g in range(groups):
            more = maxima(g + 1, 0) if g + 1 < groups else []
            for t in range(nch):
                steps.append(("prob", g, t, 0))
                if t == nch - 1 and g + 1 < groups:
                    nxt = stacks(g + 2, 0) if g + 2 < groups else [None, None]
                    steps += [nxt[0], ("mrow", g + 1, 0), nxt[1]]
                if before:
                    for part in range(parts[before[1]]):
                        steps += sums(*before, part)
                before = (g, t)
                share = (2, 1, 2, 0, 0)[t]
                steps += more[:share]
                more = more[share:]
        for part in range(parts[nch - 1]):
            steps += sums(*before, part)
    else:
        sides = "kqb" if bias else "kq"
        steps += [("dense", side, 0) for side in sides]
        first = ahead(0)
        steps += [("value", t, 0) for t in range(2)] + first[:4]
        steps += mixed(first[4:], [("value", t, 0) for t in range(2, nch)] + [("dense", side, 1) for side in sides])
        deferred = [] if poly else [("mrow", 0, 2)]
        before, due = None, []
        for g in range(groups):
            probs = [("prob", g, t, h) for t in range(nch) for h in range(heads)]
            main = mixed(probs, ahead(g + 1) if g + 1 < groups else [])
            for s in main:
                if s[0] != "prob":
                    steps.append(s)
                    continue
                steps += due + [s]
                due = []
                _, _, t, h = s
                if t == 0 and h == 1:
                    steps += deferred
                    deferred = [] if poly else [("mrow", g + 1, 2)]
                if before and h in (1, 2) and h - 1 < parts[before[1]]:
                    due = sums(*before, h - 1)
                if t == 1 and h == 0 and g:
                    steps.append(("norm", g - 1))
                if h == heads - 1:
                    before = (g, t)
        for part in range(parts[nch - 1]):
            steps += sums(*before, part)
        steps.append(("norm", groups - 1))
    out, uses = [], 0
    for s in steps:
        if s is None:
            continue
        if s[0] not in ("av", "ocopy"):
            s, uses = (*s, uses), uses + 1
        out.append(s)
    return out


def attention(nc, env, label, x, n, wqkv, out, causal=False, poly=False, bias=False, wide=False,
              bq="zero", bk="zero", bv=None, gate=None, exp_scale=1.0, prefetch=()):
    ps, vec, c32, c16, row = env["ps"], env["vec"], env["c"], env["c16"], env["row"]
    heads = 1 if wide else 4
    groups = NH // heads
    slots = 3
    sum_banks = 2 * slots
    pairs = heads // min(heads, 2)
    hd = HD2 if wide else HD
    mrows = P if bias else PART_ROWS
    krows = P if bias else MAX_ROW + 3
    cut = 256 if causal and not wide else n // 2
    toks = windows(n)
    nch = len(toks)
    hard = causal and not wide
    mask_q, mask_k = c16("soft_q" if wide else "hard_q"), c16("soft_k" if wide else "hard_k")
    halves = [(0, n // 2), (n // 2, n)]

    def bank(use, i):
        return 2 * (use % slots) + i

    def both(use, lo, hi, w):
        k = 2 * (use % slots)
        return ps[lo:hi, k:k + 2, 0:w]

    def two(ap):
        return ap.rearrange("p (i w) -> p i w", i=2)

    def q_pieces(t):
        a = P * t if hard else 0
        return [(i, max(a, lo), hi) for i, (lo, hi) in enumerate([(0, cut), (cut, n)]) if hi > a]

    def key_end(t):
        return min(P * (t + 1), n) if hard else n

    steps = attention_order(wide, poly, bias, heads, nch, [len(q_pieces(t)) for t in range(nch)])

    with stage(nc, label) as (block, sb, sem):
        sides = () if wide else ("kqb" if bias else "kq")
        high = {s: sb(f"high_{s}", [P, KC, n], F32R) for s in sides}
        low = {s: sb(f"low_{s}", [P, KC, n], F32R) for s in sides}
        kst = [sb(f"kst{i}", [P, heads, n], F32R) for i in range(2)]
        qst = [sb(f"qst{i}", [P, heads, n], F32R) for i in range(2)]
        kst2 = [sb(f"kst2_{i}", [P, heads, n], F32R) for i in range(2)] if wide else kst
        qst2 = [sb(f"qst2_{i}", [P, heads, n], F32R) for i in range(2)] if wide else qst
        value = sb("value", [P, nch] + ([NH // 2, 3 * HD2] if wide else [NH, VW]), F32)
        prob = sb("prob", [P, 2 * heads, n], F32)
        osum = sb("osum", [P, 2, n], F32)
        inv = sb("inv", [P, n], F32)
        maxes = sb("maxes", [P, nch, heads], F32)
        mneg = sb("mneg", [P, nch, heads], F32)
        mrest = sb("mrest", [P, nch, heads], F32)
        mparts = [sb(f"mparts{i}", [P, nch, heads, 3], BF16) for i in range(2)]
        gates = sb("gates", [P, nch], F32)
        filled = [sem(f"filled{i}") for i in range(slots)]
        set_up, prefetched = sem("set_up"), sem("prefetched")
        high_ready, low_ready = {s: sem(f"high_ready_{s}") for s in sides}, {s: sem(f"low_ready_{s}") for s in sides}
        pool_step, dve_step = sem("pool_step"), sem("dve_step")
        values_read, values_ready, gate_ready = sem("values_read"), sem("values_ready"), sem("gate_ready")
        maxes_taken = sem("maxes_taken")
        k_high, q_high, k_stacked, q_stacked = sem("k_high"), sem("q_high"), sem("k_stacked"), sem("q_stacked")
        mparts_ready, mrows_ready = sem("mparts_ready"), sem("mrows_ready")
        exps_ready, shifted, masked = sem("exps_ready"), sem("shifted"), sem("masked")
        probs_used, sums_copied = sem("probs_used"), sem("sums_copied")
        logs_ready, inv_ready, normalised = sem("logs_ready"), sem("inv_ready"), sem("normalised")

        last_reader = {("dense", s): low_ready[s] for s in sides}
        last_reader |= {("stack", "k"): k_stacked, ("stack", "q"): q_stacked, "value": values_read,
                        "smax": maxes_taken, "mrow": mrows_ready, "prob": exps_ready, "norm": logs_ready}
        kind_of = {step[-1]: tuple(step[:2]) if step[0] in ("dense", "stack") else step[0]
                   for step in steps if step[0] not in ("av", "ocopy")}
        nth, seen = {}, {}
        for u in sorted(kind_of):
            seen[kind_of[u]] = seen.get(kind_of[u], 0) + 1
            nth[u] = seen[kind_of[u]]

        values_by_act = not wide and not bv

        def q_by_act(g):
            return g == 0 and not wide and not poly

        def mask_into(pe, use, pieces, t, mask):
            lo = toks[t][1]
            first = toks[t][0] + lo
            for i, a, b in pieces:
                u, v = max(a, first), min(b, first + P - lo)
                if u < v:
                    mm = pe.matmul(ps[:, bank(use, i), u - a:v - a], c16("ident"),
                                   mask[:, lo + u - first:lo + v - first],
                                   start=False, stop=True, skip_group_check=True)
            return mm

        if prefetch:
            @block.sync
            def _(sp):
                for dst, src in prefetch:
                    sp.dma_start(dst, src).then_inc(prefetched, 16)
                sp.wait_ge(prefetched, 16 * len(prefetch))

        @block.tensor
        def _(pe):
            for step in steps:
                kind, use = step[0], step[-1]
                if kind not in ("av", "ocopy") and use >= slots:
                    pe.wait_ge(last_reader[kind_of[use - slots]], nth[use - slots])
                if kind == "dense":
                    _, side, mc, _ = step
                    for i, (a, b) in enumerate(halves):
                        if side == "b":
                            mm = pe.matmul(ps[:, bank(use, i), 0:b - a], env["alpha_beta"][0:24, mc * P:mc * P + P],
                                           c32("trig")[0:24, a:b], start=True, stop=True)
                            continue
                        off = (D if side == "k" else 0) + mc * P
                        for c in range(KC):
                            mm = pe.matmul(ps[:, bank(use, i), 0:b - a], wqkv[:, c, off:off + P], x[:, c, a:b],
                                           start=(c == 0), stop=(c == KC - 1))
                    mm.then_inc(filled[use % slots], 1)
                elif kind == "value":
                    _, t, w, _ = step
                    a = toks[t][0]
                    width = 512 if wide else D + (1 if gate else 0)
                    off = 4 * NH * HD2 + w * 512 if wide else 2 * D
                    for c in range(KC):
                        mm = pe.matmul(ps[:, bank(use, 0), 0:width], x[:, c, a:a + P],
                                       wqkv[:, c, off:off + width], start=(c == 0), stop=(c == KC - 1))
                    mm.then_inc(filled[use % slots], 1)
                elif kind == "stack":
                    _, side, g, h, _ = step
                    head = g * heads + h
                    if not wide and head % 8 == 0:
                        pe.wait_ge(low_ready[side], head // 8 + 1)
                        if bias and side == "q":
                            pe.wait_ge(low_ready["b"], head // 8 + 1)
                    for i, (a, b) in enumerate(halves):
                        if wide:
                            off = (2 * NH * hd if side == "k" else 0) + 2 * head * hd
                            for c in range(KC):
                                mm = pe.matmul(ps[:, bank(use, i), 0:b - a], wqkv[:, c, off:off + 2 * hd],
                                               x[:, c, a:b], start=(c == 0), stop=(c == KC - 1))
                            continue
                        chain = [(side, 0, high), (side, 1, low)]
                        if bias and side == "q":
                            chain += [("b", 0, high), ("b", 1, low)]
                        for j, (s, no, part) in enumerate(chain):
                            pick = env["pick_parts"](s, no, head % 8)
                            mm = pe.matmul(ps[0:pick.shape[1], bank(use, i), 0:b - a], pick,
                                           part[s][:, head // 8, a:b], start=(j == 0), stop=(j == len(chain) - 1),
                                           skip_group_check=True)
                    mm.then_inc(filled[use % slots], 1)
                elif kind == "smax":
                    _, g, h, t, _ = step
                    a = toks[t][0]
                    if t == 0:
                        pe.wait_ge(k_stacked, g * heads + h + 1)
                        pe.wait_ge(q_stacked, g * heads + h + 1)
                        if g < 2 and h == 0:
                            pe.wait_ge(set_up, g + 2)
                    w = key_end(t) // 2
                    pieces = [(0, 0, w), (1, w, 2 * w)]
                    for i, u, v in pieces:
                        if wide:
                            pe.matmul(ps[:, bank(use, i), 0:w], qst[g % 2][:, h, a:a + P], kst[g % 2][:, h, u:v],
                                      start=True, stop=False, skip_group_check=True)
                        mm = pe.matmul(ps[:, bank(use, i), 0:w], qst2[g % 2][0:mrows, h, a:a + P],
                                       kst2[g % 2][0:mrows, h, u:v], start=not wide, stop=not (hard or wide),
                                       skip_group_check=True)
                    if hard or wide:
                        mm = mask_into(pe, use, pieces, t, mask_q)
                    mm.then_inc(filled[use % slots], 1)
                elif kind == "mrow":
                    _, g, h, _ = step
                    pe.wait_ge(mparts_ready, g * pairs + h // 2 + 1)
                    for i in range(min(heads, 2)):
                        out16 = ps[:, bank(use, i), :].bitcast(BF16)
                        for t, (a, lo) in enumerate(toks):
                            mm = pe.transpose(out16[MAX_ROW:MAX_ROW + 3, a + lo:a + P],
                                              mparts[g % 2][lo:P, t, h + i, :], c16("ident")[lo:P, lo:P])
                    mm.then_inc(filled[use % slots], 1)
                elif kind == "prob":
                    _, g, t, h, _ = step
                    a = toks[t][0]
                    if t == 0:
                        if poly:
                            pe.wait_ge(k_stacked, g * heads + h + 1)
                            pe.wait_ge(q_stacked, g * heads + h + 1)
                        else:
                            pe.wait_ge(mrows_ready, g * pairs + h // 2 + 1)
                    k = PART_ROWS if poly else krows
                    pieces = q_pieces(t)
                    plain = not ((hard and not poly) or wide)
                    for i, u, v in pieces:
                        if wide:
                            pe.matmul(ps[:, bank(use, i), 0:v - u], kst[g % 2][:, h, a:a + P], qst[g % 2][:, h, u:v],
                                      start=True, stop=False, skip_group_check=True)
                        mm = pe.matmul(ps[:, bank(use, i), 0:v - u], kst2[g % 2][0:k, h, a:a + P],
                                       qst2[g % 2][0:k, h, u:v], start=not wide, stop=plain, skip_group_check=True)
                    if not plain:
                        mm = mask_into(pe, use, pieces, t, mask_k)
                    mm.then_inc(filled[use % slots], 1)
                elif kind == "av":
                    _, g, t, part = step
                    lo = toks[t][1]
                    block_no = g * nch + t
                    if part == 0:
                        if block_no == 0:
                            pe.wait_ge(values_ready if gate else values_read, nch * (2 if wide else 1))
                            if wide:
                                pe.wait_ge(set_up, 4)
                        pe.wait_ge(masked if poly else exps_ready, (block_no + 1) * heads)
                        if t == 0 and g:
                            pe.wait_ge(sums_copied, g)
                    start, stop = t == 0, t == nch - 1
                    i, u, v = q_pieces(t)[part]
                    o = u - (cut if i else 0)
                    if wide:
                        at = HD2 * (g % 2)
                        mm = pe.matmul(ps[:, sum_banks + i, o:o + v - u], value[lo:P, t, g // 2, at:at + P],
                                       prob[lo:P, block_no % 2, u:v], start=start, stop=stop,
                                       skip_group_check=True)
                    else:
                        for h in range(heads):
                            mm = pe.matmul(ps[VW * h:VW * h + VW, sum_banks + i, o:o + v - u],
                                           value[lo:P, t, g * heads + h, :],
                                           prob[lo:P, (block_no % 2) * heads + h, u:v], start=start, stop=stop,
                                           skip_group_check=True)
                    if part == len(q_pieces(t)) - 1:
                        mm.then_inc(probs_used, 1)
                elif kind == "norm":
                    _, g, _ = step
                    pe.wait_ge(sums_copied, g + 1)
                    for i, (a, b) in enumerate(halves):
                        mm = pe.matmul(ps[:, bank(use, i), 0:b - a], c32("sum_rows"),
                                       osum[:, g % 2, a:b], start=True, stop=True)
                    mm.then_inc(filled[use % slots], 1)

        @block.scalar
        def _(act):
            for step in steps:
                kind, use = step[0], step[-1]
                if kind == "dense":
                    _, side, mc, _ = step
                    act.wait_ge(filled[use % slots], use // slots + 1)
                    b = vec({"q": bq, "k": bk, "b": "zero"}[side], mc)
                    act.activation(two(high[side][:, mc, :]), both(use, 0, P, n // 2), ACT.Identity, bias=b)\
                        .then_inc(high_ready[side], 1)
                elif kind == "value" and values_by_act:
                    _, t, w, _ = step
                    lo = toks[t][1]
                    act.wait_ge(filled[use % slots], use // slots + 1)
                    act.wait_ge(set_up, 1)
                    act.activation(value[lo:P, t, :, 0:hd],
                                   ps[lo:P, bank(use, 0), 0:NH * hd].rearrange("p (h d) -> p h d", h=NH), ACT.Copy)\
                        .then_inc(values_read, 1)
                elif kind == "value" and gate:
                    _, t, w, _ = step
                    lo = toks[t][1]
                    act.wait_ge(filled[use % slots], use // slots + 1)
                    act.activation(gates[lo:P, t:t + 1], ps[lo:P, bank(use, 0), D:D + 1], ACT.Sigmoid,
                                   bias=row(gate)[lo:P, :]).then_inc(gate_ready, 1)
                elif kind == "stack":
                    _, side, g, h, _ = step
                    if wide:
                        act.wait_ge(filled[use % slots], use // slots + 1)
                        if side == "q":
                            act.activation(two(qst2[g % 2][0:hd, h, :]), both(use, 0, hd, n // 2), ACT.Copy)
                        dst, done = (kst, k_high) if side == "k" else (qst, q_high)
                        act.activation(two(dst[g % 2][:, h, :]), both(use, 0, P, n // 2), ACT.Copy).then_inc(done, 1)
                    elif side == "q" and q_by_act(g):
                        rows = P if bias else PART_ROWS
                        act.wait_ge(filled[use % slots], use // slots + 1)
                        act.activation(two(qst[0][0:rows, h, :]), both(use, 0, rows, n // 2), ACT.Copy)\
                            .then_inc(q_stacked, 1)
                    elif side == "k":
                        act.wait_ge(filled[use % slots], use // slots + 1)
                        rows = HD2 if bias else PART_ROWS
                        act.activation(two(kst[g % 2][0:rows, h, :]), both(use, 0, rows, n // 2), ACT.Copy)\
                            .then_inc(k_stacked, 1)
                elif kind == "prob":
                    _, g, t, h, _ = step
                    lo = toks[t][1]
                    block_no = g * nch + t
                    if block_no == 0 and h == 0:
                        act.preload_act_table_set("natural_log_exp_and_others")
                    act.wait_ge(filled[use % slots], use // slots + 1)
                    if block_no >= 2 and h == 0:
                        act.wait_ge(probs_used, block_no - 1)
                    dst = prob[lo:P, (block_no % 2) * heads + h, :]
                    func = ACT.Square if poly else ACT.Exp
                    args = {"scale": exp_scale}
                    if poly:
                        args = {"bias": vec("root_half")[lo:P], "scale": exp_scale * 0.5 ** 0.5}
                    pieces = q_pieces(t)
                    if len(pieces) == 2 and pieces[0][2] - pieces[0][1] == pieces[1][2] - pieces[1][1]:
                        act.activation(two(dst[:, pieces[0][1]:n]), both(use, lo, P, pieces[0][2] - pieces[0][1]),
                                       func, **args).then_inc(exps_ready, 1)
                    else:
                        for i, u, v in pieces:
                            e = act.activation(dst[:, u:v], ps[lo:P, bank(use, i), 0:v - u], func, **args)
                        e.then_inc(exps_ready, 1)
                elif kind == "ocopy":
                    g = step[1]
                    act.wait_ge(probs_used, (g + 1) * nch)
                    k = sum_banks
                    if wide:
                        at, pair = HD2 * (g % 2), g // 2
                        if pair >= 2:
                            act.wait_ge(inv_ready, pair - 1)
                        act.activation(two(osum[at:at + HD2, pair % 2, :]),
                                       ps[HD2 - at:P - at, k:k + 2, 0:cut], ACT.Ln)
                        act.activation(two(out[at:at + HD2, pair, :]), ps[at:at + HD2, k:k + 2, 0:cut], ACT.Copy)\
                            .then_inc(sums_copied, 1)
                        if g % 2:
                            act.wait_ge(sums_copied, g + 1)
                            if pair:
                                act.wait_ge(normalised, pair)
                            act.activation(inv[:, :], osum[:, pair % 2, :], ACT.Exp, scale=-1.0).then_inc(inv_ready, 1)
                        continue
                    if g >= 2:
                        act.wait_ge(normalised, g - 1)
                    if cut * 2 == n:
                        act.activation(two(osum[:, g % 2, :]), ps[:, k:k + 2, 0:cut], ACT.Copy).then_inc(sums_copied, 1)
                    else:
                        act.activation(osum[:, g % 2, 0:cut], ps[:, k, 0:cut], ACT.Copy)
                        act.activation(osum[:, g % 2, cut:n], ps[:, k + 1, 0:n - cut], ACT.Copy)\
                            .then_inc(sums_copied, 1)
                elif kind == "mrow":
                    _, g, h, _ = step
                    act.wait_ge(filled[use % slots], use // slots + 1)
                    k = min(heads, 2)
                    b0 = bank(use, 0)
                    src = ps[:, b0:b0 + k, :].bitcast(BF16)
                    act.activation(qst2[g % 2][MAX_ROW:MAX_ROW + 3, h:h + k, :],
                                   src[MAX_ROW:MAX_ROW + 3, :, 0:n], ACT.Copy).then_inc(mrows_ready, 1)
                elif kind == "norm":
                    g = step[1]
                    act.wait_ge(filled[use % slots], use // slots + 1)
                    if g:
                        act.wait_ge(normalised, g)
                    act.activation(two(inv[:, :]), both(use, 0, P, n // 2), ACT.Ln,
                                   bias=vec("eps6" if poly else "zero")).then_inc(logs_ready, 1)
                    act.wait_ge(logs_ready, g + 1)
                    act.activation(inv[:, :], inv[:, :], ACT.Exp, scale=-1.0).then_inc(inv_ready, 1)

        @block.gpsimd
        def _(pool):
            chain = Chain(pool, pool_step)
            if wide:
                pool.memset(maxes[:, :, :], 0.0).then_inc(set_up, 1)
                pool.wait_ge(set_up, 1)
            else:
                chain(pool.memset(value[:, :, :, :], 0.0))
                chain(pool.memset(value[:, :, :, HD:HD + 1], 1.0))
                pool.memset(maxes[:, :, :], 0.0).then_inc(set_up, 1)
                pool.wait_ge(set_up, 1)
            for i in range(2):
                if wide:
                    chain(pool.memset(kst2[i][96:128, :, :].bitcast(F32), 0.0))
                    chain(pool.memset(qst2[i][96:128, :, :].bitcast(F32), 0.0))
                    chain(pool.tensor_copy(kst2[i][64:96, 0, :], c32("fix_k")[64:96, :]))
                    chain(pool.tensor_copy(qst2[i][64:96, 0, :], c32("fix_q")[64:96, :]))
                    pool.memset(kst2[i][MAX_ROW:MAX_ROW + 3, :, :].bitcast(F32), 1.0).then_inc(set_up, 1)
                elif bias:
                    for h in range(heads):
                        chain(pool.tensor_copy(kst[i][64:128, h, :], c32("trig_k")[64:128, :]))
                    pool.sem_inc(set_up, 1)
                elif not poly:
                    pool.memset(kst[i][MAX_ROW:MAX_ROW + 3, :, :].bitcast(F32), 1.0).then_inc(set_up, 1)
                else:
                    continue
                pool.wait_ge(set_up, i + 2)
            if wide:
                pool.memset(value[:, :, :, HD2:2 * HD2], 1.0).then_inc(set_up, 1)
            for step in steps:
                kind = step[0]
                if kind == "prob" and poly:
                    _, g, t, h, _ = step
                    a, lo = toks[t]
                    block_no = g * nch + t
                    pool.wait_ge(shifted, block_no * heads + h + 1)
                    if block_no or h:
                        pool.wait_ge(masked, block_no * heads + h)
                    d = prob[lo:P, (block_no % 2) * heads + h, a + lo:a + P]
                    pool.affine_select(out=d, in_=d, compare_op=ALU.is_ge, fill=0.0, base=0,
                                       pattern=[[1, P - lo]], channel_multiplier=-1).then_inc(masked, 1)
                elif kind == "norm":
                    g = step[1]
                    pool.wait_ge(inv_ready, g + 1)
                    if poly:
                        pool.wait_ge(masked, (g + 1) * nch * heads)
                    pool.tensor_tensor(out[:, g, 0:n], osum[:, g % 2, :], inv[:, :], ALU.mult).then_inc(normalised, 1)
                elif kind == "ocopy" and wide and step[1] % 2:
                    pair = step[1] // 2
                    pool.wait_ge(inv_ready, pair + 1)
                    pool.tensor_tensor(out[:, pair, :], out[:, pair, :], inv[:, :], ALU.mult).then_inc(normalised, 1)

        @block.vector
        def _(dve):
            chain = Chain(dve, dve_step)
            for no, step in enumerate(steps):
                if no == next(k for k, s in enumerate(steps) if s[0] != "dense"):
                    dve.wait_ge(set_up, 1)
                kind, use = step[0], step[-1]
                if kind == "dense":
                    _, side, mc, _ = step
                    dve.wait_ge(high_ready[side], mc + 1)
                    dve.scalar_tensor_tensor(out=two(low[side][:, mc, :]), in0=both(use, 0, P, n // 2),
                                             scalar=vec({"q": bq, "k": bk, "b": "zero"}[side], mc),
                                             in1=two(high[side][:, mc, :].bitcast(F32)), op0=ALU.add,
                                             op1=ALU.subtract).then_inc(low_ready[side], 1)
                elif kind == "value" and not values_by_act:
                    _, t, w, _ = step
                    lo = toks[t][1]
                    dve.wait_ge(filled[use % slots], use // slots + 1)
                    if wide:
                        src = ps[lo:P, bank(use, 0), 0:512].rearrange("p (q s d) -> p q s d", q=4, s=2)
                        dst = value[lo:P, t, 4 * w:4 * w + 4, :].rearrange("p q (s d) -> p q s d", s=3)[:, :, 0:3:2, :]
                    else:
                        src = ps[lo:P, bank(use, 0), 0:NH * hd].rearrange("p (h d) -> p h d", h=NH)
                        dst = value[lo:P, t, :, 0:hd]
                    if bv:
                        bias_row = row(bv)[lo:P, :].rearrange("p (h d) -> p h d", h=NH)
                        if gate:
                            dve.wait_ge(gate_ready, t + 1)
                        v = dve.tensor_tensor(dst, src, bias_row, ALU.add)
                    else:
                        v = dve.tensor_copy(dst, src)
                    v.then_inc(values_read, 1)
                    if gate:
                        chain(dve.tensor_scalar(gates[lo:P, t:t + 1], gates[lo:P, t:t + 1], 0.1, 2.0,
                                                ALU.max, ALU.min))
                        dve.wait_ge(values_read, t + 1)
                        dve.tensor_scalar(dst, dst, gates[lo:P, t:t + 1], None, ALU.mult).then_inc(values_ready, 1)
                elif kind == "stack" and wide:
                    _, side, g, h, _ = step
                    if side == "k":
                        dve.wait_ge(k_high, g + 1)
                        dve.tensor_tensor(two(kst2[g % 2][0:hd, h, :]), both(use, 0, hd, n // 2),
                                          two(kst[g % 2][0:hd, h, :].bitcast(F32)), ALU.subtract).then_inc(k_stacked, 1)
                    else:
                        dve.wait_ge(q_high, g + 1)
                        dve.tensor_tensor(two(qst[g % 2][hd:P, h, :]), both(use, hd, P, n // 2),
                                          two(qst[g % 2][hd:P, h, :].bitcast(F32)), ALU.subtract).then_inc(q_stacked, 1)
                elif kind == "stack" and step[1] == "q" and not q_by_act(step[2]):
                    _, side, g, h, _ = step
                    rows = P if bias else PART_ROWS
                    dve.wait_ge(filled[use % slots], use // slots + 1)
                    dve.tensor_copy(two(qst[g % 2][0:rows, h, :]), both(use, 0, rows, n // 2)).then_inc(q_stacked, 1)
                elif kind == "smax":
                    _, g, h, t, _ = step
                    lo = toks[t][1]
                    dve.wait_ge(filled[use % slots], use // slots + 1)
                    dve.tensor_reduce(maxes[lo:P, t, h:h + 1], both(use, lo, P, key_end(t) // 2),
                                      op=ALU.max, axis=AX.XY).then_inc(maxes_taken, 1)
                    if t == nch - 1 and (wide or h % 2):
                        dve.wait_ge(maxes_taken, nth[use])
                        k = slice(h + 1 - min(heads, 2), h + 1)
                        out3, m, r = mparts[g % 2][:, :, k, :], mneg[:, :, k], mrest[:, :, k]
                        chain(dve.tensor_scalar(m, maxes[:, :, k], -1.0, None, ALU.mult))
                        chain(dve.tensor_copy(out3[:, :, :, 0], m))
                        chain(dve.tensor_tensor(r, m, out3[:, :, :, 0], ALU.subtract))
                        chain(dve.tensor_copy(out3[:, :, :, 1], r))
                        dve.tensor_tensor(out3[:, :, :, 2], r, out3[:, :, :, 1], ALU.subtract)\
                            .then_inc(mparts_ready, 1)
                elif kind == "prob" and poly:
                    _, g, t, h, _ = step
                    lo = toks[t][1]
                    block_no = g * nch + t
                    dve.wait_ge(exps_ready, block_no * heads + h + 1)
                    d = prob[lo:P, (block_no % 2) * heads + h, q_pieces(t)[0][1]:n]
                    dve.tensor_scalar(d, d, 0.5, None, ALU.add).then_inc(shifted, 1)


def out_projection(nc, env, label, o, n, wo, res, dst, bo="zero", parts=4):
    ps, vec = env["ps"], env["vec"]
    pieces = [(0, n // 2), (n // 2, n)]
    with stage(nc, label) as (block, sb, sem):
        projected, step = sem("projected"), sem("step")

        @block.tensor
        def _(pe):
            for mc in range(KC):
                for i, (a, b) in enumerate(pieces):
                    for k in range(parts):
                        mm = pe.matmul(ps[:, 2 * mc + i, 0:b - a], wo[:, k, mc * P:mc * P + P],
                                       o[:, k, a:b], start=(k == 0), stop=(k == parts - 1))
                mm.then_inc(projected, 1)

        @block.vector
        def _(dve):
            chain = Chain(dve, step)
            for mc in range(KC):
                dve.wait_ge(projected, mc + 1)
                src = ps[:, 2 * mc:2 * mc + 2, 0:n // 2]
                r = res[:, mc, 0:n].rearrange("p (i w) -> p i w", i=2)
                d = dst[:, mc, 0:n].rearrange("p (i w) -> p i w", i=2)
                chain(dve.scalar_tensor_tensor(out=d, in0=src, scalar=vec(bo, mc), in1=r, op0=ALU.add, op1=ALU.add))


def hash_ffn(nc, env, label, x, h, w):
    ps, vec = env["ps"], env["vec"]
    fc, n = 4, T
    half, per = n // 2, n // E
    slots = 4
    pieces = [(0, half), (half, n)]
    steps = [(k, f) for f in range(fc) for k in "ab"] + [("c", mc) for mc in range(KC)]
    for e in range(E):
        steps.append(("u", e))
        if e:
            steps.append(("d", e - 1))
    steps.append(("d", E - 1))

    def mine(t, c, e):
        lo, hi = sorted((3 * e % E, (3 * e + 3) % E))
        return t[:, c, :].rearrange("p (j r) -> p r j", r=E)[:, lo:hi + 1:hi - lo, :]

    with stage(nc, label) as (block, sb, sem):
        w1 = sb("w1", [P, E, KC, D], F32)
        w2 = sb("w2", [P, E, KC, D], F32)
        gated = sb("gated", [P, fc, n], F32)
        silu = sb("silu", [P, fc, n], F32)
        hidden = sb("hidden", [P, 2, KC, 2 * per], F32)
        tmp = sb("tmp", [P, n], F32)
        filled = [sem(f"filled{i}") for i in range(slots)]
        freed = [sem(f"freed{i}") for i in range(slots)]
        w1_loaded = [sem(f"w1_loaded{e}") for e in range(E)]
        w2_loaded = [sem(f"w2_loaded{e}") for e in range(E)]
        silu_ready, gated_ready, hidden_ready, step = map(sem, ("silu_ready", "gated_ready", "hidden_ready", "step"))

        @block.sync
        def _(sp):
            for e in range(E):
                sp.dma_start(w1[:, e, :, :], w["f0_w1"][e].rearrange("(c p) n -> p c n", p=P)).then_inc(w1_loaded[e], 16)
                sp.dma_start(w2[:, e, :, :], w["f0_w2"][e].rearrange("(c p) n -> p c n", p=P)).then_inc(w2_loaded[e], 16)

        @block.tensor
        def _(pe):
            for use, (kind, k) in enumerate(steps):
                s = use % slots
                if use >= slots:
                    pe.wait_ge(freed[s], use // slots)
                if kind in "ab":
                    m = w["f0_sw1"] if kind == "a" else w["f0_sw3"]
                    for i, (a, b) in enumerate(pieces):
                        for c in range(KC):
                            mm = pe.matmul(ps[:, 2 * s + i, 0:half], m[:, c, k * P:k * P + P], x[:, c, a:b],
                                           start=(c == 0), stop=(c == KC - 1))
                elif kind == "c":
                    pe.wait_ge(gated_ready, fc)
                    for i, (a, b) in enumerate(pieces):
                        for f in range(fc):
                            mm = pe.matmul(ps[:, 2 * s + i, 0:half], w["f0_sw2"][:, f, k * P:k * P + P],
                                           gated[:, f, a:b], start=(f == 0), stop=(f == fc - 1))
                elif kind == "u":
                    pe.wait_ge(w1_loaded[k], 16)
                    for f in range(KC):
                        for c in range(KC):
                            mm = pe.matmul(ps[:, 2 * s + f, 0:2 * per].rearrange("p (r j) -> p r j", r=2),
                                           w1[:, k, c, f * P:f * P + P], mine(x, c, k),
                                           start=(c == 0), stop=(c == KC - 1))
                else:
                    pe.wait_ge(w2_loaded[k], 16)
                    pe.wait_ge(hidden_ready, k + 1)
                    for mc in range(KC):
                        for f in range(KC):
                            mm = pe.matmul(ps[:, 2 * s + mc, 0:2 * per], w2[:, k, f, mc * P:mc * P + P],
                                           hidden[:, k % 2, f, :], start=(f == 0), stop=(f == KC - 1))
                mm.then_inc(filled[s], 1)

        @block.scalar
        def _(act):
            for use, (kind, k) in enumerate(steps):
                s = use % slots
                if kind == "a":
                    act.wait_ge(filled[s], use // slots + 1)
                    act.activation(silu[:, k, :].rearrange("p (i w) -> p i w", i=2), ps[:, 2 * s:2 * s + 2, 0:half],
                                   ACT.Silu, bias=vec("f0_sb1", k)).then_inc(silu_ready, 1)
                    act.wait_ge(silu_ready, k + 1)
                    act.sem_inc(freed[s], 1)
                elif kind == "u":
                    act.wait_ge(filled[s], use // slots + 1)
                    if k >= 2:
                        u2 = steps.index(("d", k - 2))
                        act.wait_ge(filled[u2 % slots], u2 // slots + 1)
                    for f in range(KC):
                        a = act.activation(hidden[:, k % 2, f, :], ps[:, 2 * s + f, 0:2 * per], ACT.Gelu,
                                           bias=vec("f0_b1", 2 * k + f))
                    a.then_inc(hidden_ready, 1)
                    act.wait_ge(hidden_ready, k + 1)
                    act.sem_inc(freed[s], 1)

        @block.vector
        def _(dve):
            chain = Chain(dve, step)
            for use, (kind, k) in enumerate(steps):
                s = use % slots
                src = ps[:, 2 * s:2 * s + 2, 0:half]
                if kind == "b":
                    dve.wait_ge(filled[s], use // slots + 1)
                    dve.wait_ge(silu_ready, k + 1)
                    dve.scalar_tensor_tensor(out=gated[:, k, :].rearrange("p (i w) -> p i w", i=2), in0=src,
                                             scalar=vec("f0_sb3", k),
                                             in1=silu[:, k, :].rearrange("p (i w) -> p i w", i=2),
                                             op0=ALU.add, op1=ALU.mult).then_inc(gated_ready, 1)
                    dve.wait_ge(gated_ready, k + 1)
                    dve.sem_inc(freed[s], 1)
                elif kind == "c":
                    dve.wait_ge(filled[s], use // slots + 1)
                    chain(dve.tensor_scalar(tmp[:, :].rearrange("p (i w) -> p i w", i=2), src, vec("f0_sb2", k), 0.5,
                                            ALU.add, ALU.mult))
                    dve.sem_inc(freed[s], 1)
                    chain(dve.tensor_tensor(h[:, k, :], h[:, k, :], tmp[:, :], ALU.add))
                elif kind == "d":
                    dve.wait_ge(filled[s], use // slots + 1)
                    for mc in range(KC):
                        t3 = tmp[:, 0:2 * per].rearrange("p (r j) -> p r j", r=2)
                        chain(dve.tensor_scalar(tmp[:, 0:2 * per], ps[:, 2 * s + mc, 0:2 * per],
                                                vec("f0_b2", 2 * k + mc), 0.25, ALU.add, ALU.mult))
                        chain(dve.tensor_tensor(mine(h, mc, k), mine(h, mc, k), t3, ALU.add))
                    dve.sem_inc(freed[s], 1)


def dense_layers(nc, env, label, layers):
    ps, vec = env["ps"], env["vec"]
    half = T // 2
    slots = 4
    steps = [(li, mc) for li, layer in enumerate(layers) for mc in range(layer[4])]
    with stage(nc, label) as (block, sb, sem):
        filled = [sem(f"filled{i}") for i in range(slots)]
        evacuated = sem("evacuated")

        @block.tensor
        def _(pe):
            for use, (li, mc) in enumerate(steps):
                src, rows, weight, m, _, _, _, _ = layers[li]
                s = use % slots
                if mc == 0 and use:
                    pe.wait_ge(evacuated, use)
                elif use >= slots:
                    pe.wait_ge(evacuated, use - slots + 1)
                kcs = src.shape[1]
                for i in range(2):
                    for k in range(kcs):
                        mm = pe.matmul(ps[0:m, 2 * s + i, 0:half], weight[0:rows, k, mc * P:mc * P + m],
                                       src[0:rows, k, i * half:(i + 1) * half], start=(k == 0), stop=(k == kcs - 1))
                mm.then_inc(filled[s], 1)

        @block.scalar
        def _(act):
            for use, (li, mc) in enumerate(steps):
                _, _, _, m, _, dst, func, b = layers[li]
                s = use % slots
                act.wait_ge(filled[s], use // slots + 1)
                act.activation(dst[0:m, mc, :].rearrange("p (i w) -> p i w", i=2), ps[0:m, 2 * s:2 * s + 2, 0:half],
                               func, bias=vec(b, mc)[0:m]).then_inc(evacuated, 1)


def moe(nc, env, label, x, xrows, route_x, route_rows, route_w, route_b, top, w1, w2, hidden_chunks, outw, func,
        b1=None, b2=None, dense_expert=False, gated=False, finish=None, loaded=None,
        prefetch=()):
    ps, vec, c32, row = env["ps"], env["vec"], env["c"], env["row"]
    half = T // 2
    slots = 2
    toks = chunks(T)
    nt = len(toks)
    ne = E + (1 if dense_expert else 0)
    xk = x.shape[1]
    rk = route_x.shape[1]
    rw = E + (2 if dense_expert else 0)
    width = hidden_chunks * (2 if gated else 1) * P
    mcs = -(-outw // P)
    om = min(outw, P)
    early = 1 if gated else min(4, hidden_chunks)
    steps = [("logit", 0, 0)]
    for e in range(ne):
        for f in range(hidden_chunks):
            if e == 0 and f == early:
                steps += [("turn", 0, 0), ("spread", 0, 0)]
            if e and f == 0:
                steps.append(("spread", e, 0))
            steps.append(("up", e, f))
            if gated:
                steps.append(("up2", e, f))
    if early == hidden_chunks:
        at = 1 + early
        steps[at:at] = [("turn", 0, 0), ("spread", 0, 0)]
    routed = steps.index(("spread", 0, 0))
    hid_bufs = 4
    split = xrows == P
    lag = 2 if split else 1

    with stage(nc, label) as (block, sb, sem):
        logits = sb("logits", [P, nt, rw], F32)
        names = ("left", "chosen", "first", "key", "weight", "pick1")
        left, chosen, first, key, weight, pick1 = [sb(k, [P, nt, E], F32) for k in names]
        top1, top2, mk, total, inv = [sb(k, [P, nt, 1], F32) for k in ("top1", "top2", "mk", "total", "inv")]
        cmax, csum, cinv = [sb(k, [P, nt, 1], F32) for k in ("cmax", "csum", "cinv")]
        coef = sb("coef", [P, nt, 2], F32)
        comb = sb("comb", [P, nt, 9], F32)
        comb_t = sb("comb_t", [9, T], F32)
        spread = sb("spread", [P, 2, T], F32)
        w_route, w1b = loaded or (sb("w_route", [P, rk, rw], F32), sb("w1b", [P, 2, xk, width], F32))
        w2_bufs = 1 if split else 2
        w2b = sb("w2b", [P, w2_bufs, hidden_chunks, outw], F32)
        hidden = sb("hidden", [P, hid_bufs, T], F32)
        if split:
            x_parts = [sb(f"x_{k}", [P, xk, T], F32R) for k in ("high", "low")]
            w1_parts = [sb(f"w1_{k}", [P, 2, xk, width], F32R) for k in ("high", "low")]
            w2_parts = [sb(f"w2_{k}", [P, 2, hidden_chunks, outw], F32R) for k in ("high", "low")]
            hidden_parts = [sb(f"hidden_{k}", [P, hid_bufs, T], F32R) for k in ("high", "low")]
        gate_act = sb("gate_act", [P, hid_bufs, T], F32) if gated else None
        b2_rows = sb("b2_rows", [9, outw], F32) if b2 is not None else None
        filled = [sem(f"filled{i}") for i in range(slots)]
        logits_read, product_ready = sem("logits_read"), sem("product_ready")
        route_loaded, b2_loaded, prefetched = sem("route_loaded"), sem("b2_loaded"), sem("prefetched")
        w1_loaded = [sem(f"w1_loaded{i}") for i in range(2)]
        w2_loaded = [sem(f"w2_loaded{i}") for i in range(2)]
        chain_sem, logits_ready, exp_ready, diff_ready, comb_ready, comb_t_ready = map(
            sem, ("chain", "logits_ready", "exp_ready", "diff_ready", "comb_ready", "comb_t_ready"))
        cleared, spread_ready, act_ready, hidden_ready, expert_up, down_done, acc_ready, out_step = map(
            sem, ("cleared", "spread_ready", "act_ready", "hidden_ready", "expert_up", "down_done", "acc_ready",
                  "out_step"))
        x_high_ready, x_split, weighted, high_ready = map(sem, ("x_high_ready", "x_split", "weighted", "high_ready"))
        w1_split, w2_split = sem("w1_split"), sem("w2_split")
        w1_high_ready, w2_high_ready = sem("w1_high_ready"), sem("w2_high_ready")
        w1_first_split = sem("w1_first_split")
        acc = lambda mc, i: ps[0:om, 4 + 2 * mc + i, 0:half]

        @block.sync
        def _(sp):
            if not loaded:
                sp.dma_start(w_route[0:route_rows, :, :], route_w.rearrange("(c p) n -> p c n", p=route_rows))\
                    .then_inc(route_loaded, 16)
            if b2 is not None:
                sp.dma_start(b2_rows[0:ne, :], b2).then_inc(b2_loaded, 16)
            for e in range(ne):
                if e == 2:
                    for dst, src in prefetch:
                        sp.dma_start(dst, src).then_inc(prefetched, 16)
                if e >= 2 and split:
                    sp.wait_ge(*((w1_first_split, 1) if e == 2 else (w1_split, e - 2)))
                elif e >= 2:
                    sp.wait_ge(down_done, (e - 1) * hidden_chunks)
                if e or not loaded:
                    sp.dma_start(w1b[0:xrows, e % 2, :, :], w1[e].rearrange("(c p) n -> p c n", p=xrows))\
                        .then_inc(w1_loaded[e % 2], 16)
                if e and split:
                    sp.wait_ge(w2_split, e)
                sp.dma_start(w2b[:, e % w2_bufs, :, :], w2[e].rearrange("(c p) n -> p c n", p=P))\
                    .then_inc(w2_loaded[e % 2], 16)
            if prefetch:
                sp.wait_ge(prefetched, 16 * len(prefetch))

        def last_read(use):
            kind, e, f = steps[use]
            no = e * hidden_chunks + f
            return {"logit": (logits_read, 1), "turn": (comb_t_ready, 2), "spread": (spread_ready, e + 1),
                    "up": (act_ready, no + 1), "up2": (product_ready, no + 1)}[kind]

        if split:
            @block.gpsimd
            def _(pool):
                for e in range(ne):
                    for raw, parts, high_ready_w, done in ((w1b, w1_parts, w1_high_ready, w1_split),
                                                           (w2b, w2_parts, w2_high_ready, w2_split)):
                        if e == 0 and raw is w1b:
                            continue
                        pool.wait_ge(high_ready_w, e + 1)
                        pool.tensor_tensor(parts[1][:, e % 2, :, :], raw[:, e % raw.shape[1], :, :],
                                           parts[0][:, e % 2, :, :].bitcast(F32), ALU.subtract).then_inc(done, 1)

        def products(w, x):
            return ((w[0], x[0]), (w[0], x[1]), (w[1], x[0]))

        @block.tensor
        def _(pe):
            def down(e, f):
                pe.wait_ge(hidden_ready, e * hidden_chunks + f + 1)
                if f == 0 and split:
                    pe.wait_ge(w2_split, e + 1)
                elif f == 0:
                    pe.wait_ge(w2_loaded[e % 2], 16 * (e // 2 + 1))
                no = e * hidden_chunks + f
                last = no == ne * hidden_chunks - 1 and b2 is None
                for mc in range(mcs):
                    for i in range(2):
                        if split:
                            for j, (w, hid) in enumerate(products(w2_parts, hidden_parts)):
                                mm = pe.matmul(acc(mc, i), w[:, e % 2, f, mc * P:mc * P + om],
                                               hid[:, no % hid_bufs, i * half:(i + 1) * half],
                                               start=(no == 0 and j == 0), stop=(last and j == 2))
                            continue
                        mm = pe.matmul(acc(mc, i), w2b[:, e % 2, f, mc * P:mc * P + om],
                                       hidden[:, no % hid_bufs, i * half:(i + 1) * half], start=(no == 0), stop=last)
                mm.then_inc(down_done, 1)

            pending = []
            for use, (kind, e, f) in enumerate(steps):
                s = use % slots
                if use >= slots:
                    pe.wait_ge(*last_read(use - slots))
                if kind == "logit":
                    if not loaded:
                        pe.wait_ge(route_loaded, 16)
                    for t, (a, rows) in enumerate(toks):
                        for k in range(rk):
                            mm = pe.matmul(ps[0:rows, 2 * s, 16 * t:16 * t + rw], route_x[0:route_rows, k, a:a + rows],
                                           w_route[0:route_rows, k, :], start=(k == 0), stop=(k == rk - 1),
                                           skip_group_check=True)
                elif kind == "turn":
                    pe.wait_ge(comb_ready, 1)
                    for t, (a, rows) in enumerate(toks):
                        i = a // BANK
                        mm = pe.transpose(ps[0:9, 2 * s + i, a - i * BANK:a - i * BANK + rows], comb[0:rows, t, :],
                                          c32("ident")[0:rows, 0:rows])
                elif kind == "spread":
                    if e == 0:
                        pe.wait_ge(comb_t_ready, 2)
                    for i in range(2):
                        mm = pe.matmul(ps[:, 2 * s + i, 0:half], c32("pick")[0:9, e * P:e * P + P],
                                       comb_t[:, i * half:(i + 1) * half], start=True, stop=True)
                else:
                    if f == 0 and kind == "up" and split:
                        pe.wait_ge(*((w1_split, e) if e else (w1_first_split, 1)))
                        if e == 0:
                            pe.wait_ge(x_split, 1)
                    elif f == 0 and kind == "up":
                        pe.wait_ge(w1_loaded[e % 2], 16 * (e // 2 + 1))
                    off = (hidden_chunks * P if kind == "up2" else 0) + f * P
                    for i in range(2):
                        for k in range(xk):
                            if split:
                                for j, (w, xp) in enumerate(products(w1_parts, x_parts)):
                                    mm = pe.matmul(ps[:, 2 * s + i, 0:half], w[:, e % 2, k, off:off + P],
                                                   xp[:, k, i * half:(i + 1) * half], start=(k == 0 and j == 0),
                                                   stop=(k == xk - 1 and j == 2))
                                continue
                            mm = pe.matmul(ps[:, 2 * s + i, 0:half], w1b[0:xrows, e % 2, k, off:off + P],
                                           x[0:xrows, k, i * half:(i + 1) * half], start=(k == 0), stop=(k == xk - 1))
                mm.then_inc(filled[s], 1)
                if kind == ("up2" if gated else "up"):
                    pending.append((e, f))
                    while len(pending) > lag and use > routed:
                        down(*pending.pop(0))
            while pending:
                down(*pending.pop(0))
            if b2 is not None:
                pe.wait_ge(b2_loaded, 16)
                for mc in range(mcs):
                    for i in range(2):
                        mm = pe.matmul(acc(mc, i), b2_rows[0:ne, mc * P:mc * P + om],
                                       comb_t[0:ne, i * half:(i + 1) * half], start=False, stop=True)
                mm.then_inc(acc_ready, 1)
            else:
                pe.wait_ge(down_done, ne * hidden_chunks)
                pe.sem_inc(acc_ready, 1)

        @block.scalar
        def _(act):
            def high_part(no):
                act.wait_ge(weighted, no + 1)
                if no >= hid_bufs:
                    act.wait_ge(down_done, no - hid_bufs + 1)
                act.activation(hidden_parts[0][:, no % hid_bufs, :], hidden[:, no % hid_bufs, :], ACT.Copy)\
                    .then_inc(high_ready, 1)

            def high_weights(e, second):
                raw, parts = (w2b, w2_parts) if second else (w1b, w1_parts)
                if e >= 2:
                    act.wait_ge(down_done, (e - 1) * hidden_chunks)
                if e or second:
                    act.wait_ge((w2_loaded if second else w1_loaded)[e % 2],
                                16 * (e // 2 + (1 if second or e % 2 else 0)))
                act.activation(parts[0][:, e % 2, :, :], raw[:, e % raw.shape[1], :, :], ACT.Copy)\
                    .then_inc(w2_high_ready if second else w1_high_ready, 1)

            whole = []
            if split:
                act.activation(x_parts[0][:, :, :], x[:, :, :], ACT.Copy).then_inc(x_high_ready, 1)
                high_weights(0, False)
            act.wait_ge(diff_ready, 1)
            a = act.activation(weight[:, :, :], left[:, :, :], ACT.Exp)
            if dense_expert:
                a = act.activation(coef[:, :, :], coef[:, :, :], ACT.Exp)
            a.then_inc(exp_ready, 1)
            for use, (kind, e, f) in enumerate(steps):
                s = use % slots
                no = e * hidden_chunks + f
                src = ps[:, 2 * s:2 * s + 2, 0:half]
                if kind == "turn":
                    act.wait_ge(filled[s], use // slots + 1)
                    act.activation(comb_t[:, 0:BANK], ps[0:9, 2 * s, :], ACT.Copy).then_inc(comb_t_ready, 1)
                    act.activation(comb_t[:, BANK:T], ps[0:9, 2 * s + 1, 0:T - BANK], ACT.Copy).then_inc(comb_t_ready, 1)
                elif kind == "spread":
                    act.wait_ge(filled[s], use // slots + 1)
                    if e >= 2:
                        act.wait_ge(hidden_ready, (e - 1) * hidden_chunks)
                    act.activation(spread[:, e % 2, :].rearrange("p (i w) -> p i w", i=2), src, ACT.Copy)\
                        .then_inc(spread_ready, 1)
                    while len(whole) > 1:
                        high_part(whole.pop(0))
                elif kind == "up":
                    act.wait_ge(filled[s], use // slots + 1)
                    if no >= hid_bufs and split:
                        act.wait_ge(hidden_ready, no - hid_bufs + 1)
                    elif no >= hid_bufs:
                        act.wait_ge(down_done, no - hid_bufs + 1)
                    dst = (gate_act if gated else hidden)[:, no % hid_bufs, :]
                    args = {} if b1 is None else {"bias": vec(b1, no)}
                    act.activation(dst.rearrange("p (i w) -> p i w", i=2), src, func, **args).then_inc(act_ready, 1)
                    if split:
                        whole.append(no)
                        while len(whole) > 1 and use > routed:
                            high_part(whole.pop(0))
                        if no == 0:
                            high_weights(0, True)
                        if f == 2 and e + 1 < ne:
                            high_weights(e + 1, False)
                        if f == hidden_chunks - 1 and e + 1 < ne:
                            high_weights(e + 1, True)
            for no in whole:
                high_part(no)

        @block.vector
        def _(dve):
            chain = Chain(dve, chain_sem)

            def low_part(no):
                dve.wait_ge(high_ready, no + 1)
                b = no % hid_bufs
                dve.tensor_tensor(hidden_parts[1][:, b, :], hidden[:, b, :], hidden_parts[0][:, b, :].bitcast(F32),
                                  ALU.subtract).then_inc(hidden_ready, 1)

            def over_experts(t):
                return t[:, :, 0:1].to_broadcast([P, nt, E])

            chain(dve.memset(logits[:, :, :], 0.0))
            chain(dve.memset(comb[:, :, :], 0.0))
            dve.wait_ge(filled[0], 1)
            for t, (a, rows) in enumerate(toks):
                chain(dve.tensor_copy(logits[0:rows, t, :], ps[0:rows, 0, 16 * t:16 * t + rw]))
            dve.sem_inc(logits_read, 1)
            if route_b:
                bias_row = row(route_b)
                nb = 2 if dense_expert else E
                off = E if dense_expert else 0
                for t in range(nt):
                    chain(dve.tensor_tensor(logits[:, t, off:off + nb], logits[:, t, off:off + nb], bias_row, ALU.add))
            lg = logits[:, :, 0:E]
            chain(dve.tensor_reduce(top1[:, :, :], lg, op=ALU.max, axis=AX.X))
            chain(dve.tensor_tensor(left[:, :, :], lg, over_experts(top1), ALU.subtract))
            if dense_expert:
                lc = logits[:, :, E:E + 2]
                chain(dve.tensor_reduce(cmax[:, :, :], lc, op=ALU.max, axis=AX.X))
                chain(dve.tensor_tensor(coef[:, :, :], lc, cmax[:, :, 0:1].to_broadcast([P, nt, 2]), ALU.subtract))
            dve.sem_inc(diff_ready, 1)
            if split:
                dve.wait_ge(x_high_ready, 1)
                dve.tensor_tensor(x_parts[1][:, :, :], x[:, :, :], x_parts[0][:, :, :].bitcast(F32), ALU.subtract)\
                    .then_inc(x_split, 1)
                dve.wait_ge(w1_high_ready, 1)
                dve.tensor_tensor(w1_parts[1][:, 0, :, :], w1b[:, 0, :, :], w1_parts[0][:, 0, :, :].bitcast(F32),
                                  ALU.subtract).then_inc(w1_first_split, 1)

            def pick_first(dst, of, best):
                chain(dve.tensor_tensor(key[:, :, :], of, over_experts(best), ALU.is_equal))
                for t in range(nt):
                    chain(dve.tensor_tensor(key[:, t, :], key[:, t, :], row("falling"), ALU.mult))
                chain(dve.tensor_reduce(mk[:, :, :], key[:, :, :], op=ALU.max, axis=AX.X))
                chain(dve.tensor_tensor(dst, key[:, :, :], over_experts(mk), ALU.is_equal))

            pick_first(pick1[:, :, :], lg, top1)
            if top == 2:
                chain(dve.scalar_tensor_tensor(out=chosen[:, :, :], in0=pick1[:, :, :], scalar=-1e30, in1=lg,
                                               op0=ALU.mult, op1=ALU.add))
                chain(dve.tensor_reduce(top2[:, :, :], chosen[:, :, :], op=ALU.max, axis=AX.X))
                pick_first(first[:, :, :], chosen[:, :, :], top2)
                chain(dve.tensor_tensor(pick1[:, :, :], pick1[:, :, :], first[:, :, :], ALU.add))
            dve.wait_ge(exp_ready, 1)
            if top == 2:
                chain(dve.tensor_tensor(weight[:, :, :], weight[:, :, :], pick1[:, :, :], ALU.mult))
                chain(dve.tensor_reduce(total[:, :, :], weight[:, :, :], op=ALU.add, axis=AX.X))
                chain(dve.reciprocal(inv[:, :, :], total[:, :, :]))
                chain(dve.tensor_tensor(comb[:, :, 0:E], weight[:, :, :], over_experts(inv), ALU.mult))
            else:
                chain(dve.tensor_reduce(total[:, :, :], weight[:, :, :], op=ALU.add, axis=AX.X))
                chain(dve.reciprocal(inv[:, :, :], total[:, :, :]))
                chain(dve.tensor_reduce(csum[:, :, :], coef[:, :, :], op=ALU.add, axis=AX.X))
                chain(dve.reciprocal(cinv[:, :, :], csum[:, :, :]))
                chain(dve.tensor_tensor(coef[:, :, :], coef[:, :, :], cinv[:, :, 0:1].to_broadcast([P, nt, 2]), ALU.mult))
                chain(dve.tensor_tensor(inv[:, :, :], inv[:, :, :], coef[:, :, 0:1], ALU.mult))
                chain(dve.tensor_tensor(comb[:, :, 0:E], pick1[:, :, :], over_experts(inv), ALU.mult))
                chain(dve.tensor_copy(comb[:, :, E:E + 1], coef[:, :, 1:2]))
            dve.sem_inc(comb_ready, 1)
            for use, (kind, e, f) in enumerate(steps):
                s = use % slots
                no = e * hidden_chunks + f
                if kind != ("up2" if gated else "up"):
                    continue
                buf = hidden[:, no % hid_bufs, :]
                weights = spread[:, e % 2, :]
                dve.wait_ge(act_ready, no + 1)
                if gated:
                    g = gate_act[:, no % hid_bufs, :]
                    dve.wait_ge(filled[s], use // slots + 1)
                    if no >= hid_bufs and not split:
                        dve.wait_ge(down_done, no - hid_bufs + 1)
                    dve.tensor_tensor(buf.rearrange("p (i w) -> p i w", i=2), ps[:, 2 * s:2 * s + 2, 0:half],
                                      g.rearrange("p (i w) -> p i w", i=2), ALU.mult).then_inc(product_ready, 1)
                    dve.wait_ge(product_ready, no + 1)
                if f == 0:
                    dve.wait_ge(spread_ready, e + 1)
                if not split:
                    dve.tensor_tensor(buf, buf, weights, ALU.mult).then_inc(hidden_ready, 1)
                    continue
                dve.tensor_tensor(buf, buf, weights, ALU.mult).then_inc(weighted, 1)
                if no:
                    low_part(no - 1)
            if split:
                low_part(ne * hidden_chunks - 1)
            dve.wait_ge(acc_ready, 1)
            for mc in range(mcs):
                src = ps[0:om, 4 + 2 * mc:6 + 2 * mc, 0:half]
                finish(dve, chain, mc, src)


def build(nc, a):
    vec_at, vec_n = columns(VECTORS)
    row_at, row_n = columns(ROWS)
    c_at, c_n = columns(CONSTS)
    c16_at, c16_n = columns(CONSTS16)
    with ExitStack() as scope:
        def sb(name, shape, dt=F32):
            return scope.enter_context(nc.sbuf_tensor(name, shape, dt))

        ps = scope.enter_context(nc.psum_tensor("banks", [P, 8, BANK], F32))
        vectors, rows = sb("vectors", [P, vec_n]), sb("rows", [P, row_n])
        consts, consts16 = sb("consts", [P, c_n]), sb("consts16", [P, c16_n], BF16)
        h, xa, xb = sb("h", [P, KC, T]), sb("xa", [P, KC, T]), sb("xb", [P, KC, T])
        ab = sb("alpha_beta_sb", [24, D])
        wqkv = [sb(f"wqkv{k}", [P, KC, 3 * D + 1]) for k in range(2)]
        wo = [sb(f"wo{k}", [P, 4, D]) for k in range(2)]
        place = {"tok": 0, "a0": 1, "a1": 0, "a2": 1, "a3": 0}
        stacks = {k: sb(f"stack_{k}", [P, 2, 8, w], F32R) for k, (_, w) in STACKS.items()}

        def vec(name, k=0):
            return vectors[:, vec_at[name][0] + k:vec_at[name][0] + k + 1]

        def row(name):
            return rows[:, row_at[name][0]:row_at[name][0] + row_at[name][1]]

        def c(name):
            return consts[:, c_at[name][0]:c_at[name][0] + c_at[name][1]]

        def c16(name):
            return consts16[:, c16_at[name][0]:c16_at[name][0] + c16_at[name][1]]

        def pick_parts(side, part, head):
            return stacks[side][:, part, head, :]

        def weights(label):
            k = place[label]
            width = a[f"{label}_qkv"].shape[-1]
            return [(wqkv[k][:, :, 0:width], a[f"{label}_qkv"]), (wo[k][:, :, :], a[f"{label}_o"])]

        env = {"ps": ps, "vec": vec, "row": row, "c": c, "c16": c16, "pick_parts": pick_parts, "alpha_beta": ab}

        with stage(nc, "load") as (block, sb2, sem):
            loads = [(vectors[:, :], a["vectors"]), (rows[:, :], a["rows"]), (consts[:, :], a["consts"]),
                     (consts16[:, :], a["consts16"]), (ab[:, :], a["alpha_beta"])]
            loads += weights("tok")
            raw = {k: sb2(f"raw_{k}", [P, 2, 8, w], F32) for k, (_, w) in STACKS.items()}
            loaded, stacks_loaded = sem("loaded"), sem("stacks_loaded")
            rounded = sem("rounded")

            @block.sync
            def _(sp):
                for k, t in raw.items():
                    sp.dma_start(t[:, :, :, :], a[f"stack_{k}"]).then_inc(stacks_loaded, 16)
                for dst, src in loads:
                    sp.dma_start(dst, src).then_inc(loaded, 16)
                sp.wait_ge(loaded, 16 * len(loads))

            @block.vector
            def _(dve):
                dve.wait_ge(stacks_loaded, 16 * len(raw))
                for k, t in raw.items():
                    dve.tensor_copy(stacks[k][:, :, :, :], t[:, :, :, :]).then_inc(rounded, 1)

        with nc.Fori(0, B) as b:
            with stage(nc, "input") as (block, _, sem):
                loaded = sem("loaded")

                @block.sync
                def _(sp):
                    sp.dma_start(h[:, :, 0:S_IMG], a["x"][b]).then_inc(loaded, 16)
                    sp.dma_start(h[:, :, S_IMG:T], a["txt"][b]).then_inc(loaded, 16)
                    sp.wait_ge(loaded, 32)

            def small_attention(label, x, n, bo="zero", factor=None, **kw):
                o = scope2.enter_context(nc.sbuf_tensor(f"{label}_o", [P, 4, n], F32))
                k = place[label]
                attention(nc, env, label, x, n, wqkv[k], o, **kw)
                return o, wo[k], 4, bo, factor

            with ExitStack() as scope2:
                project = small_attention("tok", h, S_IMG, bo="tok_bo", bq="tok_bq", bk="tok_bk", bv="tok_bv",
                                          exp_scale=HD ** -0.5, prefetch=weights("a0"))
                layer_norm(nc, env, "ln_tok", h, h, S_IMG, "eps5", "tok_g", "tok_b", project=project)

            layer_norm(nc, env, "ln_a0", h, xa, T, "eps5")
            with ExitStack() as scope2:
                project = small_attention("a0", xa, T, causal=True, bias=True, exp_scale=HD ** -0.5,
                                          prefetch=weights("a1"))
                f0 = {k: scope2.enter_context(nc.sbuf_tensor(f"{k}_sb", list(a[k].shape), F32))
                      for k in ("f0_sw1", "f0_sw3", "f0_sw2")}
                layer_norm(nc, env, "ln_f0", h, xa, T, "eps5",
                           prefetch=[(t[:, :, :], a[k]) for k, t in f0.items()], project=project)
                hash_ffn(nc, env, "f0", xa, h, {**f0, "f0_w1": a["f0_w1"], "f0_w2": a["f0_w2"]})

            layer_norm(nc, env, "ln_a1", h, xa, T, "eps5")
            with ExitStack() as scope2:
                project = small_attention("a1", xa, T, causal=True, poly=True, exp_scale=HD ** -0.5,
                                          prefetch=weights("a2"))

                def sb2(name, shape):
                    return scope2.enter_context(nc.sbuf_tensor(name, shape, F32))
                f1 = {k: sb2(f"{k}_sb", list(a[k].shape)) for k in
                      ("f1_enc_w", "f1_s2c_w", "f1_r_w1", "f1_c2s_w", "f1_dec_w")}
                spikes = sb2("spikes", [P, 4, T])
                cont, rh, moe_out = sb2("cont", [64, 1, T]), sb2("rh", [64, 1, T]), sb2("moe_out", [64, 1, T])
                layer_norm(nc, env, "ln_f1", h, xa, T, "eps5",
                           prefetch=[(t[:, :, :], a[k]) for k, t in f1.items()], project=project)
                dense_layers(nc, env, "f1_in", [
                    (xa, P, f1["f1_enc_w"], P, 4, spikes, ACT.Sigmoid, "f1_enc"),
                    (spikes, P, f1["f1_s2c_w"], 64, 1, cont, ACT.Identity, "f1_s2c"),
                    (cont, 64, f1["f1_r_w1"], 64, 1, rh, ACT.Relu, "f1_rb1")])

                def keep(dve, chain, mc, src):
                    chain(dve.tensor_copy(moe_out[:, 0, :].rearrange("p (i w) -> p i w", i=2), src))

                moe(nc, env, "m1", cont, 64, rh, 64, a["f1_r_w2"], "f1_rb2", 2, a["f1_e_w1"], a["f1_e_w2"], 2, 64,
                    ACT.Relu, b1="f1_eb1", b2=a["f1_e_b2"], finish=keep)
                dense_layers(nc, env, "f1_out", [
                    (moe_out, 64, f1["f1_c2s_w"], P, 4, spikes, ACT.Sigmoid, "f1_c2s"),
                    (spikes, P, f1["f1_dec_w"], P, 2, xa, ACT.Sigmoid, "f1_dec")])
            with ExitStack() as scope2:
                o = scope2.enter_context(nc.sbuf_tensor("w2_o", [P, NH // 2, T], F32))
                wr = scope2.enter_context(nc.sbuf_tensor("w2_r_sb", list(a["w2_r"].shape), F32))
                w = scope2.enter_context(nc.sbuf_tensor("w2_qkv_sb", list(a["w2_qkv"].shape), F32))
                layer_norm(nc, env, "ln_f1_out", xa, xb, T, "eps5", "f1_g", "f1_b", add_to=h,
                           prefetch=[(w[:, 0, :], a["w2_qkv"][:, 0, :])])
                layer_norm(nc, env, "ln_w2", h, xa, T, "eps5", prefetch=[(w[:, 1, :], a["w2_qkv"][:, 1, :])])
                attention(nc, env, "w2", xa, T, w, o, causal=True, wide=True, exp_scale=HD2 ** -0.5,
                          prefetch=[(wr[:, :, :], a["w2_r"])])
                layer_norm(nc, env, "ln_a2x", h, xa, T, "eps5", project=(o, wr, NH // 2, "zero", None))

            layer_norm(nc, env, "ln_a2", xa, xb, T, "eps5", "a2_g1", "a2_b1")
            with ExitStack() as scope2:
                o, w, _, bo, _ = small_attention("a2", xb, T, bo="a2_bo", bq="a2_bq", bk="a2_bk", bv="a2_bv",
                                                 exp_scale=HD ** -0.5, prefetch=weights("a3"))
                out_projection(nc, env, "a2_out", o, T, w, xa, xa, bo=bo)

            def expert_inputs(stack, label, width, n):
                route = stack.enter_context(nc.sbuf_tensor(f"{label}_route_sb", [P, KC, n], F32))
                first = stack.enter_context(nc.sbuf_tensor(f"{label}_w1_sb", [P, 2, KC, width], F32))
                sources = a[f"{label}_route"], a[f"{label}_w1"][0]
                return (route, first), [(dst, src.rearrange("(c p) n -> p c n", p=P))
                                        for dst, src in zip((route[:, :, :], first[:, 0, :, :]), sources)]

            def add_both(dve, chain, mc, src):
                d = h[:, mc, :]
                chain(dve.tensor_tensor(d, d, xa[:, mc, :], ALU.add))
                d = d.rearrange("p (i w) -> p i w", i=2)
                chain(dve.tensor_tensor(d, d, src, ALU.add))

            with ExitStack() as scope2:
                buffers, prefetch = expert_inputs(scope2, "f2", 8 * P, E + 2)
                layer_norm(nc, env, "ln_f2", xa, xb, T, "eps5", "a2_g2", "a2_b2", prefetch=prefetch)
                moe(nc, env, "m2", xb, P, xb, P, a["f2_route"], "f2_coefb", 1, a["f2_w1"], a["f2_w2"], 8, D,
                    ACT.Gelu, b1="f2_b1", b2=a["f2_b2"], dense_expert=True, finish=add_both, loaded=buffers)

            layer_norm(nc, env, "ln_a3x", h, xa, T, "eps5")
            layer_norm(nc, env, "ln_a3", xa, xb, T, "eps6", "a3_g", "a3_b")
            def add_one(dve, chain, mc, src):
                d = h[:, mc, :].rearrange("p (i w) -> p i w", i=2)
                chain(dve.tensor_tensor(d, d, src, ALU.add))

            with ExitStack() as scope2:
                project = small_attention("a3", xb, T, bo="a3_bo", factor=0.1, causal=True, bq="a3_bq", bk="a3_bk",
                                          bv="a3_bv", gate="a3_ent", exp_scale=HD ** -0.5 / 0.1)
                buffers, prefetch = expert_inputs(scope2, "f3", 2 * 4 * P, E)
                layer_norm(nc, env, "ln_f3", h, xa, T, "eps5", prefetch=prefetch, project=project)
                moe(nc, env, "m3", xa, P, xa, P, a["f3_route"], None, 2, a["f3_w1"], a["f3_w2"], 4, D, ACT.Silu,
                    gated=True, finish=add_one, loaded=buffers, prefetch=weights("tok"))

            with stage(nc, "output") as (block, _, sem):
                stored = sem("stored")

                @block.sync
                def _(sp):
                    sp.dma_start(a["out"][b], h[:, :, :]).then_inc(stored, 16)
                    sp.wait_ge(stored, 16)


def kernel(**inputs):
    import ml_dtypes
    import numpy as np
    import concourse.bacc as bacc
    from concourse.bass_utils import run_bass_kernel_spmd

    i = {k: np.asarray(v) for k, v in inputs.items()}
    f32 = np.float32

    def halves(w, p=P):
        return np.ascontiguousarray(w.reshape(-1, p, w.shape[-1]).transpose(1, 0, 2))

    def by_partition(v, p=P):
        v = v.reshape(-1, p).T
        return np.concatenate([v, np.zeros((P - p, v.shape[1]), f32)]) if p < P else v

    def head_rows(w):
        out = np.zeros((4, VW, 4, w.shape[-1]), f32)
        out[:, :HD] = w.reshape(4, 4, HD, -1).transpose(1, 2, 0, 3)
        return out.reshape(P, 4, -1)

    def twice(w):
        return np.repeat(w.reshape(D, NH, 1, HD2), 2, 2).reshape(D, -1)

    tok_w = i["L0_tok_W_qkv"].reshape(D, NH, 3, HD).transpose(0, 2, 1, 3).reshape(D, 3 * D)
    tok_b = i["L0_tok_b_qkv"].reshape(NH, 3, HD).transpose(1, 0, 2).reshape(3, D)
    a2_b = i["L2_ffn_bqkv"].reshape(3, D)
    a3_b = i["L3_attn_b_qkv"].reshape(3, D)
    vectors = {
        "zero": np.zeros((P, 4), f32), "eps5": np.full((P, 1), 1e-5, f32), "eps6": np.full((P, 1), 1e-6, f32),
        "root_half": np.full((P, 1), 0.5 ** 0.5, f32),
        "tok_bq": by_partition(tok_b[0]), "tok_bk": by_partition(tok_b[1]), "tok_bo": by_partition(i["L0_tok_b_out"]),
        "tok_g": by_partition(i["L0_tok_ln_gamma"]), "tok_b": by_partition(i["L0_tok_ln_beta"]),
        "f0_sb1": by_partition(i["L0_ffn_sb1"]), "f0_sb3": by_partition(i["L0_ffn_sb3"]),
        "f0_sb2": by_partition(i["L0_ffn_sb2"]), "f0_b1": by_partition(i["L0_ffn_b1"]),
        "f0_b2": by_partition(i["L0_ffn_b2"]),
        "f1_enc": by_partition(i["L1_ffn_enc_b"]), "f1_s2c": by_partition(i["L1_ffn_s2c_b"], 64),
        "f1_rb1": by_partition(i["L1_ffn_r_b1"], 64), "f1_eb1": by_partition(i["L1_ffn_e_b1"]),
        "f1_c2s": by_partition(i["L1_ffn_c2s_b"]), "f1_dec": by_partition(i["L1_ffn_dec_b"]),
        "f1_g": by_partition(i["L1_ffn_ln_g"]), "f1_b": by_partition(i["L1_ffn_ln_b"]),
        "a2_g1": by_partition(i["L2_ffn_ln1_g"]), "a2_b1": by_partition(i["L2_ffn_ln1_b"]),
        "a2_bq": by_partition(a2_b[0]), "a2_bk": by_partition(a2_b[1]), "a2_bo": by_partition(i["L2_ffn_bo"]),
        "a2_g2": by_partition(i["L2_ffn_ln2_g"]), "a2_b2": by_partition(i["L2_ffn_ln2_b"]),
        "f2_b1": np.concatenate([by_partition(i["L2_ffn_b1"]), by_partition(i["L2_ffn_rb1"])], 1),
        "a3_g": by_partition(i["L3_attn_ln_g"]), "a3_b": by_partition(i["L3_attn_ln_b"]),
        "a3_bq": by_partition(a3_b[0]), "a3_bk": by_partition(a3_b[1]), "a3_bo": by_partition(i["L3_attn_b_out"]),
    }
    rows = {"tok_bv": tok_b[2], "a2_bv": a2_b[2], "a3_bv": a3_b[2], "f1_rb2": i["L1_ffn_r_b2"],
            "f2_coefb": i["L2_ffn_coef_b"], "a3_ent": i["L3_attn_b_ent"], "falling": np.arange(E, 0, -1, dtype=f32)}

    eye = np.eye(P, dtype=f32)
    sum_rows = np.zeros((P, P), f32)
    for g in range(4):
        sum_rows[VW * g + HD, VW * g:VW * g + VW] = 1
    pick = np.zeros((P, 9, P), f32)
    for e in range(9):
        pick[e, e] = 1
    omega = (f32(10000.0) ** (f32(-2.0) * np.arange(HD // 2, dtype=f32) / f32(HD))).astype(np.float64)
    angle = omega[:, None] * np.arange(T)[None]
    cos, sin = np.cos(angle).astype(f32), np.sin(angle).astype(f32)
    trig = np.zeros((P, T), f32)
    trig[0:8], trig[8:16], trig[16:24] = 4 * cos, 4 * sin, -4 * cos
    keys = np.concatenate([cos, sin])
    key_high = (keys.view(np.uint32) + np.uint32(1 << 11) & np.uint32(0xFFFFF000)).view(f32)
    trig_k = np.zeros((P, T), f32)
    for at, part in TRIG_PARTS:
        trig_k[at:at + HD] = (key_high, keys - key_high)[part]
    trig_k[MAX_ROW:MAX_ROW + 3] = 1
    fix_k, fix_q = np.zeros((P, T), f32), np.zeros((P, T), f32)
    for t in range(1, 5):
        fix_k[HD2 + t - 1, P * t:P * t + P] = 1
        fix_q[HD2 + t - 1, :P * t] = -50.0 * 8
    consts = {"mean": np.full((P, P), 1 / D, f32), "ident": eye, "sum_rows": sum_rows, "trig_k": trig_k,
              "pick": pick.reshape(P, -1), "trig": trig, "fix_k": fix_k, "fix_q": fix_q}
    bf = ml_dtypes.bfloat16
    above = np.triu(np.ones((P, P), f32), 1)
    stacks = {}
    for side, (order, width) in STACKS.items():
        stacks[side] = np.zeros((P, 2, 8, width), f32)
        for at, part in order:
            for head in range(8):
                for d in range(HD):
                    stacks[side][head * HD + d, part, head, at + d] = 1
    consts16 = {"ident": eye.astype(bf), "hard_q": (above * f32(-1e30)).astype(bf),
                "hard_k": (above.T * f32(-1e30)).astype(bf), "soft_q": (above * f32(-400)).astype(bf),
                "soft_k": (above.T * f32(-400)).astype(bf)}

    al, be = i["L0_attn_alpha"], i["L0_attn_beta"]
    ab = np.zeros((3, 8, NH, 2, 8), f32)
    for r in range(8):
        ab[0, r, :, 0, r] = al[:, r]
        ab[1, r, :, 0, r] = be[:, r]
        ab[1, r, :, 1, r] = al[:, r]
        ab[2, r, :, 1, r] = be[:, r]

    arrays = {
        "x": np.ascontiguousarray(i["x"].reshape(B, S_IMG, KC, P).transpose(0, 3, 2, 1)),
        "txt": np.ascontiguousarray(i["txt"].reshape(B, S_TXT, KC, P).transpose(0, 3, 2, 1)),
        "vectors": np.concatenate([vectors[k] for k, _ in VECTORS], 1),
        "rows": np.ascontiguousarray(np.broadcast_to(np.concatenate([rows[k] for k, _ in ROWS])[None],
                                                     (P, columns(ROWS)[1]))),
        "consts": np.concatenate([consts[k] for k, _ in CONSTS], 1),
        "consts16": np.concatenate([consts16[k] for k, _ in CONSTS16], 1),
        "alpha_beta": ab.reshape(24, D),
        "tok_qkv": halves(tok_w), "tok_o": head_rows(i["L0_tok_W_out"]),
        "a0_qkv": halves(i["L0_attn_Wqkv"].T), "a0_o": head_rows(i["L0_attn_Wout"].T),
        "a1_qkv": halves(np.concatenate([i["L1_attn_Wq"].T, i["L1_attn_Wk"].T, i["L1_attn_Wv"].T], 1)),
        "a1_o": head_rows(i["L1_attn_Wo"].T),
        "a2_qkv": halves(i["L2_ffn_Wqkv"]), "a2_o": head_rows(i["L2_ffn_Wo"]),
        "a3_qkv": halves(np.concatenate([i["L3_attn_w_qkv"].T, i["L3_attn_w_ent"].T], 1)),
        "a3_o": head_rows(i["L3_attn_w_out"].T),
        "w2_qkv": halves(np.concatenate([twice(i["L2_attn_Wq"]), twice(i["L2_attn_Wk"]), i["L2_attn_Wv"]], 1)),
        **{f"stack_{k}": v for k, v in stacks.items()},
        "w2_r": halves(i["L2_attn_Wr"]),
        "f0_sw1": halves(i["L0_ffn_sw1"]), "f0_sw3": halves(i["L0_ffn_sw3"]), "f0_sw2": halves(i["L0_ffn_sw2"]),
        "f0_w1": i["L0_ffn_w1"], "f0_w2": i["L0_ffn_w2"],
        "f1_enc_w": halves(i["L1_ffn_enc_w"]), "f1_s2c_w": halves(i["L1_ffn_s2c_w"]),
        "f1_r_w1": halves(i["L1_ffn_r_w1"], 64), "f1_r_w2": i["L1_ffn_r_w2"],
        "f1_e_w1": i["L1_ffn_e_w1"], "f1_e_w2": i["L1_ffn_e_w2"], "f1_e_b2": i["L1_ffn_e_b2"],
        "f1_c2s_w": halves(i["L1_ffn_c2s_w"], 64), "f1_dec_w": halves(i["L1_ffn_dec_w"]),
        "f2_route": np.concatenate([i["L2_ffn_gate_w"], i["L2_ffn_coef_w"]], 1),
        "f2_w1": np.concatenate([i["L2_ffn_W1"], i["L2_ffn_rW1"][None]]),
        "f2_w2": np.concatenate([i["L2_ffn_W2"], i["L2_ffn_rW2"][None]]),
        "f2_b2": np.concatenate([i["L2_ffn_b2"], i["L2_ffn_rb2"][None]]),
        "f3_route": i["L3_ffn_gate_w"].T, "f3_w1": i["L3_ffn_w12"].transpose(0, 2, 1),
        "f3_w2": i["L3_ffn_w3"].transpose(0, 2, 1),
    }
    nc = bacc.Bacc("TRN2", target_bir_lowering=False, num_devices=1)
    fed, aps = {}, {}
    for name, v in arrays.items():
        v = np.ascontiguousarray(v)
        fed[f"in_{name}"] = v
        aps[name] = nc.dram_tensor(f"in_{name}", v.shape, mybir.dt.from_np(v.dtype), kind="ExternalInput").ap()
    aps["out"] = nc.dram_tensor("out_0", (B, P, KC, T), F32, kind="ExternalOutput").ap()
    build(nc, aps)
    r = run_bass_kernel_spmd(nc, [fed], core_ids=[0])
    got = r.results[0]["out_0"]
    return np.ascontiguousarray(got.transpose(0, 3, 2, 1).reshape(B, T, D))
```
